# Optimizing a Trainium2 kernel written in Bass

```python
import numpy as np
import jax
import jax.numpy as jnp

def _softmax(x, axis=-1):
    return jax.nn.softmax(x, axis=axis)

def _gelu(x):
    return jax.nn.gelu(x, approximate=True)

def _silu(x):
    return jax.nn.silu(x)

def _sigmoid(x):
    return jax.nn.sigmoid(x)

def _layernorm(x, axis=-1, eps=1e-05):
    m = jnp.mean(x, axis=axis, keepdims=True)
    v = jnp.var(x, axis=axis, keepdims=True)
    return (x - m) / jnp.sqrt(v + eps)

def _scatter_add(tgt, idx, src, axis=0):
    return tgt.at[idx].add(src)

def _segment_sum(src, seg, n):
    return jax.ops.segment_sum(src, seg, n)
kernel_name = 'mk_perceiver_d2_seqx_r8_7a02e3'

def setup_inputs(seed: int=0):
    np.random.seed(seed)
    _w = jnp.asarray

    def _rec_inputs():
        import jax
        import jax.numpy as jnp
        _rk = jax.random.key(seed)
        x = 7.22e-05 + 1 * jax.random.normal(jax.random.fold_in(_rk, 1), (128, 32, 128), jnp.float32)
        _lenS = 32 - jax.random.randint(jax.random.fold_in(_rk, 7), (128,), 0, max(1, 32 // 4) + 1, jnp.int32)
        _lenS2 = 257 - jax.random.randint(jax.random.fold_in(_rk, 8), (128,), 0, max(1, 257 // 4) + 1, jnp.int32)
        _ctx_1024P = jax.random.normal(jax.random.fold_in(_rk, 11), (128, 16, 128), jnp.float32)
        _ctx_1024c = jax.random.dirichlet(jax.random.fold_in(_rk, 511), 0.3 * jnp.ones((16,), jnp.float32), (128, 257))
        _ctx_1024t = jnp.einsum('bsk,bkd->bsd', _ctx_1024c, _ctx_1024P)
        _ctx_1024t = _ctx_1024t * jax.lax.rsqrt(jnp.mean(jnp.square(_ctx_1024t)) + 1e-12) * 0.953939
        ctx_1024 = 2.81802e-05 + 1.00001 * (_ctx_1024t + 0.3 * jax.random.normal(jax.random.fold_in(_rk, 611), (128, 257, 128), jnp.float32))
        return (x, ctx_1024)
    x, ctx_1024 = _rec_inputs()

    def _L0_xattn_setup():
        import jax, jax.numpy as jnp
        import numpy as np
        B, T, S, D = (4, 256, 512, 128)
        TOP_K = 32

        def _read(query, mem_state, top_k, Wq, bq, Wk, bk, Wv, bv, Wo, bo):
            b, t, d = query.shape
            s = mem_state.shape[1]
            scale = 1.0 / np.sqrt(d)
            q = query @ Wq.T + bq
            k = mem_state @ Wk.T + bk
            v = mem_state @ Wv.T + bv
            scores = jnp.einsum('btd,bsd->bts', q, k) * scale
            if top_k < s:
                vals, idx = jax.lax.top_k(scores, top_k)
                b_ix = jnp.arange(b)[:, None, None]
                t_ix = jnp.arange(t)[None, :, None]
                masked = jnp.full_like(scores, -jnp.inf)
                scores = masked.at[b_ix, t_ix, idx].set(vals)
            attn = jax.nn.softmax(scores, axis=-1)
            ctx = jnp.einsum('bts,bsd->btd', attn, v)
            return ctx @ Wo.T + bo
        key = jax.random.key(seed)
        ks = jax.random.split(key, 12)
        std = 0.02
        inp = {'query': jax.random.normal(ks[0], (B, T, D), dtype=jnp.float32), 'mem_state': jax.random.normal(ks[1], (B, S, D), dtype=jnp.float32), 'top_k': TOP_K, 'Wq': jax.random.normal(ks[2], (D, D), dtype=jnp.float32) * std, 'bq': jnp.zeros((D,), dtype=jnp.float32), 'Wk': jax.random.normal(ks[3], (D, D), dtype=jnp.float32) * std, 'bk': jnp.zeros((D,), dtype=jnp.float32), 'Wv': jax.random.normal(ks[4], (D, D), dtype=jnp.float32) * std, 'bv': jnp.zeros((D,), dtype=jnp.float32), 'Wo': jax.random.normal(ks[5], (D, D), dtype=jnp.float32) * std, 'bo': jnp.zeros((D,), dtype=jnp.float32)}
        return inp
    _L0_xattn_all = _L0_xattn_setup()
    _L0_xattn_in = {k: v for k, v in _L0_xattn_all.items() if k in ('Wq', 'bq', 'Wk', 'bk', 'Wv', 'bv', 'Wo', 'bo')}
    del _L0_xattn_all

    def _L0_attn_setup():
        import jax, jax.numpy as jnp
        import numpy as np
        import math
        D_MODEL = 128
        NUM_HEADS = 16
        HEAD_DIM = D_MODEL // NUM_HEADS
        ROPE_THETA = 10000.0

        def _rope_tables(seq_len, dim, theta=ROPE_THETA):
            inv = 1.0 / theta ** (jnp.arange(0, dim, 2, dtype=jnp.float32) / dim)
            t = jnp.arange(seq_len, dtype=jnp.float32)
            f = jnp.outer(t, inv)
            cos = jnp.repeat(jnp.cos(f), 2, axis=-1)
            sin = jnp.repeat(jnp.sin(f), 2, axis=-1)
            return (cos, sin)

        def _rotate_half(x):
            x1 = x[..., ::2]
            x2 = x[..., 1::2]
            return jnp.stack((-x2, x1), axis=-1).reshape(x.shape)
        key = jax.random.key(seed)
        ks = jax.random.split(key, 5)
        scale = 1.0 / math.sqrt(D_MODEL)
        return {'x': jax.random.normal(ks[0], (2, 256, D_MODEL), dtype=jnp.float32), 'W_Q': jax.random.normal(ks[1], (D_MODEL, D_MODEL), dtype=jnp.float32) * scale, 'W_K': jax.random.normal(ks[2], (D_MODEL, D_MODEL), dtype=jnp.float32) * scale, 'W_V': jax.random.normal(ks[3], (D_MODEL, D_MODEL), dtype=jnp.float32) * scale, 'W_O': jax.random.normal(ks[4], (D_MODEL, D_MODEL), dtype=jnp.float32) * scale}
    _L0_attn_all = _L0_attn_setup()
    _L0_attn_in = {k: v for k, v in _L0_attn_all.items() if k in ('W_Q', 'W_K', 'W_V', 'W_O')}
    del _L0_attn_all

    def _L0_ffn_setup():
        import math
        import jax, jax.numpy as jnp
        import numpy as np
        D_MODEL = 128
        D_FF = 512
        N_EXPERTS = 8
        CAPACITY_FACTOR = 1.25
        L, B = (64, 8)

        def _route(tokens, router_w):
            T = tokens.shape[0]
            E = router_w.shape[0]
            capacity = int(math.ceil(T / E * CAPACITY_FACTOR))
            logits = tokens @ router_w.T
            probs = jax.nn.softmax(logits, axis=-1)
            top1_idx = jnp.argmax(probs, axis=-1)
            top1_prob = jnp.max(probs, axis=-1)
            order = jnp.lexsort((-top1_prob, top1_idx))
            sorted_e = top1_idx[order]
            counts = jnp.bincount(top1_idx, length=E)
            start = jnp.cumsum(counts) - counts
            pos_in_group = jnp.arange(T) - start[sorted_e]
            keep_sorted = pos_in_group < capacity
            keep = jnp.zeros((T,), bool).at[order].set(keep_sorted)
            return jnp.where(keep, top1_idx, 0).astype(jnp.int32)
        key = jax.random.key(seed)
        ks = jax.random.split(key, 6)
        s_in = 1.0 / math.sqrt(D_MODEL)
        s_ff = 1.0 / math.sqrt(D_FF)
        return {'x': jax.random.normal(ks[0], (L, B, D_MODEL), dtype=jnp.float32), 'router_w': jax.random.uniform(ks[1], (N_EXPERTS, D_MODEL), minval=-s_in, maxval=s_in), 'W1': jax.random.uniform(ks[2], (N_EXPERTS, D_MODEL, D_FF), minval=-s_in, maxval=s_in), 'b1': jax.random.uniform(ks[3], (N_EXPERTS, D_FF), minval=-s_in, maxval=s_in), 'W2': jax.random.uniform(ks[4], (N_EXPERTS, D_FF, D_MODEL), minval=-s_ff, maxval=s_ff), 'b2': jax.random.uniform(ks[5], (N_EXPERTS, D_MODEL), minval=-s_ff, maxval=s_ff)}
    _L0_ffn_all = _L0_ffn_setup()
    _L0_ffn_in = {k: v for k, v in _L0_ffn_all.items() if k in ('router_w', 'W1', 'b1', 'W2', 'b2')}
    del _L0_ffn_all

    def _L1_xattn_setup():
        import jax, jax.numpy as jnp
        import numpy as np
        HEADS = 16
        EMBED = 128
        HEAD_DIM = EMBED // HEADS
        key = jax.random.key(seed)
        ks = jax.random.split(key, 11)
        B, S, E = (4, 256, EMBED)
        s = 1.0 / np.sqrt(E)
        return {'query': jax.random.normal(ks[0], (B, S, E), jnp.float32), 'key': jax.random.normal(ks[1], (B, S, E), jnp.float32), 'value': jax.random.normal(ks[2], (B, S, E), jnp.float32), 'Wq': jax.random.normal(ks[3], (E, E), jnp.float32) * s, 'bq': jax.random.normal(ks[4], (E,), jnp.float32) * s, 'Wk': jax.random.normal(ks[5], (E, E), jnp.float32) * s, 'bk': jax.random.normal(ks[6], (E,), jnp.float32) * s, 'Wv': jax.random.normal(ks[7], (E, E), jnp.float32) * s, 'bv': jax.random.normal(ks[8], (E,), jnp.float32) * s, 'Wo': jax.random.normal(ks[9], (E, E), jnp.float32) * s, 'bo': jax.random.normal(ks[10], (E,), jnp.float32) * s}
    _L1_xattn_all = _L1_xattn_setup()
    _L1_xattn_in = {k: v for k, v in _L1_xattn_all.items() if k in ('Wq', 'bq', 'Wk', 'bk', 'Wv', 'bv', 'Wo', 'bo')}
    del _L1_xattn_all

    def _L1_attn_setup():
        import jax, jax.numpy as jnp
        import numpy as np
        DIM = 128
        HEADS = 16
        DIM_HEAD = 64
        DIM_INNER = HEADS * DIM_HEAD

        def rms_norm(x, gamma):
            eps = 1e-12
            norm = jnp.maximum(jnp.linalg.norm(x, axis=-1, keepdims=True), eps)
            return x / norm * x.shape[-1] ** 0.5 * (gamma + 1.0)
        key = jax.random.key(seed)
        k1, k2, k3 = jax.random.split(key, 3)
        x = jax.random.normal(k1, (2, 256, DIM), dtype=jnp.float32)
        gamma = jnp.zeros((DIM,), dtype=jnp.float32)
        w_qkv = jax.random.normal(k2, (DIM, DIM_INNER * 3), dtype=jnp.float32) * DIM ** (-0.5)
        w_out = jax.random.normal(k3, (DIM_INNER, DIM), dtype=jnp.float32) * DIM_INNER ** (-0.5)
        return {'x': x, 'gamma': gamma, 'w_qkv': w_qkv, 'w_out': w_out}
    _L1_attn_all = _L1_attn_setup()
    _L1_attn_in = {k: v for k, v in _L1_attn_all.items() if k in ('gamma', 'w_qkv', 'w_out')}
    del _L1_attn_all

    def _L1_ffn_setup():
        import jax, jax.numpy as jnp
        import numpy as np
        TOP_K = 2
        N_EXPERTS = 8
        key = jax.random.key(seed)
        k_x, k_g, k_w1, k_w2 = jax.random.split(key, 4)
        B, S, d_in, d_hid, d_out, E = (8, 256, 128, 256, 128, N_EXPERTS)
        s_gate = float(np.sqrt(6.0 / (d_in + E)))
        s_w1 = float(np.sqrt(6.0 / (d_in + d_hid)))
        s_w2 = float(np.sqrt(6.0 / (d_hid + d_out)))
        x = jax.random.normal(k_x, (B, S, d_in), dtype=jnp.float32)
        gate_W = jax.random.uniform(k_g, (d_in, E), jnp.float32, -s_gate, s_gate)
        W1 = jax.random.uniform(k_w1, (E, d_in, d_hid), jnp.float32, -s_w1, s_w1)
        b1 = jnp.zeros((E, d_hid), jnp.float32)
        W2 = jax.random.uniform(k_w2, (E, d_hid, d_out), jnp.float32, -s_w2, s_w2)
        b2 = jnp.zeros((E, d_out), jnp.float32)
        return {'x': x, 'gate_W': gate_W, 'W1': W1, 'b1': b1, 'W2': W2, 'b2': b2}
    _L1_ffn_all = _L1_ffn_setup()
    _L1_ffn_in = {k: v for k, v in _L1_ffn_all.items() if k in ('gate_W', 'W1', 'b1', 'W2', 'b2')}
    del _L1_ffn_all
    return {'x': x, 'ctx_1024': ctx_1024, 'L0_xattn_Wq': _L0_xattn_in['Wq'], 'L0_xattn_bq': _L0_xattn_in['bq'], 'L0_xattn_Wk': _L0_xattn_in['Wk'], 'L0_xattn_bk': _L0_xattn_in['bk'], 'L0_xattn_Wv': _L0_xattn_in['Wv'], 'L0_xattn_bv': _L0_xattn_in['bv'], 'L0_xattn_Wo': _L0_xattn_in['Wo'], 'L0_xattn_bo': _L0_xattn_in['bo'], 'L0_attn_W_Q': _L0_attn_in['W_Q'], 'L0_attn_W_K': _L0_attn_in['W_K'], 'L0_attn_W_V': _L0_attn_in['W_V'], 'L0_attn_W_O': _L0_attn_in['W_O'], 'L0_ffn_router_w': _L0_ffn_in['router_w'], 'L0_ffn_W1': _L0_ffn_in['W1'], 'L0_ffn_b1': _L0_ffn_in['b1'], 'L0_ffn_W2': _L0_ffn_in['W2'], 'L0_ffn_b2': _L0_ffn_in['b2'], 'L1_xattn_Wq': _L1_xattn_in['Wq'], 'L1_xattn_bq': _L1_xattn_in['bq'], 'L1_xattn_Wk': _L1_xattn_in['Wk'], 'L1_xattn_bk': _L1_xattn_in['bk'], 'L1_xattn_Wv': _L1_xattn_in['Wv'], 'L1_xattn_bv': _L1_xattn_in['bv'], 'L1_xattn_Wo': _L1_xattn_in['Wo'], 'L1_xattn_bo': _L1_xattn_in['bo'], 'L1_attn_gamma': _L1_attn_in['gamma'], 'L1_attn_w_qkv': _L1_attn_in['w_qkv'], 'L1_attn_w_out': _L1_attn_in['w_out'], 'L1_ffn_gate_W': _L1_ffn_in['gate_W'], 'L1_ffn_W1': _L1_ffn_in['W1'], 'L1_ffn_b1': _L1_ffn_in['b1'], 'L1_ffn_W2': _L1_ffn_in['W2'], 'L1_ffn_b2': _L1_ffn_in['b2']}

def reference(x, ctx_1024, L0_xattn_Wq, L0_xattn_bq, L0_xattn_Wk, L0_xattn_bk, L0_xattn_Wv, L0_xattn_bv, L0_xattn_Wo, L0_xattn_bo, L0_attn_W_Q, L0_attn_W_K, L0_attn_W_V, L0_attn_W_O, L0_ffn_router_w, L0_ffn_W1, L0_ffn_b1, L0_ffn_W2, L0_ffn_b2, L1_xattn_Wq, L1_xattn_bq, L1_xattn_Wk, L1_xattn_bk, L1_xattn_Wv, L1_xattn_bv, L1_xattn_Wo, L1_xattn_bo, L1_attn_gamma, L1_attn_w_qkv, L1_attn_w_out, L1_ffn_gate_W, L1_ffn_W1, L1_ffn_b1, L1_ffn_W2, L1_ffn_b2):
    import jax
    import jax.numpy as jnp

    def _L0_xattn_ref(query, mem_state, top_k, Wq, bq, Wk, bk, Wv, bv, Wo, bo):
        import jax, jax.numpy as jnp
        import numpy as np
        B, T, S, D = (4, 256, 512, 128)
        TOP_K = 32

        def _read(query, mem_state, top_k, Wq, bq, Wk, bk, Wv, bv, Wo, bo):
            b, t, d = query.shape
            s = mem_state.shape[1]
            scale = 1.0 / np.sqrt(d)
            q = query @ Wq.T + bq
            k = mem_state @ Wk.T + bk
            v = mem_state @ Wv.T + bv
            scores = jnp.einsum('btd,bsd->bts', q, k) * scale
            if top_k < s:
                vals, idx = jax.lax.top_k(scores, top_k)
                b_ix = jnp.arange(b)[:, None, None]
                t_ix = jnp.arange(t)[None, :, None]
                masked = jnp.full_like(scores, -jnp.inf)
                scores = masked.at[b_ix, t_ix, idx].set(vals)
            attn = jax.nn.softmax(scores, axis=-1)
            ctx = jnp.einsum('bts,bsd->btd', attn, v)
            return ctx @ Wo.T + bo
        return _read(query, mem_state, top_k, Wq, bq, Wk, bk, Wv, bv, Wo, bo)

    def _L0_attn_ref(x, W_Q, W_K, W_V, W_O):
        import jax, jax.numpy as jnp
        import numpy as np
        import math
        D_MODEL = 128
        NUM_HEADS = 16
        HEAD_DIM = D_MODEL // NUM_HEADS
        ROPE_THETA = 10000.0

        def _rope_tables(seq_len, dim, theta=ROPE_THETA):
            inv = 1.0 / theta ** (jnp.arange(0, dim, 2, dtype=jnp.float32) / dim)
            t = jnp.arange(seq_len, dtype=jnp.float32)
            f = jnp.outer(t, inv)
            cos = jnp.repeat(jnp.cos(f), 2, axis=-1)
            sin = jnp.repeat(jnp.sin(f), 2, axis=-1)
            return (cos, sin)

        def _rotate_half(x):
            x1 = x[..., ::2]
            x2 = x[..., 1::2]
            return jnp.stack((-x2, x1), axis=-1).reshape(x.shape)
        B, L, _ = x.shape

        def proj(W):
            return jnp.einsum('bld,ed->ble', x, W).reshape(B, L, NUM_HEADS, HEAD_DIM).transpose(0, 2, 1, 3)
        q, k, v = (proj(W_Q), proj(W_K), proj(W_V))
        cos, sin = _rope_tables(L, HEAD_DIM)
        cos = cos[None, None].astype(x.dtype)
        sin = sin[None, None].astype(x.dtype)
        q = q * cos + _rotate_half(q) * sin
        k = k * cos + _rotate_half(k) * sin
        scores = jnp.einsum('bhqd,bhkd->bhqk', q, k) / math.sqrt(HEAD_DIM)
        attn = jax.nn.softmax(scores, axis=-1)
        ctx = jnp.einsum('bhqk,bhkd->bhqd', attn, v)
        ctx = ctx.transpose(0, 2, 1, 3).reshape(B, L, D_MODEL)
        return jnp.einsum('bld,ed->ble', ctx, W_O)

    def _L0_ffn_ref(x, router_w, W1, b1, W2, b2):
        import math
        import jax, jax.numpy as jnp
        import numpy as np
        D_MODEL = 128
        D_FF = 512
        N_EXPERTS = 8
        CAPACITY_FACTOR = 1.25
        L, B = (64, 8)

        def _route(tokens, router_w):
            T = tokens.shape[0]
            E = router_w.shape[0]
            capacity = int(math.ceil(T / E * CAPACITY_FACTOR))
            logits = tokens @ router_w.T
            probs = jax.nn.softmax(logits, axis=-1)
            top1_idx = jnp.argmax(probs, axis=-1)
            top1_prob = jnp.max(probs, axis=-1)
            order = jnp.lexsort((-top1_prob, top1_idx))
            sorted_e = top1_idx[order]
            counts = jnp.bincount(top1_idx, length=E)
            start = jnp.cumsum(counts) - counts
            pos_in_group = jnp.arange(T) - start[sorted_e]
            keep_sorted = pos_in_group < capacity
            keep = jnp.zeros((T,), bool).at[order].set(keep_sorted)
            return jnp.where(keep, top1_idx, 0).astype(jnp.int32)
        Lx, Bx, D = x.shape
        T = Lx * Bx
        E = router_w.shape[0]
        tokens = x.reshape(T, D)
        final_e = _route(tokens, router_w)
        out = jnp.zeros_like(tokens)
        for e in range(E):
            h = jax.nn.relu(tokens @ W1[e] + b1[e])
            y = h @ W2[e] + b2[e]
            out = out + jnp.where((final_e == e)[:, None], y, 0.0)
        return out.reshape(Lx, Bx, D)

    def _L1_xattn_ref(query, key, value, Wq, bq, Wk, bk, Wv, bv, Wo, bo):
        import jax, jax.numpy as jnp
        import numpy as np
        HEADS = 16
        EMBED = 128
        HEAD_DIM = EMBED // HEADS
        B, Sq, E = query.shape
        Sk = key.shape[1]
        H, D = (HEADS, HEAD_DIM)
        q = (query @ Wq.T + bq).reshape(B, Sq, H, D)
        k = (key @ Wk.T + bk).reshape(B, Sk, H, D)
        v = (value @ Wv.T + bv).reshape(B, Sk, H, D)
        scores = jnp.einsum('bqhd,bkhd->bhqk', q, k) / np.sqrt(D).astype(jnp.float32)
        attn = jax.nn.softmax(scores, axis=-1)
        out = jnp.einsum('bhqk,bkhd->bqhd', attn, v).reshape(B, Sq, E)
        return out @ Wo.T + bo

    def _L1_attn_ref(x, gamma, w_qkv, w_out):
        import jax, jax.numpy as jnp
        import numpy as np
        DIM = 128
        HEADS = 16
        DIM_HEAD = 64
        DIM_INNER = HEADS * DIM_HEAD

        def rms_norm(x, gamma):
            eps = 1e-12
            norm = jnp.maximum(jnp.linalg.norm(x, axis=-1, keepdims=True), eps)
            return x / norm * x.shape[-1] ** 0.5 * (gamma + 1.0)
        b, n, _ = x.shape
        scale = DIM_HEAD ** (-0.5)
        xn = rms_norm(x, gamma)
        qkv = xn @ w_qkv
        qkv = qkv.reshape(b, n, 3, HEADS, DIM_HEAD)
        qkv = jnp.transpose(qkv, (2, 0, 3, 1, 4))
        q, k, v = (qkv[0], qkv[1], qkv[2])
        q = q * scale
        sim = jnp.einsum('bhid,bhjd->bhij', q, k)
        attn = jax.nn.softmax(sim, axis=-1)
        out = jnp.einsum('bhij,bhjd->bhid', attn, v)
        out = jnp.transpose(out, (0, 2, 1, 3)).reshape(b, n, DIM_INNER)
        return out @ w_out

    def _L1_ffn_ref(x, gate_W, W1, b1, W2, b2):
        import jax, jax.numpy as jnp
        import numpy as np
        TOP_K = 2
        N_EXPERTS = 8
        E = W1.shape[0]
        d_in = x.shape[-1]
        d_out = W2.shape[-1]
        x_flat = x.reshape(-1, d_in)
        logits = x_flat @ gate_W
        gates = jax.nn.softmax(logits, axis=-1)
        tk_g, tk_i = jax.lax.top_k(gates, TOP_K)
        tk_g = tk_g / (jnp.sum(tk_g, axis=-1, keepdims=True) + 1e-08)
        cw = jnp.sum(jax.nn.one_hot(tk_i, E, dtype=x.dtype) * tk_g[..., None], axis=1)
        out = x_flat
        for e in range(E):
            h = jax.nn.relu(x_flat @ W1[e] + b1[e])
            out = out + cw[:, e:e + 1] * (h @ W2[e] + b2[e])
        return out.reshape(x.shape[:-1] + (d_out,))
    x = x + _L0_xattn_ref(_layernorm(x, axis=-1), ctx_1024, 32, L0_xattn_Wq, L0_xattn_bq, L0_xattn_Wk, L0_xattn_bk, L0_xattn_Wv, L0_xattn_bv, L0_xattn_Wo, L0_xattn_bo)
    x = x + _L0_attn_ref(_layernorm(x, axis=-1), L0_attn_W_Q, L0_attn_W_K, L0_attn_W_V, L0_attn_W_O)
    x = x + _L0_ffn_ref(_layernorm(x, axis=-1), L0_ffn_router_w, L0_ffn_W1, L0_ffn_b1, L0_ffn_W2, L0_ffn_b2)
    x = x + _L1_xattn_ref(_layernorm(x, axis=-1), ctx_1024, ctx_1024, L1_xattn_Wq, L1_xattn_bq, L1_xattn_Wk, L1_xattn_bk, L1_xattn_Wv, L1_xattn_bv, L1_xattn_Wo, L1_xattn_bo)
    x = x + _L1_attn_ref(_layernorm(x, axis=-1), L1_attn_gamma, L1_attn_w_qkv, L1_attn_w_out)
    x = x + _L1_ffn_ref(_layernorm(x, axis=-1), L1_ffn_gate_W, L1_ffn_W1, L1_ffn_b1, L1_ffn_W2, L1_ffn_b2)
    return x

_drawn_inputs = setup_inputs


def setup_inputs(seed=0):
    import zlib

    import numpy as np

    out = dict(_drawn_inputs(seed))
    spreads = {'L0_xattn_bq': (0.0, 0.1),
     'L0_xattn_bk': (0.0, 0.8),
     'L0_xattn_bv': (0.0, 0.1),
     'L0_xattn_bo': (0.0, 0.1),
     'L1_attn_gamma': (0.0, 0.1),
     'L1_ffn_b1': (0.0, 0.303),
     'L1_ffn_b2': (0.0, 0.1)}
    factors = {'L1_xattn_bk': 8.0}
    for name, (base, spread) in spreads.items():
        noise = np.random.default_rng([zlib.crc32(name.encode()), seed]).standard_normal(out[name].shape)
        drawn = base * np.exp(spread * noise) if base else spread * noise
        out[name] = jnp.asarray(drawn.astype(out[name].dtype))
    for name, factor in factors.items():
        out[name] = (out[name] * factor).astype(out[name].dtype)
    return out
```

```python
from contextlib import ExitStack

import numpy as np

import concourse.bass as bass
from concourse import mybir

F32 = mybir.dt.float32
I32 = mybir.dt.int32
ALU = mybir.AluOpType
ACT = mybir.ActivationFunctionType
AX = mybir.AxisListType

B, T, D, S = 128, 32, 128, 257
P = 128
BG = P // T
G = B // BG
SC = S // P
SM = SC * P
TOP = 32
H = 16
HD = D // H
HQ = 4
NQ = H // HQ
RH = 64
RI = H * RH
RP = RI // P
E = 8
F0, F1 = 512, 256
CAP = 640
TG = 4
NB = G // TG
EPS = 1e-5
NEG = -3.0e38
FIRST_PROB = 0x3E000000
PROB_BITS = 25

SQ = ["wq0", "wk0", "wv0", "wo0", "aq", "aqr", "ak", "akr", "av", "ao", "wq1", "wk1", "wv1", "wo1"]
VEC = ["bq0", "bk0", "bv0", "bq1", "bk1", "bv1", "gamma"]
NVEC = len(VEC)
VB1_0 = NVEC
VB1_1 = VB1_0 + E * F0 // P
NV = VB1_1 + E * F1 // P
CONST = {"ident": 128, "rope": 64, "quad": 4, "vmask": 128, "batch": 4, "qsel": 32, "row4": 128,
         "before": 128, "ones": 128, "rank": 8, "half": 1, "root": 1, "eps": 1}
COFF = {}
_o = 0
for _n, _w in CONST.items():
    COFF[_n] = _o
    _o += _w
NC = _o


class Phase(ExitStack):

    def __init__(self, nc, name):
        super().__init__()
        self.nc, self.semaphores = nc, []
        self.passed = self.semaphore(f"{name}_passed")
        self.callback(self.retire)

    def semaphore(self, name):
        self.semaphores.append(self.nc.alloc_semaphore(name))
        return self.semaphores[-1]

    def retire(self):
        self.nc.clear_and_free_semaphores(self.semaphores)
        self.nc.all_engine_barrier()


class Signal:

    def __init__(self, ctx, nc, name, per=1, credit=0):
        self.sem, self.per, self.credit = ctx.semaphore(name), per, credit

    def at(self, r, j=None):
        return r * self.per + (self.per if j is None else j) + self.credit


def carry(eng, phase):
    eng.sem_inc(phase.passed, 1)


def build_program(nc, io):
    ctx = ExitStack()
    with ctx:
        def sb(name, shape, dt=F32, c=ctx):
            return c.enter_context(nc.sbuf_tensor(name, shape, dt))

        X = sb("X", [P, G, D])
        HT_all = sb("HT_all", [P, G, P])
        LG = sb("LG", [P, G, E])
        MASK = sb("MASK", [P, G, E])
        wsq = sb("wsq", [P, len(SQ), P])
        vec = sb("vec", [P, NV])
        cst = sb("cst", [P, NC])
        bo0 = sb("bo0", [P, D])
        bo1 = sb("bo1", [P, D])
        loaded = ctx.enter_context(nc.semaphore("loaded"))

        def w(name):
            return wsq[:, SQ.index(name), :]

        def v(name):
            i = VEC.index(name)
            return vec[:, i:i + 1]

        def k(name):
            return cst[:, COFF[name]:COFF[name] + CONST[name]]

        env = dict(nc=nc, io=io, X=X, HT_all=HT_all, LG=LG, MASK=MASK, w=w, v=v, k=k, vec=vec, bo0=bo0, bo1=bo1)

        with nc.Block() as block:
            @block.sync
            def _(sp):
                for q in range(4):
                    n = G // 4
                    sp.dma_start(X[:, n * q:n * q + n, :],
                                 io["x"].rearrange("(g bb) t d -> (bb t) g d", bb=BG)[:, n * q:n * q + n, :]
                                 ).then_inc(loaded, 16)
                sp.dma_start(wsq[:, :, :], io["wsq"]).then_inc(loaded, 16)
                sp.dma_start(vec[:, :], io["vec"]).then_inc(loaded, 16)
                sp.dma_start(cst[:, :], io["cst"]).then_inc(loaded, 16)
                sp.dma_start(bo0[:, :], io["bo0"]).then_inc(loaded, 16)
                sp.dma_start(bo1[:, :], io["bo1"]).then_inc(loaded, 16)
                sp.wait_ge(loaded, 9 * 16)

        attend_layer0(env)
        route_layer0(env)
        experts(env, "f0", io["f0_w1"], io["f0_w2"], io["f0_b2"], F0 // P, VB1_0, None)
        cross_layer1(env)
        self_layer1(env)
        gate_layer1(env)
        experts(env, "f1", io["f1_w1"], io["f1_w2"], io["f1_b2"], F1 // P, VB1_1, io["out"])


class Norm:

    def __init__(self, ctx, nc, name, env):
        self.env, self.ctx = env, ctx
        f = lambda n, s: ctx.enter_context(nc.sbuf_tensor(f"{name}_{n}", s, F32))
        self.stats, self.mv, self.ve, self.rstd = f("stats", [P, 6]), f("mv", [P, 2]), f("ve", [P, 1]), f("rstd", [P, 1])
        self.h = f("h", [P, D])
        self.stats_ready = Signal(ctx, nc, f"{name}_stats_ready")
        self.mv_ready = Signal(ctx, nc, f"{name}_mv_ready")
        self.ve_ready = Signal(ctx, nc, f"{name}_ve_ready")
        self.rstd_ready = Signal(ctx, nc, f"{name}_rstd_ready")
        self.h_ready = Signal(ctx, nc, f"{name}_h_ready")

    def vector_stats(self, dve, x, r):
        dve.bn_stats(self.stats[:, :], x).then_inc(self.stats_ready.sem, 1)
        dve.wait_ge(self.stats_ready.sem, self.stats_ready.at(r))
        carry(dve, self.ctx)
        dve.bn_aggr(self.mv[:, :], self.stats[:, :]).then_inc(self.mv_ready.sem, 1)

    def gpsimd(self, pool, r):
        pool.wait_ge(self.mv_ready.sem, self.mv_ready.at(r))
        pool.tensor_tensor(self.ve[:, :], self.mv[:, 1:2], self.env["k"]("eps"), ALU.add).then_inc(self.ve_ready.sem, 1)
        pool.wait_ge(self.ve_ready.sem, self.ve_ready.at(r))
        pool.tensor_tensor(self.rstd[:, :], self.ve[:, :], self.env["k"]("half"), ALU.pow).then_inc(self.rstd_ready.sem, 1)

    def vector_scale(self, dve, x, r):
        dve.wait_ge(self.rstd_ready.sem, self.rstd_ready.at(r))
        dve.tensor_scalar(self.h[:, :], x, self.mv[:, 0:1], self.rstd[:, :], ALU.subtract, ALU.mult
                          ).then_inc(self.h_ready.sem, 1)


def attend_layer0(env):
    nc, io, X, HT_all, LG, w, v, k, bo0 = (env[n] for n in ("nc", "io", "X", "HT_all", "LG", "w", "v", "k", "bo0"))
    ctx = Phase(nc, "a")
    with ctx:
        def sb(name, shape, dt=F32):
            return ctx.enter_context(nc.sbuf_tensor("a_" + name, shape, dt))

        def ps(name, shape):
            return ctx.enter_context(nc.psum_tensor("a_" + name, shape, F32))

        def sig(name, per=1, credit=0):
            return Signal(ctx, nc, "a_" + name, per, credit)

        ctxN = sb("ctxN", [P, 2, SC, BG, D])
        ctxT = sb("ctxT", [P, 2, BG, S])
        ctxL = sb("ctxL", [BG, 2, D])
        wr = sb("router", [P, E])
        hT, q, q2, qb = sb("hT", [P, P]), sb("q", [P, P]), sb("q2", [P, P]), sb("qb", [P, 1])
        sc, work, top = sb("sc", [P, S]), sb("work", [P, S]), sb("top", [P, TOP])
        nmax, ex, pr, rsum, rinv = sb("nmax", [P, 1]), sb("ex", [P, S]), sb("pr", [P, S]), sb("rsum", [P, 1]), sb("rinv", [P, 1])
        prL, prT, prLT = sb("prL", [P, BG]), sb("prT", [P, SC, P]), sb("prLT", [BG, P])
        u, uT, vT, yb = sb("u", [P, D]), sb("uT", [P, P]), sb("vT", [P, P]), sb("yb", [P, D])
        hT2, rot, qk = sb("hT2", [P, P]), sb("rot", [P, 2, 8, T]), sb("qk", [P, 2, P])
        kquad = sb("kquad", [P, BG, HQ, T])
        smax, sd, se, ssum, sinv = sb("smax", [P, H]), sb("sd", [P, H, T]), sb("se", [P, H, T]), sb("ssum", [P, H]), sb("sinv", [P, H])
        seT, vq, o, oT = sb("seT", [P, NQ, P]), sb("vq", [P, BG, D]), sb("o", [P, D]), sb("oT", [P, P])
        h3T = sb("h3T", [P, P])

        pS = ps("pS", [P, 512])
        pT = ps("pT", [P, 512])
        pM = ps("pM", [P, 4, P])
        pN = ps("pN", [P, 4, P])
        pQ = ps("pQ", [P, 4, 512])

        n1 = Norm(ctx, nc, "a_n1", env)
        n2 = Norm(ctx, nc, "a_n2", env)
        n3 = Norm(ctx, nc, "a_n3", env)
        router_loaded = sig("router_loaded", 16)
        ctx_loaded = [sig(f"ctx_loaded{p}", 48) for p in range(2)]
        hT_done, hT_ready = sig("hT_done"), sig("hT_ready")
        q_done, q_ready = sig("q_done"), sig("q_ready")
        q2_done, q2_ready, qb_ready = sig("q2_done"), sig("q2_ready"), sig("qb_ready")
        s_done, s_ready = sig("s_done", credit=2), sig("s_ready")
        topk = sig("topk", 8)
        nmax_ready, e_ready = sig("nmax_ready"), sig("e_ready")
        p_ready, rinv_ready, pL_ready = sig("p_ready"), sig("rinv_ready"), sig("pL_ready")
        pT_done, pT_ready = sig("pT_done"), sig("pT_ready", 2)
        u_done, u_ready = sig("u_done", credit=2), sig("u_ready")
        uT_done, uT_ready = sig("uT_done"), sig("uT_ready")
        v_done, v_ready = sig("v_done"), sig("v_ready")
        y_done, yb_ready, x1_ready = sig("y_done"), sig("yb_ready"), sig("x1_ready")
        h2T_done, h2T_ready = sig("h2T_done"), sig("h2T_ready")
        qk_done, rot_ready, qk_ready, kq_ready = sig("qk_done"), sig("rot_ready"), sig("qk_ready"), sig("kq_ready")
        ss_done, smax_ready, sd_ready, se_ready = sig("ss_done"), sig("smax_ready"), sig("sd_ready"), sig("se_ready")
        ssum_ready, sinv_ready = sig("ssum_ready"), sig("sinv_ready")
        seT_done, seT_ready = sig("seT_done"), sig("seT_ready")
        vq_done, vq_ready = sig("vq_done"), sig("vq_ready")
        o_done, o_ready, oT_done, oT_ready = sig("o_done"), sig("o_ready"), sig("oT_done"), sig("oT_ready")
        y2_done, x2_ready = sig("y2_done"), sig("x2_ready")
        h3T_done, h3T_ready, h3T_kept = sig("h3T_done"), sig("h3T_ready"), sig("h3T_kept", credit=1)
        lg_done, lg_ready = sig("lg_done"), sig("lg_ready")
        SCALE = float(D) ** -0.5
        SCALE2 = float(HD) ** -0.5
        ident = k("ident")

        def slots(eng, slot):
            slot(0, None, 0, 0)
            with eng.Fori(0, (G - 2) // 2) as i:
                slot(i * 2 + 1, i * 2, 1, i)
                slot(i * 2 + 2, i * 2 + 1, 0, i + 1)
            slot(G - 1, G - 2, 1, G // 2 - 1)
            slot(None, G - 1, 0, None)

        block = ctx.enter_context(nc.Block())

        @block.sync
        def _(sp):
            sp.dma_start(wr[:, :], io["router"]).then_inc(router_loaded.sem, 16)

            def load(g, p):
                sp.wait_ge(s_done.sem, s_done.at(g, -1))
                sp.wait_ge(u_done.sem, u_done.at(g, -1))
                sp.dma_start(ctxT[:, p, :, :].unsqueeze(1), io["ctxT"][bass.ds(g, 1), :, :, :].rearrange("g p b s -> p g b s")
                             ).then_inc(ctx_loaded[p].sem, 16)
                sp.dma_start(ctxN[:, p, :, :, :].rearrange("p c b d -> p (c b d)").unsqueeze(1),
                             io["ctxR"][bass.ds(g, 1), :, :].rearrange("g p n -> p g n")).then_inc(ctx_loaded[p].sem, 16)
                sp.dma_start(ctxL[:, p, :], io["ctxL"][bass.ds(g * BG, BG), :]).then_inc(ctx_loaded[p].sem, 16)

            with sp.Fori(0, G // 2) as i:
                load(i * 2, 0)
                load(i * 2 + 1, 1)

        @block.tensor
        def _(pe):
            pe.wait_ge(router_loaded.sem, 16)
            pe.sem_inc(s_done.sem, s_done.credit)
            pe.sem_inc(u_done.sem, u_done.credit)

            def slot(g, a, p, r):
                if g is not None:
                    if a is not None:
                        pe.wait_ge(yb_ready.sem, yb_ready.at(g - 1))
                    pe.wait_ge(n1.h_ready.sem, n1.h_ready.at(g))
                    pe.transpose(pM[:, 0, :], n1.h[:, :], ident).then_inc(hT_done.sem, 1)
                if a is not None:
                    pe.wait_ge(n2.h_ready.sem, n2.h_ready.at(a))
                    pe.transpose(pN[:, 0, :], n2.h[:, :], ident).then_inc(h2T_done.sem, 1)
                if g is not None:
                    pe.wait_ge(hT_ready.sem, hT_ready.at(g))
                    pe.matmul(pM[:, 1, :], w("wq0"), hT[:, :], start=True, stop=True).then_inc(q_done.sem, 1)
                if a is not None:
                    pe.wait_ge(h2T_ready.sem, h2T_ready.at(a))
                    for j, name in enumerate(("aq", "ak", "aqr", "akr")):
                        mm = pe.matmul(pQ[:, 0, j * P:(j + 1) * P], w(name), hT2[:, :], start=True, stop=True)
                    mm.then_inc(qk_done.sem, 1)
                    for b in range(BG):
                        for h in range(HQ):
                            mm = pe.matmul(pQ[h * T:(h + 1) * T, 1, b * D:(b + 1) * D], hT2[:, b * T:(b + 1) * T], w("av"),
                                           start=True, stop=True)
                    mm.then_inc(vq_done.sem, 1)
                if g is not None:
                    pe.wait_ge(q_ready.sem, q_ready.at(g))
                    pe.matmul(pM[:, 2, :], w("wk0"), q[:, :], start=True, stop=True)
                    pe.matmul(pM[:, 3, 0:1], q[:, :], v("bk0"), start=True, stop=True).then_inc(q2_done.sem, 1)
                    pe.wait_ge(q2_ready.sem, q2_ready.at(g))
                    pe.wait_ge(ctx_loaded[p].sem, ctx_loaded[p].at(r))
                    for b in range(BG):
                        mm = pe.matmul(pS[b * T:(b + 1) * T, 0:S], q2[:, b * T:(b + 1) * T], ctxT[:, p, b, :],
                                       start=True, stop=True)
                    mm.then_inc(s_done.sem, 1)
                if a is not None:
                    pe.wait_ge(kq_ready.sem, kq_ready.at(a))
                    pe.wait_ge(vq_ready.sem, vq_ready.at(a))
                    carry(pe, ctx)
                    for b in range(BG):
                        for c in range(NQ):
                            r = slice(c * T, (c + 1) * T)
                            mm = pe.matmul(pQ[b * T:(b + 1) * T, c, 0:P], qk[r, 0, b * T:(b + 1) * T],
                                           kquad[r, b, :, :], start=True, stop=True)
                    mm.then_inc(ss_done.sem, 1)
                    pe.wait_ge(se_ready.sem, se_ready.at(a))
                    for c in range(NQ):
                        mm = pe.transpose(pN[:, c, :], se[:, c * HQ:(c + 1) * HQ, :], ident)
                    mm.then_inc(seT_done.sem, 1)
                    pe.wait_ge(seT_ready.sem, seT_ready.at(a))
                    for b in range(BG):
                        for c in range(NQ):
                            mm = pe.matmul(pN[b * T:(b + 1) * T, 0, c * T:(c + 1) * T], seT[:, c, b * T:(b + 1) * T],
                                           vq[:, b, c * T:(c + 1) * T], start=True, stop=True)
                    mm.then_inc(o_done.sem, 1)
                    pe.wait_ge(o_ready.sem, o_ready.at(a))
                    pe.transpose(pN[:, 1, :], o[:, :], ident).then_inc(oT_done.sem, 1)
                    pe.wait_ge(oT_ready.sem, oT_ready.at(a))
                    pe.matmul(pN[:, 2, :], oT[:, :], w("ao"), start=True, stop=True).then_inc(y2_done.sem, 1)
                if g is not None:
                    pe.wait_ge(pL_ready.sem, pL_ready.at(g))
                    for c in range(SC):
                        pe.transpose(pT[:, c * P:(c + 1) * P], pr[:, c * P:(c + 1) * P], ident)
                    pe.transpose(pT[0:BG, SM:SM + P], prL[:, :], ident).then_inc(pT_done.sem, 1)
                    pe.wait_ge(pT_ready.sem, pT_ready.at(g))
                    for c in range(SC):
                        for b in range(BG):
                            pe.matmul(pM[b * T:(b + 1) * T, 0, :], prT[:, c, b * T:(b + 1) * T], ctxN[:, p, c, b, :],
                                      start=(c == 0), stop=False, skip_group_check=True)
                    pe.matmul(pM[:, 0, :], prLT[:, :], ctxL[:, p, :], start=False, stop=True,
                              skip_group_check=True).then_inc(u_done.sem, 1)
                    pe.wait_ge(u_ready.sem, u_ready.at(g))
                    pe.transpose(pM[:, 1, :], u[:, :], ident).then_inc(uT_done.sem, 1)
                if a is not None:
                    pe.wait_ge(n3.h_ready.sem, n3.h_ready.at(a))
                    pe.transpose(pN[:, 3, :], n3.h[:, :], ident).then_inc(h3T_done.sem, 1)
                if g is not None:
                    pe.wait_ge(uT_ready.sem, uT_ready.at(g))
                    pe.matmul(pM[:, 2, :], w("wv0"), uT[:, :], start=True, stop=True).then_inc(v_done.sem, 1)
                if a is not None:
                    pe.wait_ge(h3T_ready.sem, h3T_ready.at(a))
                    pe.matmul(pN[:, 0, 0:E], h3T[:, :], wr[:, :], start=True, stop=True).then_inc(lg_done.sem, 1)
                if g is not None:
                    pe.wait_ge(v_ready.sem, v_ready.at(g))
                    pe.matmul(pM[:, 3, :], vT[:, :], w("wo0"), start=True, stop=True).then_inc(y_done.sem, 1)

            slots(pe, slot)

        @block.scalar
        def _(act):
            def slot(g, a, p, r):
                if g is not None:
                    act.wait_ge(hT_done.sem, hT_done.at(g))
                    act.activation(hT[:, :], pM[:, 0, :], ACT.Copy).then_inc(hT_ready.sem, 1)
                if a is not None:
                    act.wait_ge(h2T_done.sem, h2T_done.at(a))
                    act.activation(hT2[:, :], pN[:, 0, :], ACT.Copy).then_inc(h2T_ready.sem, 1)
                if g is not None:
                    act.wait_ge(q_done.sem, q_done.at(g))
                    act.activation(q[:, :], pM[:, 1, :], ACT.Identity, bias=v("bq0")).then_inc(q_ready.sem, 1)
                    act.wait_ge(q2_done.sem, q2_done.at(g))
                    act.activation(qb[:, :], pM[:, 3, 0:1], ACT.Copy).then_inc(qb_ready.sem, 1)
                    act.activation(q2[:, :], pM[:, 2, :], ACT.Copy).then_inc(q2_ready.sem, 1)
                    act.wait_ge(s_done.sem, s_done.at(g))
                    act.wait_ge(qb_ready.sem, qb_ready.at(g))
                    act.activation(sc[:, :], pS[:, 0:S], ACT.Identity, bias=qb[:, :]).then_inc(s_ready.sem, 1)
                    act.wait_ge(nmax_ready.sem, nmax_ready.at(g))
                    act.activation(ex[:, :], sc[:, :], ACT.Exp, bias=nmax[:, :], scale=SCALE).then_inc(e_ready.sem, 1)
                if a is not None:
                    act.wait_ge(sd_ready.sem, sd_ready.at(a))
                    act.activation(se[:, :, :], sd[:, :, :], ACT.Exp, scale=SCALE2).then_inc(se_ready.sem, 1)
                    act.wait_ge(seT_done.sem, seT_done.at(a))
                    act.activation(seT[:, :, :], pN[:, :, :], ACT.Copy).then_inc(seT_ready.sem, 1)
                    act.wait_ge(oT_done.sem, oT_done.at(a))
                    act.activation(oT[:, :], pN[:, 1, :], ACT.Copy).then_inc(oT_ready.sem, 1)
                if g is not None:
                    act.wait_ge(pT_done.sem, pT_done.at(g))
                    act.activation(prT[:, :, :], pT[:, 0:SM].rearrange("p (c t) -> p c t", c=SC), ACT.Copy).then_inc(pT_ready.sem, 1)
                    act.activation(prLT[:, :], pT[0:BG, SM:SM + P], ACT.Copy).then_inc(pT_ready.sem, 1)
                    act.wait_ge(rinv_ready.sem, rinv_ready.at(g))
                    act.wait_ge(u_done.sem, u_done.at(g))
                    act.activation(u[:, :], pM[:, 0, :], ACT.Copy, scale=rinv[:, :]).then_inc(u_ready.sem, 1)
                    act.wait_ge(uT_done.sem, uT_done.at(g))
                    act.activation(uT[:, :], pM[:, 1, :], ACT.Copy).then_inc(uT_ready.sem, 1)
                if a is not None:
                    act.wait_ge(h3T_kept.sem, h3T_kept.at(a, 0))
                    act.wait_ge(h3T_done.sem, h3T_done.at(a))
                    act.activation(h3T[:, :], pN[:, 3, :], ACT.Copy).then_inc(h3T_ready.sem, 1)
                if g is not None:
                    act.wait_ge(v_done.sem, v_done.at(g))
                    act.activation(vT[:, :], pM[:, 2, :], ACT.Identity, bias=v("bv0")).then_inc(v_ready.sem, 1)

            slots(act, slot)

        @block.gpsimd
        def _(pool):
            pool.sem_inc(h3T_kept.sem, h3T_kept.credit)
            n1.gpsimd(pool, 0)

            def slot(g, a, p, r):
                if a is not None:
                    n2.gpsimd(pool, a)
                    pool.wait_ge(qk_ready.sem, qk_ready.at(a))
                    pool.tensor_tensor(kquad[:, :, :, :],
                                       qk[:, 1, :].rearrange("p (b s) -> p b s", b=BG).unsqueeze(2).broadcast_to([P, BG, HQ, T]),
                                       k("quad").unsqueeze(1).unsqueeze(3).broadcast_to([P, BG, HQ, T]), ALU.mult
                                       ).then_inc(kq_ready.sem, 1)
                    n3.gpsimd(pool, a)
                if g is not None and not (isinstance(g, int) and g == G - 1):
                    n1.gpsimd(pool, g + 1)
                if a is not None:
                    pool.wait_ge(h3T_ready.sem, h3T_ready.at(a))
                    pool.tensor_copy(HT_all[:, bass.ds(a, 1), :].rearrange("p g t -> p (g t)"), h3T[:, :]).then_inc(h3T_kept.sem, 1)

            slots(pool, slot)

        @block.vector
        def _(dve):
            def x_of(g):
                return X[:, bass.ds(g, 1), :].rearrange("p g d -> p (g d)")

            n1.vector_stats(dve, X[:, 0, :], 0)
            n1.vector_scale(dve, X[:, 0, :], 0)

            def slot(g, a, p, r):
                if a is not None:
                    n2.vector_stats(dve, x_of(a), a)
                    n2.vector_scale(dve, x_of(a), a)
                    dve.wait_ge(qk_done.sem, qk_done.at(a))
                    dve.tensor_tensor(rot[:, :, :, :], pQ[:, 0, :].rearrange("p (c n t) -> p c n t", c=2, t=T),
                                      k("rope").rearrange("p (c t) -> p c t", c=2).unsqueeze(2).broadcast_to([P, 2, 8, T]),
                                      ALU.mult).then_inc(rot_ready.sem, 1)
                    dve.wait_ge(rot_ready.sem, rot_ready.at(a))
                    dve.tensor_tensor(qk[:, :, :].rearrange("p a t -> p (a t)"), rot[:, 0, :, :].rearrange("p n t -> p (n t)"),
                                      rot[:, 1, :, :].rearrange("p n t -> p (n t)"), ALU.add).then_inc(qk_ready.sem, 1)
                    dve.wait_ge(vq_done.sem, vq_done.at(a))
                    dve.tensor_tensor(vq[:, :, :], pQ[:, 1, :].rearrange("p (b d) -> p b d", b=BG),
                                      k("vmask").unsqueeze(1).broadcast_to([P, BG, D]), ALU.mult).then_inc(vq_ready.sem, 1)
                if g is not None:
                    dve.wait_ge(s_ready.sem, s_ready.at(g))
                    carry(dve, ctx)
                    n = 0
                    for r in range(TOP // 8):
                        src = sc if r == 0 else work
                        dve.max(top[:, r * 8:r * 8 + 8], src[:, :]).then_inc(topk.sem, 1)
                        n += 1
                        dve.wait_ge(topk.sem, topk.at(g, n))
                        carry(dve, ctx)
                        if r == 0:
                            dve.tensor_scalar(nmax[:, :], top[:, 0:1], -SCALE, None, ALU.mult).then_inc(nmax_ready.sem, 1)
                        dve.match_replace(work[:, :], top[:, r * 8:r * 8 + 8], src[:, :], NEG).then_inc(topk.sem, 1)
                        n += 1
                        dve.wait_ge(topk.sem, topk.at(g, n))
                        carry(dve, ctx)
                if a is not None:
                    dve.wait_ge(ss_done.sem, ss_done.at(a))
                    s4 = pQ[:, :, 0:P].rearrange("p c (h s) -> p c h s", h=HQ)
                    dve.tensor_reduce(smax[:, :], s4, AX.X, ALU.max).then_inc(smax_ready.sem, 1)
                    dve.wait_ge(smax_ready.sem, smax_ready.at(a))
                    dve.tensor_tensor(sd[:, :, :].rearrange("p (c h) s -> p c h s", c=NQ), s4,
                                      smax[:, :].rearrange("p (c h) -> p c h", c=NQ).unsqueeze(3).broadcast_to([P, NQ, HQ, T]),
                                      ALU.subtract).then_inc(sd_ready.sem, 1)
                if g is not None:
                    dve.wait_ge(e_ready.sem, e_ready.at(g))
                    dve.scalar_tensor_tensor(pr[:, :], work[:, :], NEG, ex[:, :], ALU.is_equal, ALU.mult,
                                             accum_out=rsum[:, :]).then_inc(p_ready.sem, 1)
                    dve.wait_ge(p_ready.sem, p_ready.at(g))
                    dve.tensor_scalar(prL[:, :], k("batch"), pr[:, SM:S], None, ALU.mult).then_inc(pL_ready.sem, 1)
                    dve.reciprocal(rinv[:, :], rsum[:, :]).then_inc(rinv_ready.sem, 1)
                if a is not None:
                    dve.wait_ge(se_ready.sem, se_ready.at(a))
                    dve.tensor_reduce(ssum[:, :], se[:, :, :], AX.X, ALU.add).then_inc(ssum_ready.sem, 1)
                    dve.wait_ge(ssum_ready.sem, ssum_ready.at(a))
                    dve.reciprocal(sinv[:, :], ssum[:, :]).then_inc(sinv_ready.sem, 1)
                    dve.wait_ge(sinv_ready.sem, sinv_ready.at(a))
                    dve.wait_ge(o_done.sem, o_done.at(a))
                    dve.tensor_tensor(o[:, :].rearrange("p (h d) -> p h d", h=H), pN[:, 0, :].rearrange("p (h d) -> p h d", h=H),
                                      sinv[:, :].unsqueeze(2).broadcast_to([P, H, HD]), ALU.mult).then_inc(o_ready.sem, 1)
                    dve.wait_ge(y2_done.sem, y2_done.at(a))
                    dve.tensor_tensor(x_of(a), pN[:, 2, :], x_of(a), ALU.add).then_inc(x2_ready.sem, 1)
                    dve.wait_ge(x2_ready.sem, x2_ready.at(a))
                    carry(dve, ctx)
                    n3.vector_stats(dve, x_of(a), a)
                    n3.vector_scale(dve, x_of(a), a)
                if g is not None:
                    if not (isinstance(g, int) and g == G - 1):
                        n1.vector_stats(dve, x_of(g + 1), g + 1)
                        n1.vector_scale(dve, x_of(g + 1), g + 1)
                    dve.wait_ge(y_done.sem, y_done.at(g))
                    dve.tensor_tensor(yb[:, :], pM[:, 3, :], bo0[:, :], ALU.add).then_inc(yb_ready.sem, 1)
                    dve.wait_ge(yb_ready.sem, yb_ready.at(g))
                    dve.tensor_tensor(x_of(g), yb[:, :], x_of(g), ALU.add).then_inc(x1_ready.sem, 1)
                    dve.wait_ge(x1_ready.sem, x1_ready.at(g))
                    carry(dve, ctx)
                if a is not None:
                    dve.wait_ge(lg_done.sem, lg_done.at(a))
                    dve.tensor_copy(LG[:, bass.ds(a, 1), :].rearrange("p g e -> p (g e)"), pN[:, 0, 0:E]).then_inc(lg_ready.sem, 1)

            slots(dve, slot)


def route_layer0(env):
    nc, LG, MASK, k = (env[n] for n in ("nc", "LG", "MASK", "k"))
    ctx = Phase(nc, "r")
    with ctx:
        def sb(name, shape, dt=F32):
            return ctx.enter_context(nc.sbuf_tensor("r_" + name, shape, dt))

        def sig(name, per=1, credit=0):
            return Signal(ctx, nc, "r_" + name, per, credit)

        lmax, d, e8, sm, prob = sb("lmax", [P, G]), sb("d", [P, G, E]), sb("e8", [P, G, E]), sb("sum", [P, G]), sb("prob", [P, G])
        eq, first, hot = sb("eq", [P, G, E]), sb("first", [P, G]), sb("hot", [P, G, E])
        pm, hit = sb("pm", [P, G, E]), sb("hit", [P, G, E])
        least, cand, bit, count, kept = (sb("least", [P, E], I32), sb("cand", [P, E], I32), sb("bit", [P, 1], I32),
                                         sb("count", [P, E]), sb("kept", [P, E]))
        over, same, need, scan, rank, fit = (sb("over", [P, G, E]), sb("same", [P, G, E]), sb("need", [P, E]),
                                             sb("scan", [P, E, G]), sb("rank", [P, G, E]), sb("fit", [P, G, E]))
        held = sb("held", [P, G])
        pC = ctx.enter_context(nc.psum_tensor("r_pC", [P, 512], F32))
        pB = ctx.enter_context(nc.psum_tensor("r_pB", [P, 512], F32))
        d_ready, e_ready = sig("d_ready"), sig("e_ready")
        step = sig("step", 1)
        found = sig("found", 7)
        count_ready, total_ready = sig("count_ready"), sig("total_ready")
        over_ready, over_total = sig("over_ready"), sig("over_total")
        same_ready, same_total = sig("same_ready"), sig("same_total")
        block = ctx.enter_context(nc.Block())

        def per_group(t):
            return t[:, :].unsqueeze(2).broadcast_to([P, G, E])

        def per_expert(t):
            return t.unsqueeze(1).broadcast_to([P, G, E])

        @block.scalar
        def _(act):
            act.wait_ge(d_ready.sem, 1)
            act.activation(e8[:, :, :], d[:, :, :], ACT.Exp).then_inc(e_ready.sem, 1)

        @block.tensor
        def _(pe):
            with pe.Fori(0, PROB_BITS) as n:
                pe.wait_ge(count_ready.sem, count_ready.at(n))
                pe.matmul(pC[:, 0:E], k("ones"), count[:, :], start=True, stop=True).then_inc(total_ready.sem, 1)
            pe.wait_ge(over_ready.sem, 1)
            pe.matmul(pC[:, 0:E], k("ones"), count[:, :], start=True, stop=True).then_inc(over_total.sem, 1)
            pe.wait_ge(same_ready.sem, 1)
            pe.matmul(pB[:, 0:G * E], k("ones"), same[:, :, :], start=True, stop=True)
            pe.matmul(pB[:, G * E:2 * G * E], k("before"), same[:, :, :], start=True, stop=True).then_inc(same_total.sem, 1)

        @block.vector
        def _(dve):
            done = [0]

            def then(ins):
                done[0] += 1
                ins.then_inc(step.sem, 1)
                dve.wait_ge(step.sem, done[0])

            then(dve.tensor_reduce(lmax[:, :], LG[:, :, :], AX.X, ALU.max))
            dve.tensor_tensor(d[:, :, :], LG[:, :, :], per_group(lmax), ALU.subtract).then_inc(d_ready.sem, 1)
            then(dve.tensor_tensor(eq[:, :, :], LG[:, :, :], per_group(lmax), ALU.is_equal))
            then(dve.tensor_tensor(eq[:, :, :], eq[:, :, :], per_expert(k("rank")), ALU.mult))
            then(dve.tensor_reduce(first[:, :], eq[:, :, :], AX.X, ALU.max))
            then(dve.tensor_tensor(hot[:, :, :], eq[:, :, :], per_group(first), ALU.is_equal))
            dve.wait_ge(e_ready.sem, 1)
            then(dve.tensor_reduce(sm[:, :], e8[:, :, :], AX.X, ALU.add))
            then(dve.reciprocal(prob[:, :], sm[:, :]))
            then(dve.tensor_tensor(pm[:, :, :], hot[:, :, :], per_group(prob), ALU.mult))
            then(dve.memset(least[:, :], FIRST_PROB))
            then(dve.memset(bit[:, :], 1 << (PROB_BITS - 1)))
            with dve.Fori(0, PROB_BITS) as n:
                at = [0]

                def then_bit(ins):
                    at[0] += 1
                    ins.then_inc(found.sem, 1)
                    dve.wait_ge(found.sem, found.at(n, at[0]))

                then_bit(dve.tensor_tensor(cand[:, :], least[:, :], bit[:, 0:1].broadcast_to([P, E]), ALU.bitwise_or))
                then_bit(dve.tensor_tensor(hit[:, :, :], pm[:, :, :], per_expert(cand[:, :].bitcast(F32)), ALU.is_ge))
                dve.tensor_reduce(count[:, :], hit[:, :, :].rearrange("p g e -> p e g"), AX.X, ALU.add).then_inc(count_ready.sem, 1)
                then_bit(dve.tensor_single_scalar(bit[:, :], bit[:, :], 1, ALU.logical_shift_right))
                dve.wait_ge(total_ready.sem, total_ready.at(n))
                then_bit(dve.tensor_scalar(kept[:, :], pC[:, 0:E], float(CAP), None, ALU.is_ge))
                then_bit(dve.tensor_tensor(kept[:, :], kept[:, :], cand[:, :].bitcast(F32), ALU.mult))
                then_bit(dve.tensor_tensor(least[:, :].bitcast(F32), least[:, :].bitcast(F32), kept[:, :], ALU.max))
                then_bit(dve.memset(kept[:, :], 0.0))
            then(dve.tensor_tensor(over[:, :, :], pm[:, :, :], per_expert(least[:, :].bitcast(F32)), ALU.is_gt))
            dve.tensor_reduce(count[:, :], over[:, :, :].rearrange("p g e -> p e g"), AX.X, ALU.add).then_inc(over_ready.sem, 1)
            dve.tensor_tensor(same[:, :, :], pm[:, :, :], per_expert(least[:, :].bitcast(F32)), ALU.is_equal).then_inc(same_ready.sem, 1)
            dve.wait_ge(over_total.sem, 1)
            then(dve.tensor_scalar(need[:, :], pC[:, 0:E], -1.0, float(CAP), ALU.mult, ALU.add))
            dve.wait_ge(same_total.sem, 1)
            totals = pB[:, 0:G * E].rearrange("p (g e) -> p g e", e=E)
            for e in range(E):
                last = dve.tensor_tensor_scan(scan[:, e, :], k("ones")[:, 0:G], totals[:, :, e], 0.0, ALU.mult, ALU.add)
                if e < E - 1:
                    last.then_inc(step.sem, 1)
                    done[0] += 1
            then(last)
            then(dve.tensor_tensor(rank[:, :, :], scan[:, :, :].rearrange("p e g -> p g e"), totals, ALU.subtract))
            then(dve.tensor_tensor(rank[:, :, :], rank[:, :, :], pB[:, G * E:2 * G * E].rearrange("p (g e) -> p g e", e=E), ALU.add))
            then(dve.tensor_tensor(fit[:, :, :], rank[:, :, :], per_expert(need[:, :]), ALU.is_lt))
            then(dve.tensor_tensor(fit[:, :, :], fit[:, :, :], same[:, :, :], ALU.mult))
            then(dve.tensor_tensor(MASK[:, :, :], over[:, :, :], fit[:, :, :], ALU.add))
            then(dve.tensor_reduce(held[:, :], MASK[:, :, 1:E], AX.X, ALU.add))
            then(dve.tensor_scalar(MASK[:, :, 0], held[:, :], -1.0, 1.0, ALU.mult, ALU.add))


def gate_layer1(env):
    nc, LG, MASK, k = (env[n] for n in ("nc", "LG", "MASK", "k"))
    ctx = Phase(nc, "t")
    with ctx:
        def sb(name, shape, dt=F32):
            return ctx.enter_context(nc.sbuf_tensor("t_" + name, shape, dt))

        def sig(name, per=1, credit=0):
            return Signal(ctx, nc, "t_" + name, per, credit)

        lmax, d, gates, sm, inv = sb("lmax", [P, G]), sb("d", [P, G, E]), sb("gates", [P, G, E]), sb("sum", [P, G]), sb("inv", [P, G])
        eq, first, hot, rest = sb("eq", [P, G, E]), sb("first", [P, G]), [sb("hot0", [P, G, E]), sb("hot1", [P, G, E])], sb("rest", [P, G, E])
        best = [sb("best0", [P, G]), sb("best1", [P, G])]
        d_ready, e_ready, step = sig("d_ready"), sig("e_ready"), sig("step")
        block = ctx.enter_context(nc.Block())

        def per_group(t):
            return t[:, :].unsqueeze(2).broadcast_to([P, G, E])

        @block.scalar
        def _(act):
            act.wait_ge(d_ready.sem, 1)
            act.activation(gates[:, :, :], d[:, :, :], ACT.Exp).then_inc(e_ready.sem, 1)

        @block.vector
        def _(dve):
            done = [0]

            def then(ins):
                done[0] += 1
                ins.then_inc(step.sem, 1)
                dve.wait_ge(step.sem, done[0])

            then(dve.tensor_reduce(lmax[:, :], LG[:, :, :], AX.X, ALU.max))
            dve.tensor_tensor(d[:, :, :], LG[:, :, :], per_group(lmax), ALU.subtract).then_inc(d_ready.sem, 1)
            dve.wait_ge(e_ready.sem, 1)
            then(dve.tensor_reduce(sm[:, :], gates[:, :, :], AX.X, ALU.add))
            then(dve.reciprocal(inv[:, :], sm[:, :]))
            then(dve.tensor_tensor(gates[:, :, :], gates[:, :, :], per_group(inv), ALU.mult))
            for n in range(2):
                src = gates if n == 0 else rest
                then(dve.tensor_reduce(best[n][:, :], src[:, :, :], AX.X, ALU.max))
                then(dve.tensor_tensor(eq[:, :, :], src[:, :, :], per_group(best[n]), ALU.is_equal))
                then(dve.tensor_tensor(eq[:, :, :], eq[:, :, :], k("rank").unsqueeze(1).broadcast_to([P, G, E]), ALU.mult))
                then(dve.tensor_reduce(first[:, :], eq[:, :, :], AX.X, ALU.max))
                then(dve.tensor_tensor(hot[n][:, :, :], eq[:, :, :], per_group(first), ALU.is_equal))
                if n == 0:
                    then(dve.scalar_tensor_tensor(rest[:, :, :], hot[0][:, :, :], -2.0, gates[:, :, :], ALU.mult, ALU.add))
            then(dve.tensor_tensor(sm[:, :], best[0][:, :], best[1][:, :], ALU.add))
            then(dve.tensor_scalar(sm[:, :], sm[:, :], 1e-8, None, ALU.add))
            then(dve.reciprocal(inv[:, :], sm[:, :]))
            then(dve.tensor_tensor(hot[0][:, :, :], hot[0][:, :, :], hot[1][:, :, :], ALU.add))
            then(dve.tensor_tensor(gates[:, :, :], gates[:, :, :], hot[0][:, :, :], ALU.mult))
            then(dve.tensor_tensor(MASK[:, :, :], gates[:, :, :], per_group(inv), ALU.mult))


def experts(env, name, w1_in, w2_in, b2_in, NF, vb1, out):
    nc, X, HT_all, MASK, k, vec = (env[n] for n in ("nc", "X", "HT_all", "MASK", "k", "vec"))
    ctx = Phase(nc, name)
    with ctx:
        def sb(n, shape, dt=F32):
            return ctx.enter_context(nc.sbuf_tensor(f"{name}_{n}", shape, dt))

        def sig(n, per=1, credit=0):
            return Signal(ctx, nc, f"{name}_{n}", per, credit)

        N = TG * P
        w1, w2, b2 = sb("w1", [P, E, NF * P]), sb("w2", [P, E, NF, D]), sb("b2", [E, D])
        mk, mkT = sb("mk", [P, TG, E]), sb("mkT", [E, TG, P])
        hid = sb("hid", [P, 2, NF, N])
        pH = ctx.enter_context(nc.psum_tensor(f"{name}_pH", [P, 4, N], F32))
        pY = ctx.enter_context(nc.psum_tensor(f"{name}_pY", [P, 2, TG, D], F32))
        pB = ctx.enter_context(nc.psum_tensor(f"{name}_pB", [P, TG, D], F32))
        w_loaded = [ctx.semaphore(f"{name}_w_loaded{e}") for e in range(E)]
        b2_loaded = ctx.semaphore(f"{name}_b2_loaded")
        mk_ready, mkT_done, mkT_ready = sig("mk_ready"), sig("mkT_done"), sig("mkT_ready")
        b_done, b_added = sig("b_done"), sig("b_added", TG)
        h_done, h_ready = sig("h_done", E * NF), sig("h_ready", E * NF, credit=4)
        y_done, y_added = sig("y_done", E, credit=2), sig("y_added", E * TG, credit=2 * TG)
        stored = ctx.semaphore(f"{name}_stored")
        block = ctx.enter_context(nc.Block())

        @block.sync
        def _(sp):
            for e in range(E):
                sp.dma_start(w1[:, e, :], w1_in[:, e, :]).then_inc(w_loaded[e], 16)
                sp.dma_start(w2[:, e, :, :], w2_in[:, e, :, :]).then_inc(w_loaded[e], 16)
            sp.dma_start(b2[:, :], b2_in).then_inc(b2_loaded, 16)
            if out is not None:
                with sp.Fori(0, NB) as n:
                    sp.wait_ge(y_added.sem, y_added.at(n))
                    sp.dma_start(out.rearrange("(g bb) t d -> (bb t) g d", bb=BG)[:, bass.ds(n * TG, TG), :],
                                 X[:, bass.ds(n * TG, TG), :]).then_inc(stored, 16)
                sp.wait_ge(stored, 16 * NB)

        @block.tensor
        def _(pe):
            for e in range(E):
                pe.wait_ge(w_loaded[e], 32)
            pe.wait_ge(b2_loaded, 16)
            pe.sem_inc(y_done.sem, y_done.credit)
            with pe.Fori(0, NB) as n:
                pe.wait_ge(mk_ready.sem, mk_ready.at(n))
                for t in range(TG):
                    mm = pe.transpose(pB[0:E, t, :], mk[:, t, :], k("ident"))
                mm.then_inc(mkT_done.sem, 1)
                pe.wait_ge(mkT_ready.sem, mkT_ready.at(n))
                for t in range(TG):
                    mm = pe.matmul(pB[:, t, :], mkT[:, t, :], b2[:, :], start=True, stop=True)
                mm.then_inc(b_done.sem, 1)

                def up(e):
                    for c in range(NF):
                        m = e * NF + c
                        pe.wait_ge(h_ready.sem, h_ready.at(n, m + 1) - 4)
                        pe.matmul(pH[:, m % 4, :], w1[:, e, c * P:(c + 1) * P],
                                  HT_all[:, bass.ds(n * TG, TG), :].rearrange("p g t -> p (g t)"),
                                  start=True, stop=True).then_inc(h_done.sem, 1)

                def down(e):
                    pe.wait_ge(h_ready.sem, h_ready.at(n, (e + 1) * NF))
                    pe.wait_ge(y_added.sem, y_added.at(n, (e - 1) * TG))
                    for t in range(TG):
                        for c in range(NF):
                            mm = pe.matmul(pY[:, e % 2, t, :], hid[:, e % 2, c, t * P:(t + 1) * P], w2[:, e, c, :],
                                           start=(c == 0), stop=(c == NF - 1))
                    mm.then_inc(y_done.sem, 1)

                up(0)
                for e in range(E):
                    if e + 1 < E:
                        up(e + 1)
                    down(e)

        @block.scalar
        def _(act):
            act.sem_inc(h_ready.sem, h_ready.credit)
            with act.Fori(0, NB) as n:
                act.wait_ge(mkT_done.sem, mkT_done.at(n))
                act.activation(mkT[:, :, :], pB[0:E, :, :], ACT.Copy).then_inc(mkT_ready.sem, 1)
                for e in range(E):
                    act.wait_ge(y_done.sem, y_done.at(n, e - 1))
                    for c in range(NF):
                        m = e * NF + c
                        act.wait_ge(h_done.sem, h_done.at(n, m + 1))
                        act.activation(hid[:, e % 2, c, :], pH[:, m % 4, :], ACT.Relu, bias=vec[:, vb1 + m:vb1 + m + 1]
                                       ).then_inc(h_ready.sem, 1)

        @block.vector
        def _(dve):
            dve.sem_inc(y_added.sem, y_added.credit)
            with dve.Fori(0, NB) as n:
                dve.tensor_copy(mk[:, :, :], MASK[:, bass.ds(n * TG, TG), :]).then_inc(mk_ready.sem, 1)
                dve.wait_ge(mk_ready.sem, mk_ready.at(n))
                dve.wait_ge(b_done.sem, b_done.at(n))
                for t in range(TG):
                    x = X[:, bass.ds(n * TG + t, 1), :].rearrange("p g d -> p (g d)")
                    dve.tensor_tensor(x, pB[:, t, :], x, ALU.add).then_inc(b_added.sem, 1)
                dve.wait_ge(b_added.sem, b_added.at(n))
                for e in range(E):
                    dve.wait_ge(y_done.sem, y_done.at(n, e + 1))
                    if e > 0:
                        dve.wait_ge(y_added.sem, y_added.at(n, e * TG))
                    for t in range(TG):
                        x = X[:, bass.ds(n * TG + t, 1), :].rearrange("p g d -> p (g d)")
                        dve.scalar_tensor_tensor(x, pY[:, e % 2, t, :], mk[:, t, e:e + 1], x, ALU.mult, ALU.add
                                                 ).then_inc(y_added.sem, 1)
                dve.wait_ge(y_added.sem, y_added.at(n))


def cross_layer1(env):
    nc, io, X, w, v, k, bo1 = (env[n] for n in ("nc", "io", "X", "w", "v", "k", "bo1"))
    ctx = Phase(nc, "c")
    with ctx:
        def sb(name, shape, dt=F32):
            return ctx.enter_context(nc.sbuf_tensor("c_" + name, shape, dt))

        def ps(name, shape):
            return ctx.enter_context(nc.psum_tensor("c_" + name, shape, F32))

        def sig(name, per=1, credit=0):
            return Signal(ctx, nc, "c_" + name, per, credit)

        ctxT = sb("ctxT", [P, BG, S])
        hT, q = sb("hT", [P, P]), sb("q", [P, P])
        qq = sb("qq", [P, 2, HQ, T])
        ks = sb("ks", [P, 2, S])
        vs, vl = sb("vs", [P, BG, SC, D]), sb("vl", [NQ, BG, D])
        nm, den, rinv = sb("nm", [P, NQ]), sb("den", [P, 2, NQ]), sb("rinv", [P, BG, NQ])
        pr = sb("pr", [P, 2, NQ, S])
        prT, prl = sb("prT", [P, SC, NQ, P]), sb("prl", [NQ, P])
        rm = sb("rm", [P, BG, NQ, HQ * HD])
        om, osum, on, ob, yb = sb("om", [P, BG, HQ, T]), sb("osum", [P, BG, T]), sb("on", [P, P]), sb("ob", [P, P]), sb("yb", [P, D])
        pS = ps("pS", [P, NQ, 512])
        pT = ps("pT", [P, SC, NQ, P])
        pM = ps("pM", [P, 512])
        pO = ps("pO", [P, BG, HQ, T])

        n4 = Norm(ctx, nc, "c_n4", env)
        ctx_loaded = [sig(f"ctx_loaded{b}", 16) for b in range(BG)]
        hT_done, hT_ready, q_done, q_ready = sig("hT_done"), sig("hT_ready"), sig("q_done"), sig("q_ready")
        qq_ready = sig("qq_ready")
        k_done, k_ready = sig("k_done"), sig("k_ready")
        v_done, v_ready = sig("v_done", credit=BG), sig("v_ready")
        vl_ready, prl_ready = sig("vl_ready"), sig("prl_ready")
        s_done, max_ready, e_ready = sig("s_done", NQ), sig("max_ready", NQ), sig("e_ready", NQ, credit=NQ)
        pT_done, pT0_ready, pT1_ready = sig("pT_done"), sig("pT0_ready"), sig("pT1_ready")
        o_done, rinv_ready, rm_ready = sig("o_done"), sig("rinv_ready"), sig("rm_ready")
        om_ready, osum_ready = sig("om_ready"), sig("osum_ready")
        rT_done, on_ready, ob_ready, y_done, yb_ready, x_ready = (sig("rT_done"), sig("on_ready"), sig("ob_ready"), sig("y_done"),
                                                                 sig("yb_ready"), sig("x_ready"))
        SCALE = float(HD) ** -0.5

        block = ctx.enter_context(nc.Block())

        @block.sync
        def _(sp):
            with sp.Fori(0, G) as g:
                for b in range(BG):
                    sp.wait_ge(v_done.sem, v_done.at(g * BG + b - BG))
                    sp.dma_start(ctxT[:, b, :].unsqueeze(1), io["ctxT"][bass.ds(g, 1), :, b, :].rearrange("g p s -> p g s")
                                 ).then_inc(ctx_loaded[b].sem, 16)

        @block.tensor
        def _(pe):
            pe.sem_inc(v_done.sem, v_done.credit)

            def norm_T(g):
                pe.wait_ge(n4.h_ready.sem, n4.h_ready.at(g))
                pe.transpose(pM[:, 0:P], n4.h[:, :], k("ident")).then_inc(hT_done.sem, 1)

            def queries(g):
                pe.wait_ge(hT_ready.sem, hT_ready.at(g))
                pe.matmul(pM[:, P:2 * P], w("wq1"), hT[:, :], start=True, stop=True).then_inc(q_done.sem, 1)

            def keys(g, b, n):
                pe.wait_ge(ctx_loaded[b].sem, ctx_loaded[b].at(g))
                pe.matmul(pM[:, 0:S], w("wk1"), ctxT[:, b, :], start=True, stop=True).then_inc(k_done.sem, 1)

            def values(b, n):
                pe.wait_ge(k_ready.sem, k_ready.at(n))
                for c in range(SC):
                    pe.matmul(pM[:, c * D:(c + 1) * D], ctxT[:, b, c * P:(c + 1) * P], w("wv1"), start=True, stop=True)
                return pe.matmul(pM[0:NQ, SC * D:(SC + 1) * D], ctxT[:, b, SM:S].broadcast_to([P, NQ]), w("wv1"),
                                 start=True, stop=True)

            def values_left(n):
                pe.wait_ge(v_ready.sem, v_ready.at(n))
                pe.wait_ge(vl_ready.sem, vl_ready.at(n))

            def last_weights(b):
                return pe.transpose(pM[0:NQ, (SC + 1) * D:(SC + 2) * D], pr[:, b % 2, :, SM], k("ident"))

            def scores(b, n):
                pe.wait_ge(k_ready.sem, k_ready.at(n))
                pe.wait_ge(qq_ready.sem, qq_ready.at(n))
                for c in range(NQ):
                    r = slice(c * T, (c + 1) * T)
                    pe.wait_ge(e_ready.sem, e_ready.at(n - 1, c + 1))
                    pe.matmul(pS[:, c, 0:S], qq[r, b % 2, :, :], ks[r, b % 2, :], start=True, stop=True).then_inc(s_done.sem, 1)

            def turn(b, n):
                pe.wait_ge(e_ready.sem, e_ready.at(n))
                for c in range(SC):
                    for j in range(NQ):
                        mm = pe.transpose(pT[:, c, j, :], pr[:, b % 2, j, c * P:(c + 1) * P], k("ident"))
                mm.then_inc(pT_done.sem, 1)

            def sums(b, n):
                pe.wait_ge(prl_ready.sem, prl_ready.at(n))
                for c, ready in enumerate((pT0_ready, pT1_ready)):
                    pe.wait_ge(ready.sem, ready.at(n))
                    for j in range(NQ):
                        pe.matmul(pO[j * T:(j + 1) * T, b, :, :], vs[:, b, c, j * T:(j + 1) * T], prT[:, c, j, :],
                                  start=(c == 0), stop=False, skip_group_check=True)
                pe.matmul(pO[:, b, :, :], vl[:, b, :], prl[:, :], start=False, stop=True,
                          skip_group_check=True).then_inc(o_done.sem, 1)

            def scales(g):
                pe.wait_ge(rm_ready.sem, rm_ready.at(g))
                for b in range(BG):
                    mm = pe.matmul(pM[:, b * T:(b + 1) * T], rm[:, b, :, :], k("qsel"), start=True, stop=True)
                mm.then_inc(rT_done.sem, 1)

            def project(g):
                pe.wait_ge(ob_ready.sem, ob_ready.at(g))
                pe.matmul(pM[:, P:2 * P], ob[:, :], w("wo1"), start=True, stop=True).then_inc(y_done.sem, 1)

            def body(g, first, last):
                for b in range(BG):
                    n = g * BG + b
                    scores(b, n)
                    values_left(n)
                    if b < BG - 1:
                        keys(g, b + 1, n + 1)
                    elif not last:
                        queries(g + 1)
                        pe.wait_ge(q_ready.sem, q_ready.at(g + 1))
                        keys(g + 1, 0, n + 1)
                    if not first or b > 0:
                        turn((b - 1) % BG, n - 1)
                    if b < BG - 1 or not last:
                        mm = values((b + 1) % BG, n + 1)
                    if not first or b > 0:
                        mm = last_weights((b - 1) % BG)
                    mm.then_inc(v_done.sem, 1)
                    if not first or b > 0:
                        if b == 1 and not first:
                            pe.wait_ge(om_ready.sem, om_ready.at(g - 1))
                        sums((b - 1) % BG, n - 1)
                    if b == 1 and not first:
                        values_left(n + 1)
                        scales(g - 1)
                        project(g - 1)
                        pe.wait_ge(yb_ready.sem, yb_ready.at(g - 1))
                    if b == 2 and not last:
                        values_left(n + 1)
                        norm_T(g + 1)
                        pe.wait_ge(hT_ready.sem, hT_ready.at(g + 1))

            norm_T(0)
            queries(0)
            pe.wait_ge(q_ready.sem, q_ready.at(0))
            keys(0, 0, 0)
            values(0, 0).then_inc(v_done.sem, 1)
            body(0, True, False)
            with pe.Fori(1, G - 1) as g:
                body(g, False, False)
            body(G - 1, False, True)
            turn(BG - 1, B - 1)
            last_weights(BG - 1).then_inc(v_done.sem, 1)
            sums(BG - 1, B - 1)
            scales(G - 1)
            project(G - 1)

        @block.scalar
        def _(act):
            act.sem_inc(e_ready.sem, e_ready.credit)

            def keys(b, n):
                act.wait_ge(k_done.sem, k_done.at(n))
                act.activation(ks[:, b % 2, :], pM[:, 0:S], ACT.Identity, bias=v("bk1")).then_inc(k_ready.sem, 1)

            def exps(b, n, quads):
                for c in quads:
                    act.wait_ge(max_ready.sem, max_ready.at(n, c + 1))
                    act.activation(pr[:, b % 2, c, :], pS[:, c, 0:S], ACT.Exp, bias=nm[:, c:c + 1],
                                   accum_out=den[:, b % 2, c:c + 1]).then_inc(e_ready.sem, 1)

            def turned(n):
                act.wait_ge(pT_done.sem, pT_done.at(n))
                act.activation(prT[:, 0, :, :], pT[:, 0, :, :], ACT.Copy).then_inc(pT0_ready.sem, 1)

            def norm_T(g):
                act.wait_ge(hT_done.sem, hT_done.at(g))
                act.activation(hT[:, :], pM[:, 0:P], ACT.Copy).then_inc(hT_ready.sem, 1)

            def body(g, first, last):
                for b in range(BG):
                    n = g * BG + b
                    if b < BG - 1 or not last:
                        keys((b + 1) % BG, n + 1)
                    exps(b, n, (0, 1))
                    if not first or b > 0:
                        turned(n - 1)
                    exps(b, n, (2, 3))
                    if b == 2 and not last:
                        norm_T(g + 1)

            norm_T(0)
            keys(0, 0)
            body(0, True, False)
            with act.Fori(1, G - 1) as g:
                body(g, False, False)
            body(G - 1, False, True)
            turned(B - 1)

        @block.gpsimd
        def _(pool):
            def spread(b, n, g):
                pool.wait_ge(q_ready.sem, q_ready.at(g))
                if not (isinstance(n, int) and n < 2):
                    pool.wait_ge(s_done.sem, s_done.at(n - 2))
                pool.tensor_tensor(qq[:, b % 2, :, :], q[:, b * T:(b + 1) * T].unsqueeze(1).broadcast_to([P, HQ, T]),
                                   k("quad").unsqueeze(2).broadcast_to([P, HQ, T]), ALU.mult).then_inc(qq_ready.sem, 1)

            def scales(g):
                pool.wait_ge(rinv_ready.sem, rinv_ready.at(g * BG + BG - 1))
                pool.tensor_tensor(rm[:, :, :, :], rinv[:, :, :].unsqueeze(3).broadcast_to([P, BG, NQ, HQ * HD]),
                                   k("vmask").rearrange("p (c f) -> p c f", c=NQ).unsqueeze(1).broadcast_to([P, BG, NQ, HQ * HD]),
                                   ALU.mult).then_inc(rm_ready.sem, 1)

            def body(g, first, last):
                for b in range(BG):
                    n = g * BG + b
                    if b == 0 and not first:
                        scales(g - 1)
                    if b == 1 and not last:
                        n4.gpsimd(pool, g + 1)
                    if b < BG - 1:
                        spread(b + 1, n + 1, g)
                    elif not last:
                        spread(0, n + 1, g + 1)

            n4.gpsimd(pool, 0)
            spread(0, 0, 0)
            body(0, True, False)
            with pool.Fori(1, G - 1) as g:
                body(g, False, False)
            body(G - 1, False, True)
            scales(G - 1)

        @block.vector
        def _(dve):
            def x_of(g):
                return X[:, bass.ds(g, 1), :].rearrange("p g d -> p (g d)")

            def queries(g):
                dve.wait_ge(q_done.sem, q_done.at(g))
                if not (isinstance(g, int) and g == 0):
                    dve.wait_ge(qq_ready.sem, qq_ready.at(g * BG - 1))
                dve.tensor_scalar(q[:, :], pM[:, P:2 * P], v("bq1"), SCALE, ALU.add, ALU.mult).then_inc(q_ready.sem, 1)

            def maxima(n):
                for c in range(NQ):
                    dve.wait_ge(s_done.sem, s_done.at(n, c + 1))
                    dve.tensor_reduce(nm[:, c:c + 1], pS[:, c, 0:S], AX.X, ALU.max, negate=True).then_inc(max_ready.sem, 1)

            def values(b, n):
                dve.wait_ge(v_done.sem, v_done.at(n))
                dve.tensor_copy(vs[:, b, :, :], pM[:, 0:SM].rearrange("p (c d) -> p c d", c=SC)).then_inc(v_ready.sem, 1)
                dve.tensor_tensor(vl[:, b, :], pM[0:NQ, SC * D:(SC + 1) * D], k("row4")[0:NQ, :], ALU.mult).then_inc(vl_ready.sem, 1)

            def turned(n):
                dve.wait_ge(pT_done.sem, pT_done.at(n))
                dve.tensor_copy(prT[:, 1, :, :], pT[:, 1, :, :]).then_inc(pT1_ready.sem, 1)

            def last_weights(b, n, g_read):
                dve.wait_ge(v_done.sem, v_done.at(n + 2))
                dve.tensor_copy(prl[:, :], pM[0:NQ, (SC + 1) * D:(SC + 2) * D]).then_inc(prl_ready.sem, 1)
                if g_read is not None:
                    dve.wait_ge(rm_ready.sem, rm_ready.at(g_read))
                dve.reciprocal(rinv[:, b, :], den[:, b % 2, :]).then_inc(rinv_ready.sem, 1)

            def gather(g):
                dve.wait_ge(o_done.sem, o_done.at(g * BG + BG - 1))
                dve.tensor_tensor(om[:, :, :, :], pO[:, :, :, :],
                                  k("quad").unsqueeze(1).unsqueeze(3).broadcast_to([P, BG, HQ, T]), ALU.mult).then_inc(om_ready.sem, 1)
                dve.wait_ge(om_ready.sem, om_ready.at(g))
                dve.tensor_reduce(osum[:, :, :], om[:, :, :, :].rearrange("p b h t -> p b t h"), AX.X, ALU.add
                                  ).then_inc(osum_ready.sem, 1)

            def finish(g):
                dve.wait_ge(rT_done.sem, rT_done.at(g))
                dve.wait_ge(osum_ready.sem, osum_ready.at(g))
                dve.tensor_tensor(on[:, :], pM[:, 0:P], osum[:, :, :].rearrange("p b t -> p (b t)"), ALU.mult).then_inc(on_ready.sem, 1)
                dve.wait_ge(on_ready.sem, on_ready.at(g))
                dve.tensor_scalar(ob[:, :], on[:, :], v("bv1"), None, ALU.add).then_inc(ob_ready.sem, 1)
                dve.wait_ge(y_done.sem, y_done.at(g))
                dve.tensor_tensor(yb[:, :], pM[:, P:2 * P], bo1[:, :], ALU.add).then_inc(yb_ready.sem, 1)
                dve.wait_ge(yb_ready.sem, yb_ready.at(g))
                dve.tensor_tensor(x_of(g), yb[:, :], x_of(g), ALU.add).then_inc(x_ready.sem, 1)

            def body(g, first, last):
                for b in range(BG):
                    n = g * BG + b
                    maxima(n)
                    if b == BG - 1 and not last:
                        queries(g + 1)
                    if not first or b > 0:
                        turned(n - 1)
                    if b < BG - 1 or not last:
                        values((b + 1) % BG, n + 1)
                    if not first or b > 0:
                        last_weights((b - 1) % BG, n - 1, g - 1 if (b == 1 and not first) else None)
                    if b == 0 and not first:
                        gather(g - 1)
                    if b == 1 and not first:
                        finish(g - 1)
                    if b == 1 and not last:
                        n4.vector_stats(dve, x_of(g + 1), g + 1)
                        n4.vector_scale(dve, x_of(g + 1), g + 1)

            n4.vector_stats(dve, x_of(0), 0)
            n4.vector_scale(dve, x_of(0), 0)
            queries(0)
            values(0, 0)
            body(0, True, False)
            with dve.Fori(1, G - 1) as g:
                body(g, False, False)
            body(G - 1, False, True)
            turned(B - 1)
            last_weights(BG - 1, B - 1, None)
            gather(G - 1)
            finish(G - 1)


def self_layer1(env):
    nc, io, X, HT_all, LG, w, v, k = (env[n] for n in ("nc", "io", "X", "HT_all", "LG", "w", "v", "k"))
    ctx = Phase(nc, "s")
    with ctx:
        def sb(name, shape, dt=F32):
            return ctx.enter_context(nc.sbuf_tensor("s_" + name, shape, dt))

        def ps(name, shape):
            return ctx.enter_context(nc.psum_tensor("s_" + name, shape, F32))

        def sig(name, per=1, credit=0):
            return Signal(ctx, nc, "s_" + name, per, credit)

        wqkv, wout, gate = sb("wqkv", [P, 3, RI]), sb("wout", [P, RP, D]), sb("gate", [P, E])
        gamma1, sq, ss, root, rms, xn = (sb("gamma1", [P, 1]), sb("sq", [P, D]), sb("ss", [P, 1]), sb("root", [P, 1]), sb("rms", [P, 1]),
                                         sb("xn", [P, D]))
        irms = sb("irms", [P, 1])
        hT = sb("hT", [P, P])
        qT = sb("qT", [P, RP, P])
        kp = sb("kp", [P, RP, BG, 2, T])
        vs = sb("vs", [P, RI])
        smax, sd, se, ssum, sinv, sn = (sb("smax", [P, H]), sb("sd", [P, H, T]), sb("se", [P, H, T]), sb("ssum", [P, H]), sb("sinv", [P, H]),
                                        sb("sn", [P, H, T]))
        pt = sb("pt", [P, H, P])
        oT, h5T = sb("oT", [P, RP, P]), sb("h5T", [P, P])
        pA = ps("pA", [P, RP, P])
        pK = ps("pK", [P, RP, P])
        pV = ps("pV", [P, RI])
        pS = ps("pS", [P, H, T])
        pM = ps("pM", [P, 4, P])
        n5 = Norm(ctx, nc, "s_n5", env)
        n6 = Norm(ctx, nc, "s_n6", env)
        w_loaded, gamma_ready, zeroed = sig("w_loaded", 48), sig("gamma_ready"), sig("zeroed", 2)
        ss_ready, root_ready, rms_ready, irms_ready, xn_ready = (sig("ss_ready"), sig("root_ready"), sig("rms_ready"), sig("irms_ready"),
                                                                sig("xn_ready"))
        hT_done, hT_ready = sig("hT_done"), sig("hT_ready")
        q_done, q_ready = sig("q_done"), sig("q_ready")
        k_done, k0_ready, k1_ready = sig("k_done"), sig("k0_ready"), sig("k1_ready")
        v_done, v_ready = sig("v_done"), sig("v_ready")
        s_done, max_ready, sd_ready, se_ready = sig("s_done"), sig("max_ready"), sig("sd_ready"), sig("se_ready")
        sum_ready, sinv_ready, sn_ready, pt_ready = sig("sum_ready"), sig("sinv_ready"), sig("sn_ready"), sig("pt_ready")
        o_done, o_ready, y_done, x_ready = sig("o_done"), sig("o_ready"), sig("y_done"), sig("x_ready")
        h5T_done, h5T_ready, h5T_kept = sig("h5T_done"), sig("h5T_ready"), sig("h5T_kept", credit=1)
        xh_ready, lg_done, lg_ready = sig("xh_ready"), sig("lg_done"), sig("lg_ready")
        SCALE = float(RH) ** -0.5
        HB = RP // 2
        block = ctx.enter_context(nc.Block())

        def is_first(g):
            return isinstance(g, int) and g == 0

        @block.sync
        def _(sp):
            sp.dma_start(wqkv[:, :, :].rearrange("p a n -> p (a n)"), io["wqkv"]).then_inc(w_loaded.sem, 16)
            sp.dma_start(wout[:, :, :], io["wout"]).then_inc(w_loaded.sem, 16)
            sp.dma_start(gate[:, :], io["gate"]).then_inc(w_loaded.sem, 16)

        @block.tensor
        def _(pe):
            pe.wait_ge(w_loaded.sem, 3 * 16)

            def norm_T(g):
                pe.wait_ge(xn_ready.sem, xn_ready.at(g))
                pe.transpose(pM[:, 0, :], xn[:, :], k("ident")).then_inc(hT_done.sem, 1)

            def queries_keys(g):
                pe.wait_ge(hT_ready.sem, hT_ready.at(g))
                for j in range(RP):
                    mm = pe.matmul(pA[:, j, :], wqkv[:, 0, j * P:(j + 1) * P], hT[:, :], start=True, stop=True)
                mm.then_inc(q_done.sem, 1)
                for j in range(RP):
                    mm = pe.matmul(pK[:, j, :], wqkv[:, 1, j * P:(j + 1) * P], hT[:, :], start=True, stop=True)
                mm.then_inc(k_done.sem, 1)

            def values(g):
                for c in range(2):
                    mm = pe.matmul(pV[:, c * 512:(c + 1) * 512], hT[:, :], wqkv[:, 2, c * 512:(c + 1) * 512], start=True, stop=True)
                mm.then_inc(v_done.sem, 1)

            def scores(g):
                pe.wait_ge(q_ready.sem, q_ready.at(g))
                pe.wait_ge(k0_ready.sem, k0_ready.at(g))
                pe.wait_ge(k1_ready.sem, k1_ready.at(g))
                for j in range(RP):
                    for b in range(BG):
                        mm = pe.matmul(pS[b * T:(b + 1) * T, 2 * j:2 * j + 2, :], qT[:, j, b * T:(b + 1) * T], kp[:, j, b, :, :],
                                       start=True, stop=True)
                mm.then_inc(s_done.sem, 1)

            def sums(g):
                pe.wait_ge(pt_ready.sem, pt_ready.at(g))
                pe.wait_ge(v_ready.sem, v_ready.at(g))
                for h in range(H):
                    r = slice(RH * (h % 2), RH * (h % 2) + RH)
                    mm = pe.matmul(pA[r, h // 2, :], vs[:, h * RH:(h + 1) * RH], pt[:, h, :], start=True, stop=True)
                mm.then_inc(o_done.sem, 1)

            def project(g):
                pe.wait_ge(o_ready.sem, o_ready.at(g))
                for j in range(RP):
                    mm = pe.matmul(pM[:, 1, :], oT[:, j, :], wout[:, j, :], start=(j == 0), stop=(j == RP - 1))
                mm.then_inc(y_done.sem, 1)

            def logits(g):
                pe.wait_ge(n6.h_ready.sem, n6.h_ready.at(g))
                pe.transpose(pM[:, 2, :], n6.h[:, :], k("ident")).then_inc(h5T_done.sem, 1)
                pe.wait_ge(h5T_ready.sem, h5T_ready.at(g))
                pe.matmul(pM[:, 3, 0:E], h5T[:, :], gate[:, :], start=True, stop=True).then_inc(lg_done.sem, 1)

            def slot(g, last):
                scores(g)
                if not last:
                    norm_T(g + 1)
                    queries_keys(g + 1)
                    values(g + 1)
                    pe.wait_ge(q_ready.sem, q_ready.at(g + 1))
                sums(g)
                project(g)
                logits(g)
                pe.wait_ge(lg_ready.sem, lg_ready.at(g))

            norm_T(0)
            queries_keys(0)
            values(0)
            with pe.Fori(0, G - 1) as g:
                slot(g, False)
            slot(G - 1, True)

        @block.scalar
        def _(act):
            act.wait_ge(gamma_ready.sem, 1)
            act.wait_ge(zeroed.sem, 2)

            def norm_T(g):
                act.wait_ge(hT_done.sem, hT_done.at(g))
                act.activation(hT[:, :], pM[:, 0, :], ACT.Copy, scale=gamma1[:, :]).then_inc(hT_ready.sem, 1)

            def queries(g):
                act.wait_ge(q_done.sem, q_done.at(g))
                act.activation(qT[:, :, :], pA[:, :, :], ACT.Copy, scale=SCALE).then_inc(q_ready.sem, 1)

            def keys(g):
                act.wait_ge(k_done.sem, k_done.at(g))
                act.wait_ge(k0_ready.sem, k0_ready.at(g))
                act.activation(kp[RH:P, :, :, 1, :].rearrange("p j b s -> p (j b) s"),
                               pK[RH:P, :, :].rearrange("p j (b s) -> p (j b) s", b=BG), ACT.Copy).then_inc(k1_ready.sem, 1)

            def values(g):
                act.wait_ge(v_done.sem, v_done.at(g))
                if not is_first(g):
                    act.wait_ge(o_done.sem, o_done.at(g - 1))
                act.activation(vs[:, :], pV[:, :], ACT.Copy).then_inc(v_ready.sem, 1)

            def slot(g, last):
                if not last:
                    norm_T(g + 1)
                act.wait_ge(sd_ready.sem, sd_ready.at(g))
                act.activation(se[:, :, :], sd[:, :, :], ACT.Exp).then_inc(se_ready.sem, 1)
                if not last:
                    queries(g + 1)
                    keys(g + 1)
                act.wait_ge(o_done.sem, o_done.at(g))
                act.activation(oT[:, :, :], pA[:, :, :], ACT.Copy).then_inc(o_ready.sem, 1)
                if not last:
                    values(g + 1)
                act.wait_ge(h5T_done.sem, h5T_done.at(g))
                act.wait_ge(h5T_kept.sem, h5T_kept.at(g, 0))
                act.activation(h5T[:, :], pM[:, 2, :], ACT.Copy).then_inc(h5T_ready.sem, 1)

            norm_T(0)
            queries(0)
            keys(0)
            values(0)
            with act.Fori(0, G - 1) as g:
                slot(g, False)
            slot(G - 1, True)

        @block.gpsimd
        def _(pool):
            pool.memset(kp[:, :, :, :, :], 0.0).then_inc(zeroed.sem, 1)
            pool.memset(pt[:, :, :], 0.0).then_inc(zeroed.sem, 1)
            pool.sem_inc(h5T_kept.sem, h5T_kept.credit)

            def rms_norm(g):
                n5.gpsimd(pool, g)
                pool.wait_ge(ss_ready.sem, ss_ready.at(g))
                pool.tensor_tensor(root[:, :], ss[:, :], k("root"), ALU.pow).then_inc(root_ready.sem, 1)

            rms_norm(0)

            def slot(g, last):
                if not last:
                    rms_norm(g + 1)
                n6.gpsimd(pool, g)
                pool.wait_ge(h5T_ready.sem, h5T_ready.at(g))
                pool.tensor_copy(HT_all[:, bass.ds(g, 1), :].rearrange("p g t -> p (g t)"), h5T[:, :]).then_inc(h5T_kept.sem, 1)

            with pool.Fori(0, G - 1) as g:
                slot(g, False)
            slot(G - 1, True)

        @block.vector
        def _(dve):
            dve.tensor_scalar(gamma1[:, :], v("gamma"), 1.0, None, ALU.add).then_inc(gamma_ready.sem, 1)
            dve.wait_ge(zeroed.sem, 2)

            def x_of(g):
                return X[:, bass.ds(g, 1), :].rearrange("p g d -> p (g d)")

            def rms_norm(g):
                n5.vector_stats(dve, x_of(g), g)
                n5.vector_scale(dve, x_of(g), g)
                dve.wait_ge(n5.h_ready.sem, n5.h_ready.at(g))
                dve.scalar_tensor_tensor(sq[:, :], n5.h[:, :], 1.0, n5.h[:, :], ALU.mult, ALU.mult, accum_out=ss[:, :]
                                         ).then_inc(ss_ready.sem, 1)
                dve.wait_ge(root_ready.sem, root_ready.at(g))
                dve.tensor_scalar(rms[:, :], root[:, :], 1e-12, None, ALU.max).then_inc(rms_ready.sem, 1)
                dve.wait_ge(rms_ready.sem, rms_ready.at(g))
                dve.reciprocal(irms[:, :], rms[:, :]).then_inc(irms_ready.sem, 1)
                dve.wait_ge(irms_ready.sem, irms_ready.at(g))
                dve.tensor_scalar(xn[:, :], n5.h[:, :], irms[:, :], float(D) ** 0.5, ALU.mult, ALU.mult).then_inc(xn_ready.sem, 1)

            def keys(g):
                dve.wait_ge(k_done.sem, k_done.at(g))
                dve.tensor_copy(kp[0:RH, :, :, 0, :].rearrange("p j b s -> p (j b) s"),
                                pK[0:RH, :, :].rearrange("p j (b s) -> p (j b) s", b=BG)).then_inc(k0_ready.sem, 1)

            def slot(g, last):
                dve.wait_ge(s_done.sem, s_done.at(g))
                dve.tensor_reduce(smax[:, :], pS[:, :, :], AX.X, ALU.max).then_inc(max_ready.sem, 1)
                dve.wait_ge(max_ready.sem, max_ready.at(g))
                dve.tensor_tensor(sd[:, :, :], pS[:, :, :], smax[:, :].unsqueeze(2).broadcast_to([P, H, T]), ALU.subtract
                                  ).then_inc(sd_ready.sem, 1)
                dve.wait_ge(se_ready.sem, se_ready.at(g))
                dve.tensor_reduce(ssum[:, :], se[:, :, :], AX.X, ALU.add).then_inc(sum_ready.sem, 1)
                dve.wait_ge(sum_ready.sem, sum_ready.at(g))
                dve.reciprocal(sinv[:, :], ssum[:, :]).then_inc(sinv_ready.sem, 1)
                dve.wait_ge(sinv_ready.sem, sinv_ready.at(g))
                dve.tensor_tensor(sn[:, :, :], se[:, :, :], sinv[:, :].unsqueeze(2).broadcast_to([P, H, T]), ALU.mult
                                  ).then_inc(sn_ready.sem, 1)
                dve.wait_ge(sn_ready.sem, sn_ready.at(g))
                for b in range(BG):
                    r = slice(b * T, (b + 1) * T)
                    ins = dve.transpose(pt[r, :, b * T:(b + 1) * T], sn[r, :, :])
                ins.then_inc(pt_ready.sem, 1)
                if not last:
                    keys(g + 1)
                dve.wait_ge(y_done.sem, y_done.at(g))
                dve.tensor_tensor(x_of(g), pM[:, 1, :], x_of(g), ALU.add).then_inc(x_ready.sem, 1)
                dve.wait_ge(x_ready.sem, x_ready.at(g))
                carry(dve, ctx)
                n6.vector_stats(dve, x_of(g), g)
                n6.vector_scale(dve, x_of(g), g)
                dve.wait_ge(n6.h_ready.sem, n6.h_ready.at(g))
                dve.tensor_tensor(x_of(g), x_of(g), n6.h[:, :], ALU.add).then_inc(xh_ready.sem, 1)
                dve.wait_ge(lg_done.sem, lg_done.at(g))
                dve.tensor_copy(LG[:, bass.ds(g, 1), :].rearrange("p g e -> p (g e)"), pM[:, 3, 0:E]).then_inc(lg_ready.sem, 1)

            rms_norm(0)
            keys(0)
            rms_norm(1)
            with dve.Fori(0, G - 2) as g:
                slot(g, False)
                rms_norm(g + 2)
            slot(G - 2, False)
            slot(G - 1, True)


def kernel(**inputs):
    import concourse.bacc as _bacc
    from concourse.bass_utils import run_bass_kernel_spmd as _run

    a = {n: np.asarray(x) for n, x in inputs.items()}
    c = np.ascontiguousarray
    ctx = a["ctx_1024"]
    pair = np.arange(D).reshape(-1, 2)[:, ::-1].ravel()
    t = lambda m: m.T
    squares = {"wq0": t(a["L0_xattn_Wq"]), "wk0": a["L0_xattn_Wk"], "wv0": t(a["L0_xattn_Wv"]), "wo0": t(a["L0_xattn_Wo"]),
               "aq": t(a["L0_attn_W_Q"]), "aqr": t(a["L0_attn_W_Q"][pair]), "ak": t(a["L0_attn_W_K"]), "akr": t(a["L0_attn_W_K"][pair]),
               "av": t(a["L0_attn_W_V"]), "ao": t(a["L0_attn_W_O"]),
               "wq1": t(a["L1_xattn_Wq"]), "wk1": t(a["L1_xattn_Wk"]), "wv1": t(a["L1_xattn_Wv"]), "wo1": t(a["L1_xattn_Wo"])}
    vectors = [a["L0_xattn_bq"], a["L0_xattn_bk"], a["L0_xattn_bv"], a["L1_xattn_bq"], a["L1_xattn_bk"], a["L1_xattn_bv"], a["L1_attn_gamma"]]
    vectors += list(a["L0_ffn_b1"].reshape(-1, P)) + list(a["L1_ffn_b1"].reshape(-1, P))
    arrays = {
        "x": a["x"],
        "ctxR": ctx[:, :SM].reshape(G, BG, SC, P, D).transpose(0, 3, 2, 1, 4).reshape(G, P, SC * BG * D),
        "ctxT": ctx.reshape(G, BG, S, D).transpose(0, 3, 1, 2),
        "ctxL": ctx[:, SM],
        "wsq": np.stack([squares[n] for n in SQ], 1),
        "vec": np.stack(vectors, 1),
        "cst": constants(),
        "bo0": np.broadcast_to(a["L0_xattn_bo"], (P, D)),
        "bo1": np.broadcast_to(a["L1_xattn_bo"], (P, D)),
        "router": t(a["L0_ffn_router_w"]),
        "gate": a["L1_ffn_gate_W"],
        "f0_w1": a["L0_ffn_W1"].transpose(1, 0, 2),
        "f0_w2": a["L0_ffn_W2"].reshape(E, F0 // P, P, D).transpose(2, 0, 1, 3),
        "f0_b2": a["L0_ffn_b2"],
        "f1_w1": a["L1_ffn_W1"].transpose(1, 0, 2),
        "f1_w2": a["L1_ffn_W2"].reshape(E, F1 // P, P, D).transpose(2, 0, 1, 3),
        "f1_b2": a["L1_ffn_b2"],
        "wqkv": a["L1_attn_w_qkv"],
        "wout": a["L1_attn_w_out"].reshape(RP, P, D).transpose(1, 0, 2),
    }
    nc = _bacc.Bacc("TRN2", target_bir_lowering=False, num_devices=1)
    arrays = {f"in_{n}": c(x) for n, x in arrays.items()}
    io = {n[3:]: nc.dram_tensor(n, x.shape, mybir.dt.from_np(x.dtype), kind="ExternalInput").ap() for n, x in arrays.items()}
    io["out"] = nc.dram_tensor("out_dram", (B, T, D), F32, kind="ExternalOutput").ap()
    build_program(nc, io)
    r = _run(nc, [arrays], core_ids=[0])
    return r.results[0]["out_dram"]


def constants():
    p = np.arange(P)
    inv = 1.0 / np.float32(10000.0) ** (np.arange(0, HD, 2, dtype=np.float32) / HD)
    f = np.outer(inv, np.arange(T, dtype=np.float32)).astype(np.float32)
    angle = f[(p % HD) // 2]
    sign = np.where(p % 2 == 0, -1.0, 1.0)[:, None]
    parts = {
        "ident": np.eye(P),
        "rope": np.concatenate([np.cos(angle), sign * np.sin(angle)], 1),
        "quad": (p[:, None] // HD) % HQ == np.arange(HQ)[None],
        "vmask": (p[None] // HD) % HQ == p[:, None] // T,
        "batch": p[:, None] // T == np.arange(BG)[None],
        "qsel": p[:, None] % T == np.arange(T)[None],
        "row4": p[None] // T == p[:, None],
        "before": p[:, None] < p[None],
        "ones": np.ones((P, P)),
        "rank": np.broadcast_to(E - np.arange(E), (P, E)),
        "half": np.full((P, 1), -0.5),
        "root": np.full((P, 1), 0.5),
        "eps": np.full((P, 1), EPS),
    }
    return np.concatenate([np.asarray(parts[n], np.float32) for n in CONST], 1)
```

```python
from contextlib import ExitStack

import numpy as np

import concourse.bass as bass
from concourse import mybir

F32 = mybir.dt.float32
I32 = mybir.dt.int32
ALU = mybir.AluOpType
ACT = mybir.ActivationFunctionType
AX = mybir.AxisListType

B, T, D, S = 128, 32, 128, 257
P = 128
BG = P // T
G = B // BG
SC = S // P
SM = SC * P
TOP = 32
H = 16
HD = D // H
HQ = 4
NQ = H // HQ
RH = 64
RI = H * RH
RP = RI // P
E = 8
F0, F1 = 512, 256
CAP = 640
TG = 4
NB = G // TG
EPS = 1e-5
NEG = -3.0e38
FIRST_PROB = 0x3E000000
PROB_BITS = 25

SQ = ["wq0", "wk0", "wv0", "wo0", "aq", "aqr", "ak", "akr", "av", "ao", "wq1", "wk1", "wv1", "wo1"]
VEC = ["bq0", "bk0", "bv0", "bq1", "bk1", "bv1", "gamma"]
NVEC = len(VEC)
VB1_0 = NVEC
VB1_1 = VB1_0 + E * F0 // P
NV = VB1_1 + E * F1 // P
CONST = {"ident": 128, "rope": 64, "quad": 4, "vmask": 128, "batch": 4, "qsel": 32, "row4": 128,
         "before": 128, "ones": 128, "rank": 8, "half": 1, "root": 1, "eps": 1}
COFF = {}
_o = 0
for _n, _w in CONST.items():
    COFF[_n] = _o
    _o += _w
NC = _o


class Phase(ExitStack):

    def __init__(self, nc, name):
        super().__init__()
        self.nc, self.semaphores = nc, []
        self.passed = self.semaphore(f"{name}_passed")
        self.callback(self.retire)

    def semaphore(self, name):
        self.semaphores.append(self.nc.alloc_semaphore(name))
        return self.semaphores[-1]

    def retire(self):
        self.nc.clear_and_free_semaphores(self.semaphores)
        self.nc.all_engine_barrier()


class Signal:

    def __init__(self, ctx, nc, name, per=1, credit=0):
        self.sem, self.per, self.credit = ctx.semaphore(name), per, credit

    def at(self, r, j=None):
        return r * self.per + (self.per if j is None else j) + self.credit


def carry(eng, phase):
    eng.sem_inc(phase.passed, 1)


def build_program(nc, io):
    ctx = ExitStack()
    with ctx:
        def sb(name, shape, dt=F32, c=ctx):
            return c.enter_context(nc.sbuf_tensor(name, shape, dt))

        X = sb("X", [P, G, D])
        HT_all = sb("HT_all", [P, G, P])
        LG = sb("LG", [P, G, E])
        MASK = sb("MASK", [P, G, E])
        wsq = sb("wsq", [P, len(SQ), P])
        vec = sb("vec", [P, NV])
        cst = sb("cst", [P, NC])
        bo0 = sb("bo0", [P, D])
        bo1 = sb("bo1", [P, D])
        loaded = ctx.enter_context(nc.semaphore("loaded"))

        def w(name):
            return wsq[:, SQ.index(name), :]

        def v(name):
            i = VEC.index(name)
            return vec[:, i:i + 1]

        def k(name):
            return cst[:, COFF[name]:COFF[name] + CONST[name]]

        env = dict(nc=nc, io=io, X=X, HT_all=HT_all, LG=LG, MASK=MASK, w=w, v=v, k=k, vec=vec, bo0=bo0, bo1=bo1)

        with nc.Block() as block:
            @block.sync
            def _(sp):
                for q in range(4):
                    n = G // 4
                    sp.dma_start(X[:, n * q:n * q + n, :],
                                 io["x"].rearrange("(g bb) t d -> (bb t) g d", bb=BG)[:, n * q:n * q + n, :]
                                 ).then_inc(loaded, 16)
                sp.dma_start(wsq[:, :, :], io["wsq"]).then_inc(loaded, 16)
                sp.dma_start(vec[:, :], io["vec"]).then_inc(loaded, 16)
                sp.dma_start(cst[:, :], io["cst"]).then_inc(loaded, 16)
                sp.dma_start(bo0[:, :], io["bo0"]).then_inc(loaded, 16)
                sp.dma_start(bo1[:, :], io["bo1"]).then_inc(loaded, 16)
                sp.wait_ge(loaded, 9 * 16)

        attend_layer0(env)
        route_layer0(env)
        experts(env, "f0", io["f0_w1"], io["f0_w2"], io["f0_b2"], F0 // P, VB1_0, None)
        cross_layer1(env)
        self_layer1(env)
        gate_layer1(env)
        experts(env, "f1", io["f1_w1"], io["f1_w2"], io["f1_b2"], F1 // P, VB1_1, io["out"])


class Norm:

    def __init__(self, ctx, nc, name, env):
        self.env, self.ctx = env, ctx
        f = lambda n, s: ctx.enter_context(nc.sbuf_tensor(f"{name}_{n}", s, F32))
        self.stats, self.mv, self.ve, self.rstd = f("stats", [P, 6]), f("mv", [P, 2]), f("ve", [P, 1]), f("rstd", [P, 1])
        self.h = f("h", [P, D])
        self.stats_ready = Signal(ctx, nc, f"{name}_stats_ready")
        self.mv_ready = Signal(ctx, nc, f"{name}_mv_ready")
        self.ve_ready = Signal(ctx, nc, f"{name}_ve_ready")
        self.rstd_ready = Signal(ctx, nc, f"{name}_rstd_ready")
        self.h_ready = Signal(ctx, nc, f"{name}_h_ready")

    def vector_stats(self, dve, x, r):
        dve.bn_stats(self.stats[:, :], x).then_inc(self.stats_ready.sem, 1)
        dve.wait_ge(self.stats_ready.sem, self.stats_ready.at(r))
        carry(dve, self.ctx)
        dve.bn_aggr(self.mv[:, :], self.stats[:, :]).then_inc(self.mv_ready.sem, 1)

    def gpsimd(self, pool, r):
        pool.wait_ge(self.mv_ready.sem, self.mv_ready.at(r))
        pool.tensor_tensor(self.ve[:, :], self.mv[:, 1:2], self.env["k"]("eps"), ALU.add).then_inc(self.ve_ready.sem, 1)
        pool.wait_ge(self.ve_ready.sem, self.ve_ready.at(r))
        pool.tensor_tensor(self.rstd[:, :], self.ve[:, :], self.env["k"]("half"), ALU.pow).then_inc(self.rstd_ready.sem, 1)

    def vector_scale(self, dve, x, r):
        dve.wait_ge(self.rstd_ready.sem, self.rstd_ready.at(r))
        dve.tensor_scalar(self.h[:, :], x, self.mv[:, 0:1], self.rstd[:, :], ALU.subtract, ALU.mult
                          ).then_inc(self.h_ready.sem, 1)


def attend_layer0(env):
    nc, io, X, HT_all, LG, w, v, k, bo0 = (env[n] for n in ("nc", "io", "X", "HT_all", "LG", "w", "v", "k", "bo0"))
    ctx = Phase(nc, "a")
    with ctx:
        def sb(name, shape, dt=F32):
            return ctx.enter_context(nc.sbuf_tensor("a_" + name, shape, dt))

        def ps(name, shape):
            return ctx.enter_context(nc.psum_tensor("a_" + name, shape, F32))

        def sig(name, per=1, credit=0):
            return Signal(ctx, nc, "a_" + name, per, credit)

        ctxN = sb("ctxN", [P, 2, SC, BG, D])
        ctxT = sb("ctxT", [P, 2, BG, S])
        ctxL = sb("ctxL", [BG, 2, D])
        wr = sb("router", [P, E])
        hT, q, q2, qb = sb("hT", [P, P]), sb("q", [P, P]), sb("q2", [P, P]), sb("qb", [P, 1])
        sc, work, top = sb("sc", [P, S]), sb("work", [P, S]), sb("top", [P, TOP])
        nmax, ex, pr, rsum, rinv = sb("nmax", [P, 1]), sb("ex", [P, S]), sb("pr", [P, S]), sb("rsum", [P, 1]), sb("rinv", [P, 1])
        prL, prT, prLT = sb("prL", [P, BG]), sb("prT", [P, SC, P]), sb("prLT", [BG, P])
        cu, uT, vT, yb = sb("u", [P, D]), sb("uT", [P, P]), sb("vT", [P, P]), sb("yb", [P, D])
        hT2, rot, qk = sb("hT2", [P, P]), sb("rot", [P, 2, 8, T]), sb("qk", [P, 2, P])
        kquad = sb("kquad", [P, BG, HQ, T])
        smax, sd, se, ssum, sinv = sb("smax", [P, H]), sb("sd", [P, H, T]), sb("se", [P, H, T]), sb("ssum", [P, H]), sb("sinv", [P, H])
        seT, vq, o, oT = sb("seT", [P, NQ, P]), sb("vq", [P, BG, D]), sb("o", [P, D]), sb("oT", [P, P])
        h3T = sb("h3T", [P, P])

        pX = ps("pX", [P, 4, P])
        pS = pX[:, :, :].rearrange("p a t -> p (a t)")[:, 0:S]
        pU = ps("pU", [P, 4, P])
        pB = ps("pB", [P, P])
        pQ = ps("pQ", [P, 4, 512])
        pO = ps("pO", [P, 4, P])

        n1 = Norm(ctx, nc, "a_n1", env)
        n2 = Norm(ctx, nc, "a_n2", env)
        n3 = Norm(ctx, nc, "a_n3", env)
        router_loaded = sig("router_loaded", 16)
        ctxT_loaded = [sig(f"ctxT_loaded{p}", 16) for p in range(2)]
        ctxN_loaded = [sig(f"ctxN_loaded{p}", 32) for p in range(2)]
        hT_done, hT_ready = sig("hT_done"), sig("hT_ready")
        q_done, q_ready = sig("q_done"), sig("q_ready")
        q2_done, q2_ready, qb_ready = sig("q2_done"), sig("q2_ready"), sig("qb_ready")
        s_done, s_ready = sig("s_done", credit=2), sig("s_ready")
        topk = sig("topk", 8)
        nmax_ready, e_ready = sig("nmax_ready"), sig("e_ready")
        p_ready, rinv_ready, pL_ready = sig("p_ready"), sig("rinv_ready"), sig("pL_ready")
        pT_done, pT_ready = sig("pT_done"), sig("pT_ready", 2)
        u_done, u_ready = sig("u_done", credit=2), sig("u_ready")
        uT_done, uT_ready = sig("uT_done"), sig("uT_ready")
        v_done, v_ready = sig("v_done"), sig("v_ready")
        y_done, yb_ready, x1_ready = sig("y_done"), sig("yb_ready"), sig("x1_ready")
        h2T_done, h2T_ready = sig("h2T_done"), sig("h2T_ready")
        qk_done, rot_ready, qk_ready, kq_ready = sig("qk_done"), sig("rot_ready"), sig("qk_ready"), sig("kq_ready")
        ss_done, smax_ready, sd_ready, se_ready = sig("ss_done"), sig("smax_ready"), sig("sd_ready"), sig("se_ready")
        ssum_ready, sinv_ready = sig("ssum_ready"), sig("sinv_ready")
        seT_done, seT_ready = sig("seT_done"), sig("seT_ready")
        vq_done, vq_ready = sig("vq_done"), sig("vq_ready")
        o_done, o_ready, oT_done, oT_ready = sig("o_done"), sig("o_ready"), sig("oT_done"), sig("oT_ready")
        y2_done, x2_ready = sig("y2_done"), sig("x2_ready")
        h3T_done, h3T_ready, h3T_kept = sig("h3T_done"), sig("h3T_ready"), sig("h3T_kept", credit=1)
        lg_done, lg_ready = sig("lg_done"), sig("lg_ready")
        SCALE = float(D) ** -0.5
        SCALE2 = float(HD) ** -0.5
        ident = k("ident")

        def slots(eng, slot):
            slot(0, 0, 0, None, None, None)
            slot(1, 1, 0, 0, None, None)
            slot(2, 0, 1, 1, 0, None)
            with eng.Fori(0, (G - 4) // 2) as i:
                slot(i * 2 + 3, 1, i + 1, i * 2 + 2, i * 2 + 1, i * 2)
                slot(i * 2 + 4, 0, i + 2, i * 2 + 3, i * 2 + 2, i * 2 + 1)
            slot(G - 1, 1, G // 2 - 1, G - 2, G - 3, G - 4)
            slot(None, 0, None, G - 1, G - 2, G - 3)
            slot(None, 1, None, None, G - 1, G - 2)
            slot(None, 0, None, None, None, G - 1)

        def later(g):
            return g is not None and not (isinstance(g, int) and g == 0)

        block = ctx.enter_context(nc.Block())

        @block.sync
        def _(sp):
            sp.dma_start(wr[:, :], io["router"]).then_inc(router_loaded.sem, 16)

            def load(g, p):
                sp.wait_ge(s_done.sem, s_done.at(g, -1))
                sp.dma_start(ctxT[:, p, :, :].unsqueeze(1), io["ctxT"][bass.ds(g, 1), :, :, :].rearrange("g p b s -> p g b s")
                             ).then_inc(ctxT_loaded[p].sem, 16)
                sp.wait_ge(u_done.sem, u_done.at(g, -1))
                sp.dma_start(ctxN[:, p, :, :, :].rearrange("p c b d -> p (c b d)").unsqueeze(1),
                             io["ctxR"][bass.ds(g, 1), :, :].rearrange("g p n -> p g n")).then_inc(ctxN_loaded[p].sem, 16)
                sp.dma_start(ctxL[:, p, :], io["ctxL"][bass.ds(g * BG, BG), :]).then_inc(ctxN_loaded[p].sem, 16)

            with sp.Fori(0, G // 2) as i:
                load(i * 2, 0)
                load(i * 2 + 1, 1)

        @block.tensor
        def _(pe):
            pe.wait_ge(router_loaded.sem, 16)
            pe.sem_inc(s_done.sem, s_done.credit)
            pe.sem_inc(u_done.sem, u_done.credit)

            def turn(out, in_):
                return pe.matmul(out, in_, ident, start=True, stop=True)

            def slot(x, p, r, u, a, z):
                if x is not None:
                    if later(x):
                        pe.wait_ge(s_ready.sem, s_ready.at(x - 1))
                    pe.wait_ge(n1.h_ready.sem, n1.h_ready.at(x))
                    turn(pX[:, 0, :], n1.h[:, :]).then_inc(hT_done.sem, 1)
                if z is not None:
                    if later(z):
                        pe.wait_ge(lg_ready.sem, lg_ready.at(z - 1))
                    pe.wait_ge(se_ready.sem, se_ready.at(z))
                    for c in range(NQ):
                        mm = turn(pO[:, c, :], se[:, c * HQ:(c + 1) * HQ, :])
                    mm.then_inc(seT_done.sem, 1)
                if u is not None:
                    pe.wait_ge(pL_ready.sem, pL_ready.at(u))
                    for c in range(SC):
                        turn(pU[:, c, :], pr[:, c * P:(c + 1) * P])
                    turn(pU[0:BG, SC, :], prL[:, :]).then_inc(pT_done.sem, 1)
                if a is not None:
                    pe.wait_ge(n2.h_ready.sem, n2.h_ready.at(a))
                    turn(pB[:, :], n2.h[:, :]).then_inc(h2T_done.sem, 1)
                if x is not None:
                    pe.wait_ge(hT_ready.sem, hT_ready.at(x))
                    pe.matmul(pX[:, 1, :], w("wq0"), hT[:, :], start=True, stop=True).then_inc(q_done.sem, 1)
                if a is not None:
                    pe.wait_ge(h2T_ready.sem, h2T_ready.at(a))
                    for j, name in enumerate(("aq", "ak", "aqr", "akr")):
                        mm = pe.matmul(pQ[:, 0, j * P:(j + 1) * P], w(name), hT2[:, :], start=True, stop=True)
                    mm.then_inc(qk_done.sem, 1)
                    for b in range(BG):
                        for h in range(HQ):
                            mm = pe.matmul(pQ[h * T:(h + 1) * T, 1, b * D:(b + 1) * D], hT2[:, b * T:(b + 1) * T], w("av"),
                                           start=True, stop=True)
                    mm.then_inc(vq_done.sem, 1)
                if z is not None:
                    pe.wait_ge(seT_ready.sem, seT_ready.at(z))
                    for b in range(BG):
                        for c in range(NQ):
                            mm = pe.matmul(pO[b * T:(b + 1) * T, 0, c * T:(c + 1) * T], seT[:, c, b * T:(b + 1) * T],
                                           vq[:, b, c * T:(c + 1) * T], start=True, stop=True)
                    mm.then_inc(o_done.sem, 1)
                if x is not None:
                    pe.wait_ge(q_ready.sem, q_ready.at(x))
                    pe.matmul(pX[:, 2, :], w("wk0"), q[:, :], start=True, stop=True)
                    pe.matmul(pX[:, 3, 0:1], q[:, :], v("bk0"), start=True, stop=True).then_inc(q2_done.sem, 1)
                if u is not None:
                    pe.wait_ge(pT_ready.sem, pT_ready.at(u))
                    pe.wait_ge(ctxN_loaded[1 - p].sem, ctxN_loaded[1 - p].at(r if p else (r - 1 if r is not None else G // 2 - 1)))
                    for c in range(SC):
                        for b in range(BG):
                            pe.matmul(pU[b * T:(b + 1) * T, 3, :], prT[:, c, b * T:(b + 1) * T], ctxN[:, 1 - p, c, b, :],
                                      start=(c == 0), stop=False, skip_group_check=True)
                    pe.matmul(pU[:, 3, :], prLT[:, :], ctxL[:, 1 - p, :], start=False, stop=True,
                              skip_group_check=True).then_inc(u_done.sem, 1)
                if z is not None:
                    pe.wait_ge(o_ready.sem, o_ready.at(z))
                    turn(pO[:, 1, :], o[:, :]).then_inc(oT_done.sem, 1)
                if x is not None:
                    pe.wait_ge(q2_ready.sem, q2_ready.at(x))
                    pe.wait_ge(ctxT_loaded[p].sem, ctxT_loaded[p].at(r))
                    for b in range(BG):
                        mm = pe.matmul(pS[b * T:(b + 1) * T, :], q2[:, b * T:(b + 1) * T], ctxT[:, p, b, :],
                                       start=True, stop=True)
                    mm.then_inc(s_done.sem, 1)
                if u is not None:
                    pe.wait_ge(u_ready.sem, u_ready.at(u))
                    turn(pU[:, 0, :], cu[:, :]).then_inc(uT_done.sem, 1)
                if a is not None:
                    pe.wait_ge(kq_ready.sem, kq_ready.at(a))
                    pe.wait_ge(vq_ready.sem, vq_ready.at(a))
                    carry(pe, ctx)
                    for b in range(BG):
                        for c in range(NQ):
                            r_ = slice(c * T, (c + 1) * T)
                            mm = pe.matmul(pQ[b * T:(b + 1) * T, c, 0:P], qk[r_, 0, b * T:(b + 1) * T],
                                           kquad[r_, b, :, :], start=True, stop=True)
                    mm.then_inc(ss_done.sem, 1)
                if z is not None:
                    pe.wait_ge(oT_ready.sem, oT_ready.at(z))
                    pe.matmul(pO[:, 2, :], oT[:, :], w("ao"), start=True, stop=True).then_inc(y2_done.sem, 1)
                if u is not None:
                    pe.wait_ge(uT_ready.sem, uT_ready.at(u))
                    pe.matmul(pU[:, 1, :], w("wv0"), uT[:, :], start=True, stop=True).then_inc(v_done.sem, 1)
                    pe.wait_ge(v_ready.sem, v_ready.at(u))
                    pe.matmul(pU[:, 2, :], vT[:, :], w("wo0"), start=True, stop=True).then_inc(y_done.sem, 1)
                if z is not None:
                    pe.wait_ge(n3.h_ready.sem, n3.h_ready.at(z))
                    turn(pO[:, 3, :], n3.h[:, :]).then_inc(h3T_done.sem, 1)
                    pe.wait_ge(h3T_ready.sem, h3T_ready.at(z))
                    pe.matmul(pO[:, 0, 0:E], h3T[:, :], wr[:, :], start=True, stop=True).then_inc(lg_done.sem, 1)

            slots(pe, slot)

        @block.scalar
        def _(act):
            def slot(x, p, r, u, a, z):
                if x is not None:
                    act.wait_ge(hT_done.sem, hT_done.at(x))
                    act.activation(hT[:, :], pX[:, 0, :], ACT.Copy).then_inc(hT_ready.sem, 1)
                if z is not None:
                    act.wait_ge(seT_done.sem, seT_done.at(z))
                    act.activation(seT[:, :, :], pO[:, :, :], ACT.Copy).then_inc(seT_ready.sem, 1)
                if u is not None:
                    act.wait_ge(pT_done.sem, pT_done.at(u))
                    act.activation(prT[:, :, :], pU[:, 0:SC, :], ACT.Copy).then_inc(pT_ready.sem, 1)
                    act.activation(prLT[:, :], pU[0:BG, SC, :], ACT.Copy).then_inc(pT_ready.sem, 1)
                if a is not None:
                    act.wait_ge(h2T_done.sem, h2T_done.at(a))
                    act.activation(hT2[:, :], pB[:, :], ACT.Copy).then_inc(h2T_ready.sem, 1)
                if x is not None:
                    act.wait_ge(q_done.sem, q_done.at(x))
                    act.activation(q[:, :], pX[:, 1, :], ACT.Identity, bias=v("bq0")).then_inc(q_ready.sem, 1)
                    act.wait_ge(q2_done.sem, q2_done.at(x))
                    act.activation(qb[:, :], pX[:, 3, 0:1], ACT.Copy).then_inc(qb_ready.sem, 1)
                    act.activation(q2[:, :], pX[:, 2, :], ACT.Copy).then_inc(q2_ready.sem, 1)
                if u is not None:
                    act.wait_ge(rinv_ready.sem, rinv_ready.at(u))
                    act.wait_ge(u_done.sem, u_done.at(u))
                    act.activation(cu[:, :], pU[:, 3, :], ACT.Copy, scale=rinv[:, :]).then_inc(u_ready.sem, 1)
                if z is not None:
                    act.wait_ge(oT_done.sem, oT_done.at(z))
                    act.activation(oT[:, :], pO[:, 1, :], ACT.Copy).then_inc(oT_ready.sem, 1)
                if x is not None:
                    act.wait_ge(s_done.sem, s_done.at(x))
                    act.wait_ge(qb_ready.sem, qb_ready.at(x))
                    act.activation(sc[:, :], pS, ACT.Identity, bias=qb[:, :]).then_inc(s_ready.sem, 1)
                if u is not None:
                    act.wait_ge(uT_done.sem, uT_done.at(u))
                    act.activation(uT[:, :], pU[:, 0, :], ACT.Copy).then_inc(uT_ready.sem, 1)
                    act.wait_ge(v_done.sem, v_done.at(u))
                    act.activation(vT[:, :], pU[:, 1, :], ACT.Identity, bias=v("bv0")).then_inc(v_ready.sem, 1)
                if a is not None:
                    act.wait_ge(sd_ready.sem, sd_ready.at(a))
                    act.activation(se[:, :, :], sd[:, :, :], ACT.Exp, scale=SCALE2).then_inc(se_ready.sem, 1)
                if x is not None:
                    act.wait_ge(nmax_ready.sem, nmax_ready.at(x))
                    act.activation(ex[:, :], sc[:, :], ACT.Exp, bias=nmax[:, :], scale=SCALE).then_inc(e_ready.sem, 1)
                if z is not None:
                    act.wait_ge(h3T_done.sem, h3T_done.at(z))
                    act.wait_ge(h3T_kept.sem, h3T_kept.at(z, 0))
                    act.activation(h3T[:, :], pO[:, 3, :], ACT.Copy).then_inc(h3T_ready.sem, 1)

            slots(act, slot)

        @block.gpsimd
        def _(pool):
            pool.sem_inc(h3T_kept.sem, h3T_kept.credit)
            n1.gpsimd(pool, 0)

            def slot(x, p, r, u, a, z):
                if a is not None:
                    pool.wait_ge(qk_ready.sem, qk_ready.at(a))
                    pool.tensor_tensor(kquad[:, :, :, :],
                                       qk[:, 1, :].rearrange("p (b s) -> p b s", b=BG).unsqueeze(2).broadcast_to([P, BG, HQ, T]),
                                       k("quad").unsqueeze(1).unsqueeze(3).broadcast_to([P, BG, HQ, T]), ALU.mult
                                       ).then_inc(kq_ready.sem, 1)
                if z is not None:
                    n3.gpsimd(pool, z)
                if x is not None and not (isinstance(x, int) and x == G - 1):
                    n1.gpsimd(pool, x + 1)
                if u is not None:
                    n2.gpsimd(pool, u)
                if z is not None:
                    pool.wait_ge(h3T_ready.sem, h3T_ready.at(z))
                    pool.tensor_copy(HT_all[:, bass.ds(z, 1), :].rearrange("p g t -> p (g t)"), h3T[:, :]).then_inc(h3T_kept.sem, 1)

            slots(pool, slot)

        @block.vector
        def _(dve):
            def x_of(g):
                return X[:, bass.ds(g, 1), :].rearrange("p g d -> p (g d)")

            n1.vector_stats(dve, X[:, 0, :], 0)
            n1.vector_scale(dve, X[:, 0, :], 0)

            def slot(x, p, r, u, a, z):
                more = x is not None and not (isinstance(x, int) and x == G - 1)
                if u is not None:
                    dve.wait_ge(e_ready.sem, e_ready.at(u))
                    dve.scalar_tensor_tensor(pr[:, :], work[:, :], NEG, ex[:, :], ALU.is_equal, ALU.mult,
                                             accum_out=rsum[:, :]).then_inc(p_ready.sem, 1)
                    dve.wait_ge(p_ready.sem, p_ready.at(u))
                    dve.tensor_scalar(prL[:, :], k("batch"), pr[:, SM:S], None, ALU.mult).then_inc(pL_ready.sem, 1)
                    dve.reciprocal(rinv[:, :], rsum[:, :]).then_inc(rinv_ready.sem, 1)
                if z is not None:
                    dve.wait_ge(se_ready.sem, se_ready.at(z))
                    dve.tensor_reduce(ssum[:, :], se[:, :, :], AX.X, ALU.add).then_inc(ssum_ready.sem, 1)
                    dve.wait_ge(ssum_ready.sem, ssum_ready.at(z))
                    dve.reciprocal(sinv[:, :], ssum[:, :]).then_inc(sinv_ready.sem, 1)
                if a is not None:
                    dve.wait_ge(qk_done.sem, qk_done.at(a))
                    dve.tensor_tensor(rot[:, :, :, :], pQ[:, 0, :].rearrange("p (c n t) -> p c n t", c=2, t=T),
                                      k("rope").rearrange("p (c t) -> p c t", c=2).unsqueeze(2).broadcast_to([P, 2, 8, T]),
                                      ALU.mult).then_inc(rot_ready.sem, 1)
                    dve.wait_ge(rot_ready.sem, rot_ready.at(a))
                    dve.tensor_tensor(qk[:, :, :].rearrange("p a t -> p (a t)"), rot[:, 0, :, :].rearrange("p n t -> p (n t)"),
                                      rot[:, 1, :, :].rearrange("p n t -> p (n t)"), ALU.add).then_inc(qk_ready.sem, 1)
                if z is not None:
                    dve.wait_ge(sinv_ready.sem, sinv_ready.at(z))
                    dve.wait_ge(o_done.sem, o_done.at(z))
                    dve.tensor_tensor(o[:, :].rearrange("p (h d) -> p h d", h=H), pO[:, 0, :].rearrange("p (h d) -> p h d", h=H),
                                      sinv[:, :].unsqueeze(2).broadcast_to([P, H, HD]), ALU.mult).then_inc(o_ready.sem, 1)
                if a is not None:
                    dve.wait_ge(vq_done.sem, vq_done.at(a))
                    dve.tensor_tensor(vq[:, :, :], pQ[:, 1, :].rearrange("p (b d) -> p b d", b=BG),
                                      k("vmask").unsqueeze(1).broadcast_to([P, BG, D]), ALU.mult).then_inc(vq_ready.sem, 1)
                if z is not None:
                    dve.wait_ge(y2_done.sem, y2_done.at(z))
                    dve.tensor_tensor(x_of(z), pO[:, 2, :], x_of(z), ALU.add).then_inc(x2_ready.sem, 1)
                    dve.wait_ge(x2_ready.sem, x2_ready.at(z))
                    carry(dve, ctx)
                    n3.vector_stats(dve, x_of(z), z)
                if a is not None:
                    dve.wait_ge(ss_done.sem, ss_done.at(a))
                    s4 = pQ[:, :, 0:P].rearrange("p c (h s) -> p c h s", h=HQ)
                    dve.tensor_reduce(smax[:, :], s4, AX.X, ALU.max).then_inc(smax_ready.sem, 1)
                if z is not None:
                    n3.vector_scale(dve, x_of(z), z)
                if a is not None:
                    dve.wait_ge(smax_ready.sem, smax_ready.at(a))
                    dve.tensor_tensor(sd[:, :, :].rearrange("p (c h) s -> p c h s", c=NQ), s4,
                                      smax[:, :].rearrange("p (c h) -> p c h", c=NQ).unsqueeze(3).broadcast_to([P, NQ, HQ, T]),
                                      ALU.subtract).then_inc(sd_ready.sem, 1)
                if x is not None:
                    dve.wait_ge(s_ready.sem, s_ready.at(x))
                    carry(dve, ctx)
                    n = 0
                    for i in range(TOP // 8):
                        src = sc if i == 0 else work
                        dve.max(top[:, i * 8:i * 8 + 8], src[:, :]).then_inc(topk.sem, 1)
                        n += 1
                        dve.wait_ge(topk.sem, topk.at(x, n))
                        carry(dve, ctx)
                        if i == 0:
                            dve.tensor_scalar(nmax[:, :], top[:, 0:1], -SCALE, None, ALU.mult).then_inc(nmax_ready.sem, 1)
                        dve.match_replace(work[:, :], top[:, i * 8:i * 8 + 8], src[:, :], NEG).then_inc(topk.sem, 1)
                        n += 1
                        if i == 1 and more:
                            n1.vector_stats(dve, x_of(x + 1), x + 1)
                        if i == 3 and more:
                            n1.vector_scale(dve, x_of(x + 1), x + 1)
                        dve.wait_ge(topk.sem, topk.at(x, n))
                        carry(dve, ctx)
                if u is not None:
                    dve.wait_ge(y_done.sem, y_done.at(u))
                    dve.tensor_tensor(yb[:, :], pU[:, 2, :], bo0[:, :], ALU.add).then_inc(yb_ready.sem, 1)
                    dve.wait_ge(yb_ready.sem, yb_ready.at(u))
                    dve.tensor_tensor(x_of(u), yb[:, :], x_of(u), ALU.add).then_inc(x1_ready.sem, 1)
                    dve.wait_ge(x1_ready.sem, x1_ready.at(u))
                    carry(dve, ctx)
                    n2.vector_stats(dve, x_of(u), u)
                if z is not None:
                    dve.wait_ge(lg_done.sem, lg_done.at(z))
                    dve.tensor_copy(LG[:, bass.ds(z, 1), :].rearrange("p g e -> p (g e)"), pO[:, 0, 0:E]).then_inc(lg_ready.sem, 1)
                if u is not None:
                    n2.vector_scale(dve, x_of(u), u)

            slots(dve, slot)


def route_layer0(env):
    nc, LG, MASK, k = (env[n] for n in ("nc", "LG", "MASK", "k"))
    ctx = Phase(nc, "r")
    with ctx:
        def sb(name, shape, dt=F32):
            return ctx.enter_context(nc.sbuf_tensor("r_" + name, shape, dt))

        def sig(name, per=1, credit=0):
            return Signal(ctx, nc, "r_" + name, per, credit)

        lmax, d, e8, sm, prob = sb("lmax", [P, G]), sb("d", [P, G, E]), sb("e8", [P, G, E]), sb("sum", [P, G]), sb("prob", [P, G])
        eq, first, hot = sb("eq", [P, G, E]), sb("first", [P, G]), sb("hot", [P, G, E])
        pm, hit = sb("pm", [P, G, E]), sb("hit", [P, G, E])
        least, cand, bit, count, kept = (sb("least", [P, E], I32), sb("cand", [P, E], I32), sb("bit", [P, 1], I32),
                                         sb("count", [P, E]), sb("kept", [P, E]))
        over, same, need, scan, rank, fit = (sb("over", [P, G, E]), sb("same", [P, G, E]), sb("need", [P, E]),
                                             sb("scan", [P, E, G]), sb("rank", [P, G, E]), sb("fit", [P, G, E]))
        held = sb("held", [P, G])
        pC = ctx.enter_context(nc.psum_tensor("r_pC", [P, 512], F32))
        pB = ctx.enter_context(nc.psum_tensor("r_pB", [P, 512], F32))
        d_ready, e_ready = sig("d_ready"), sig("e_ready")
        step = sig("step", 1)
        found = sig("found", 7)
        count_ready, total_ready = sig("count_ready"), sig("total_ready")
        over_ready, over_total = sig("over_ready"), sig("over_total")
        same_ready, same_total = sig("same_ready"), sig("same_total")
        block = ctx.enter_context(nc.Block())

        def per_group(t):
            return t[:, :].unsqueeze(2).broadcast_to([P, G, E])

        def per_expert(t):
            return t.unsqueeze(1).broadcast_to([P, G, E])

        @block.scalar
        def _(act):
            act.wait_ge(d_ready.sem, 1)
            act.activation(e8[:, :, :], d[:, :, :], ACT.Exp).then_inc(e_ready.sem, 1)

        @block.tensor
        def _(pe):
            with pe.Fori(0, PROB_BITS) as n:
                pe.wait_ge(count_ready.sem, count_ready.at(n))
                pe.matmul(pC[:, 0:E], k("ones"), count[:, :], start=True, stop=True).then_inc(total_ready.sem, 1)
            pe.wait_ge(over_ready.sem, 1)
            pe.matmul(pC[:, 0:E], k("ones"), count[:, :], start=True, stop=True).then_inc(over_total.sem, 1)
            pe.wait_ge(same_ready.sem, 1)
            pe.matmul(pB[:, 0:G * E], k("ones"), same[:, :, :], start=True, stop=True)
            pe.matmul(pB[:, G * E:2 * G * E], k("before"), same[:, :, :], start=True, stop=True).then_inc(same_total.sem, 1)

        @block.vector
        def _(dve):
            done = [0]

            def then(ins):
                done[0] += 1
                ins.then_inc(step.sem, 1)
                dve.wait_ge(step.sem, done[0])

            then(dve.tensor_reduce(lmax[:, :], LG[:, :, :], AX.X, ALU.max))
            dve.tensor_tensor(d[:, :, :], LG[:, :, :], per_group(lmax), ALU.subtract).then_inc(d_ready.sem, 1)
            then(dve.tensor_tensor(eq[:, :, :], LG[:, :, :], per_group(lmax), ALU.is_equal))
            then(dve.tensor_tensor(eq[:, :, :], eq[:, :, :], per_expert(k("rank")), ALU.mult))
            then(dve.tensor_reduce(first[:, :], eq[:, :, :], AX.X, ALU.max))
            then(dve.tensor_tensor(hot[:, :, :], eq[:, :, :], per_group(first), ALU.is_equal))
            dve.wait_ge(e_ready.sem, 1)
            then(dve.tensor_reduce(sm[:, :], e8[:, :, :], AX.X, ALU.add))
            then(dve.reciprocal(prob[:, :], sm[:, :]))
            then(dve.tensor_tensor(pm[:, :, :], hot[:, :, :], per_group(prob), ALU.mult))
            then(dve.memset(least[:, :], FIRST_PROB))
            then(dve.memset(bit[:, :], 1 << (PROB_BITS - 1)))
            with dve.Fori(0, PROB_BITS) as n:
                at = [0]

                def then_bit(ins):
                    at[0] += 1
                    ins.then_inc(found.sem, 1)
                    dve.wait_ge(found.sem, found.at(n, at[0]))

                then_bit(dve.tensor_tensor(cand[:, :], least[:, :], bit[:, 0:1].broadcast_to([P, E]), ALU.bitwise_or))
                then_bit(dve.tensor_tensor(hit[:, :, :], pm[:, :, :], per_expert(cand[:, :].bitcast(F32)), ALU.is_ge))
                dve.tensor_reduce(count[:, :], hit[:, :, :].rearrange("p g e -> p e g"), AX.X, ALU.add).then_inc(count_ready.sem, 1)
                then_bit(dve.tensor_single_scalar(bit[:, :], bit[:, :], 1, ALU.logical_shift_right))
                dve.wait_ge(total_ready.sem, total_ready.at(n))
                then_bit(dve.tensor_scalar(kept[:, :], pC[:, 0:E], float(CAP), None, ALU.is_ge))
                then_bit(dve.tensor_tensor(kept[:, :], kept[:, :], cand[:, :].bitcast(F32), ALU.mult))
                then_bit(dve.tensor_tensor(least[:, :].bitcast(F32), least[:, :].bitcast(F32), kept[:, :], ALU.max))
                then_bit(dve.memset(kept[:, :], 0.0))
            then(dve.tensor_tensor(over[:, :, :], pm[:, :, :], per_expert(least[:, :].bitcast(F32)), ALU.is_gt))
            dve.tensor_reduce(count[:, :], over[:, :, :].rearrange("p g e -> p e g"), AX.X, ALU.add).then_inc(over_ready.sem, 1)
            dve.tensor_tensor(same[:, :, :], pm[:, :, :], per_expert(least[:, :].bitcast(F32)), ALU.is_equal).then_inc(same_ready.sem, 1)
            dve.wait_ge(over_total.sem, 1)
            then(dve.tensor_scalar(need[:, :], pC[:, 0:E], -1.0, float(CAP), ALU.mult, ALU.add))
            dve.wait_ge(same_total.sem, 1)
            totals = pB[:, 0:G * E].rearrange("p (g e) -> p g e", e=E)
            for e in range(E):
                last = dve.tensor_tensor_scan(scan[:, e, :], k("ones")[:, 0:G], totals[:, :, e], 0.0, ALU.mult, ALU.add)
                if e < E - 1:
                    last.then_inc(step.sem, 1)
                    done[0] += 1
            then(last)
            then(dve.tensor_tensor(rank[:, :, :], scan[:, :, :].rearrange("p e g -> p g e"), totals, ALU.subtract))
            then(dve.tensor_tensor(rank[:, :, :], rank[:, :, :], pB[:, G * E:2 * G * E].rearrange("p (g e) -> p g e", e=E), ALU.add))
            then(dve.tensor_tensor(fit[:, :, :], rank[:, :, :], per_expert(need[:, :]), ALU.is_lt))
            then(dve.tensor_tensor(fit[:, :, :], fit[:, :, :], same[:, :, :], ALU.mult))
            then(dve.tensor_tensor(MASK[:, :, :], over[:, :, :], fit[:, :, :], ALU.add))
            then(dve.tensor_reduce(held[:, :], MASK[:, :, 1:E], AX.X, ALU.add))
            then(dve.tensor_scalar(MASK[:, :, 0], held[:, :], -1.0, 1.0, ALU.mult, ALU.add))


def gate_layer1(env):
    nc, LG, MASK, k = (env[n] for n in ("nc", "LG", "MASK", "k"))
    ctx = Phase(nc, "t")
    with ctx:
        def sb(name, shape, dt=F32):
            return ctx.enter_context(nc.sbuf_tensor("t_" + name, shape, dt))

        def sig(name, per=1, credit=0):
            return Signal(ctx, nc, "t_" + name, per, credit)

        lmax, d, gates, sm, inv = sb("lmax", [P, G]), sb("d", [P, G, E]), sb("gates", [P, G, E]), sb("sum", [P, G]), sb("inv", [P, G])
        eq, first, hot, rest = sb("eq", [P, G, E]), sb("first", [P, G]), [sb("hot0", [P, G, E]), sb("hot1", [P, G, E])], sb("rest", [P, G, E])
        best = [sb("best0", [P, G]), sb("best1", [P, G])]
        d_ready, e_ready, step = sig("d_ready"), sig("e_ready"), sig("step")
        block = ctx.enter_context(nc.Block())

        def per_group(t):
            return t[:, :].unsqueeze(2).broadcast_to([P, G, E])

        @block.scalar
        def _(act):
            act.wait_ge(d_ready.sem, 1)
            act.activation(gates[:, :, :], d[:, :, :], ACT.Exp).then_inc(e_ready.sem, 1)

        @block.vector
        def _(dve):
            done = [0]

            def then(ins):
                done[0] += 1
                ins.then_inc(step.sem, 1)
                dve.wait_ge(step.sem, done[0])

            then(dve.tensor_reduce(lmax[:, :], LG[:, :, :], AX.X, ALU.max))
            dve.tensor_tensor(d[:, :, :], LG[:, :, :], per_group(lmax), ALU.subtract).then_inc(d_ready.sem, 1)
            dve.wait_ge(e_ready.sem, 1)
            then(dve.tensor_reduce(sm[:, :], gates[:, :, :], AX.X, ALU.add))
            then(dve.reciprocal(inv[:, :], sm[:, :]))
            then(dve.tensor_tensor(gates[:, :, :], gates[:, :, :], per_group(inv), ALU.mult))
            for n in range(2):
                src = gates if n == 0 else rest
                then(dve.tensor_reduce(best[n][:, :], src[:, :, :], AX.X, ALU.max))
                then(dve.tensor_tensor(eq[:, :, :], src[:, :, :], per_group(best[n]), ALU.is_equal))
                then(dve.tensor_tensor(eq[:, :, :], eq[:, :, :], k("rank").unsqueeze(1).broadcast_to([P, G, E]), ALU.mult))
                then(dve.tensor_reduce(first[:, :], eq[:, :, :], AX.X, ALU.max))
                then(dve.tensor_tensor(hot[n][:, :, :], eq[:, :, :], per_group(first), ALU.is_equal))
                if n == 0:
                    then(dve.scalar_tensor_tensor(rest[:, :, :], hot[0][:, :, :], -2.0, gates[:, :, :], ALU.mult, ALU.add))
            then(dve.tensor_tensor(sm[:, :], best[0][:, :], best[1][:, :], ALU.add))
            then(dve.tensor_scalar(sm[:, :], sm[:, :], 1e-8, None, ALU.add))
            then(dve.reciprocal(inv[:, :], sm[:, :]))
            then(dve.tensor_tensor(hot[0][:, :, :], hot[0][:, :, :], hot[1][:, :, :], ALU.add))
            then(dve.tensor_tensor(gates[:, :, :], gates[:, :, :], hot[0][:, :, :], ALU.mult))
            then(dve.tensor_tensor(MASK[:, :, :], gates[:, :, :], per_group(inv), ALU.mult))


def experts(env, name, w1_in, w2_in, b2_in, NF, vb1, out):
    nc, X, HT_all, MASK, k, vec = (env[n] for n in ("nc", "X", "HT_all", "MASK", "k", "vec"))
    ctx = Phase(nc, name)
    with ctx:
        def sb(n, shape, dt=F32):
            return ctx.enter_context(nc.sbuf_tensor(f"{name}_{n}", shape, dt))

        def sig(n, per=1, credit=0):
            return Signal(ctx, nc, f"{name}_{n}", per, credit)

        N = TG * P
        w1, w2, b2 = sb("w1", [P, E, NF * P]), sb("w2", [P, E, NF, D]), sb("b2", [E, D])
        mk, mkT = sb("mk", [P, TG, E]), sb("mkT", [E, TG, P])
        hid = sb("hid", [P, 2, NF, N])
        pH = ctx.enter_context(nc.psum_tensor(f"{name}_pH", [P, 4, N], F32))
        pY = ctx.enter_context(nc.psum_tensor(f"{name}_pY", [P, 2, TG, D], F32))
        pB = ctx.enter_context(nc.psum_tensor(f"{name}_pB", [P, TG, D], F32))
        w_loaded = [ctx.semaphore(f"{name}_w_loaded{e}") for e in range(E)]
        b2_loaded = ctx.semaphore(f"{name}_b2_loaded")
        mk_ready, mkT_done, mkT_ready = sig("mk_ready"), sig("mkT_done"), sig("mkT_ready")
        b_done, b_added = sig("b_done"), sig("b_added", TG)
        h_done, h_ready = sig("h_done", E * NF), sig("h_ready", E * NF, credit=4)
        y_done, y_added = sig("y_done", E, credit=2), sig("y_added", E * TG, credit=2 * TG)
        stored = ctx.semaphore(f"{name}_stored")
        block = ctx.enter_context(nc.Block())

        @block.sync
        def _(sp):
            for e in range(E):
                sp.dma_start(w1[:, e, :], w1_in[:, e, :]).then_inc(w_loaded[e], 16)
                sp.dma_start(w2[:, e, :, :], w2_in[:, e, :, :]).then_inc(w_loaded[e], 16)
            sp.dma_start(b2[:, :], b2_in).then_inc(b2_loaded, 16)
            if out is not None:
                with sp.Fori(0, NB) as n:
                    sp.wait_ge(y_added.sem, y_added.at(n))
                    sp.dma_start(out.rearrange("(g bb) t d -> (bb t) g d", bb=BG)[:, bass.ds(n * TG, TG), :],
                                 X[:, bass.ds(n * TG, TG), :]).then_inc(stored, 16)
                sp.wait_ge(stored, 16 * NB)

        @block.tensor
        def _(pe):
            for e in range(E):
                pe.wait_ge(w_loaded[e], 32)
            pe.wait_ge(b2_loaded, 16)
            pe.sem_inc(y_done.sem, y_done.credit)
            with pe.Fori(0, NB) as n:
                pe.wait_ge(mk_ready.sem, mk_ready.at(n))
                for t in range(TG):
                    mm = pe.transpose(pB[0:E, t, :], mk[:, t, :], k("ident"))
                mm.then_inc(mkT_done.sem, 1)
                pe.wait_ge(mkT_ready.sem, mkT_ready.at(n))
                for t in range(TG):
                    mm = pe.matmul(pB[:, t, :], mkT[:, t, :], b2[:, :], start=True, stop=True)
                mm.then_inc(b_done.sem, 1)

                def up(e):
                    for c in range(NF):
                        m = e * NF + c
                        pe.wait_ge(h_ready.sem, h_ready.at(n, m + 1) - 4)
                        pe.matmul(pH[:, m % 4, :], w1[:, e, c * P:(c + 1) * P],
                                  HT_all[:, bass.ds(n * TG, TG), :].rearrange("p g t -> p (g t)"),
                                  start=True, stop=True).then_inc(h_done.sem, 1)

                def down(e):
                    pe.wait_ge(h_ready.sem, h_ready.at(n, (e + 1) * NF))
                    pe.wait_ge(y_added.sem, y_added.at(n, (e - 1) * TG))
                    for t in range(TG):
                        for c in range(NF):
                            mm = pe.matmul(pY[:, e % 2, t, :], hid[:, e % 2, c, t * P:(t + 1) * P], w2[:, e, c, :],
                                           start=(c == 0), stop=(c == NF - 1))
                    mm.then_inc(y_done.sem, 1)

                up(0)
                for e in range(E):
                    if e + 1 < E:
                        up(e + 1)
                    down(e)

        @block.scalar
        def _(act):
            act.sem_inc(h_ready.sem, h_ready.credit)
            with act.Fori(0, NB) as n:
                act.wait_ge(mkT_done.sem, mkT_done.at(n))
                act.activation(mkT[:, :, :], pB[0:E, :, :], ACT.Copy).then_inc(mkT_ready.sem, 1)
                for e in range(E):
                    act.wait_ge(y_done.sem, y_done.at(n, e - 1))
                    for c in range(NF):
                        m = e * NF + c
                        act.wait_ge(h_done.sem, h_done.at(n, m + 1))
                        act.activation(hid[:, e % 2, c, :], pH[:, m % 4, :], ACT.Relu, bias=vec[:, vb1 + m:vb1 + m + 1]
                                       ).then_inc(h_ready.sem, 1)

        @block.vector
        def _(dve):
            dve.sem_inc(y_added.sem, y_added.credit)
            with dve.Fori(0, NB) as n:
                dve.tensor_copy(mk[:, :, :], MASK[:, bass.ds(n * TG, TG), :]).then_inc(mk_ready.sem, 1)
                dve.wait_ge(mk_ready.sem, mk_ready.at(n))
                dve.wait_ge(b_done.sem, b_done.at(n))
                for t in range(TG):
                    x = X[:, bass.ds(n * TG + t, 1), :].rearrange("p g d -> p (g d)")
                    dve.tensor_tensor(x, pB[:, t, :], x, ALU.add).then_inc(b_added.sem, 1)
                dve.wait_ge(b_added.sem, b_added.at(n))
                for e in range(E):
                    dve.wait_ge(y_done.sem, y_done.at(n, e + 1))
                    if e > 0:
                        dve.wait_ge(y_added.sem, y_added.at(n, e * TG))
                    for t in range(TG):
                        x = X[:, bass.ds(n * TG + t, 1), :].rearrange("p g d -> p (g d)")
                        dve.scalar_tensor_tensor(x, pY[:, e % 2, t, :], mk[:, t, e:e + 1], x, ALU.mult, ALU.add
                                                 ).then_inc(y_added.sem, 1)
                dve.wait_ge(y_added.sem, y_added.at(n))


def cross_layer1(env):
    nc, io, X, w, v, k, bo1 = (env[n] for n in ("nc", "io", "X", "w", "v", "k", "bo1"))
    ctx = Phase(nc, "c")
    with ctx:
        def sb(name, shape, dt=F32):
            return ctx.enter_context(nc.sbuf_tensor("c_" + name, shape, dt))

        def ps(name, shape):
            return ctx.enter_context(nc.psum_tensor("c_" + name, shape, F32))

        def sig(name, per=1, credit=0):
            return Signal(ctx, nc, "c_" + name, per, credit)

        ctxT = sb("ctxT", [P, BG, S])
        hT, q = sb("hT", [P, P]), sb("q", [P, P])
        qq = sb("qq", [P, 2, HQ, T])
        ks = sb("ks", [P, 2, S])
        vs, vl = sb("vs", [P, BG, SC, D]), sb("vl", [NQ, BG, D])
        nm, den, rinv = sb("nm", [P, NQ]), sb("den", [P, 2, NQ]), sb("rinv", [P, BG, NQ])
        pr = sb("pr", [P, 2, NQ, S])
        prT, prl = sb("prT", [P, SC, NQ, P]), sb("prl", [NQ, P])
        rm = sb("rm", [P, BG, NQ, HQ * HD])
        om, osum, on, ob, yb = sb("om", [P, BG, HQ, T]), sb("osum", [P, BG, T]), sb("on", [P, P]), sb("ob", [P, P]), sb("yb", [P, D])
        pS = ps("pS", [P, NQ, 512])
        pT = ps("pT", [P, SC, NQ, P])
        pM = ps("pM", [P, 512])
        pO = ps("pO", [P, BG, HQ, T])

        n4 = Norm(ctx, nc, "c_n4", env)
        ctx_loaded = [sig(f"ctx_loaded{b}", 16) for b in range(BG)]
        hT_done, hT_ready, q_done, q_ready = sig("hT_done"), sig("hT_ready"), sig("q_done"), sig("q_ready")
        qq_ready = sig("qq_ready")
        k_done, k_ready = sig("k_done"), sig("k_ready")
        v_done, v_ready = sig("v_done", credit=BG), sig("v_ready")
        vl_ready, prl_ready = sig("vl_ready"), sig("prl_ready")
        s_done, max_ready, e_ready = sig("s_done", NQ), sig("max_ready", NQ), sig("e_ready", NQ, credit=NQ)
        pT_done, pT0_ready, pT1_ready = sig("pT_done", SC), sig("pT0_ready"), sig("pT1_ready")
        o_done, rinv_ready, rm_ready = sig("o_done"), sig("rinv_ready"), sig("rm_ready")
        om_ready, osum_ready = sig("om_ready"), sig("osum_ready")
        rT_done, on_ready, ob_ready, y_done, yb_ready, x_ready = (sig("rT_done"), sig("on_ready"), sig("ob_ready"), sig("y_done"),
                                                                 sig("yb_ready"), sig("x_ready"))
        SCALE = float(HD) ** -0.5

        block = ctx.enter_context(nc.Block())

        @block.sync
        def _(sp):
            with sp.Fori(0, G) as g:
                for b in range(BG):
                    sp.wait_ge(v_done.sem, v_done.at(g * BG + b - BG))
                    sp.dma_start(ctxT[:, b, :].unsqueeze(1), io["ctxT"][bass.ds(g, 1), :, b, :].rearrange("g p s -> p g s")
                                 ).then_inc(ctx_loaded[b].sem, 16)

        @block.tensor
        def _(pe):
            pe.sem_inc(v_done.sem, v_done.credit)

            def norm_T(g):
                pe.wait_ge(n4.h_ready.sem, n4.h_ready.at(g))
                pe.matmul(pM[:, 0:P], n4.h[:, :], k("ident"), start=True, stop=True).then_inc(hT_done.sem, 1)

            def queries(g):
                pe.wait_ge(hT_ready.sem, hT_ready.at(g))
                pe.matmul(pM[:, 0:P], w("wq1"), hT[:, :], start=True, stop=True).then_inc(q_done.sem, 1)

            def keys(g, b, n):
                pe.wait_ge(ctx_loaded[b].sem, ctx_loaded[b].at(g))
                pe.matmul(pM[:, 0:S], w("wk1"), ctxT[:, b, :], start=True, stop=True).then_inc(k_done.sem, 1)

            def values(b, n):
                pe.wait_ge(k_ready.sem, k_ready.at(n))
                for c in range(SC):
                    pe.matmul(pM[:, c * D:(c + 1) * D], ctxT[:, b, c * P:(c + 1) * P], w("wv1"), start=True, stop=True)
                return pe.matmul(pM[0:NQ, SC * D:(SC + 1) * D], ctxT[:, b, SM:S].broadcast_to([P, NQ]), w("wv1"),
                                 start=True, stop=True)

            def values_left(n):
                pe.wait_ge(vl_ready.sem, vl_ready.at(n))

            def last_weights(b):
                return pe.matmul(pM[0:NQ, (SC + 1) * D:(SC + 2) * D], pr[:, b % 2, :, SM], k("ident"), start=True, stop=True)

            def scores(b, n):
                pe.wait_ge(k_ready.sem, k_ready.at(n))
                pe.wait_ge(qq_ready.sem, qq_ready.at(n))
                for c in range(NQ):
                    r = slice(c * T, (c + 1) * T)
                    pe.wait_ge(e_ready.sem, e_ready.at(n - 1, c + 1))
                    pe.matmul(pS[:, c, 0:S], qq[r, b % 2, :, :], ks[r, b % 2, :], start=True, stop=True).then_inc(s_done.sem, 1)

            def turn(b, n, c):
                if c == 0:
                    pe.wait_ge(e_ready.sem, e_ready.at(n))
                for j in range(NQ):
                    mm = pe.matmul(pT[:, c, j, :], pr[:, b % 2, j, c * P:(c + 1) * P], k("ident"), start=True, stop=True)
                mm.then_inc(pT_done.sem, 1)

            def sums(b, n):
                pe.wait_ge(prl_ready.sem, prl_ready.at(n))
                for c, ready in enumerate((pT0_ready, pT1_ready)):
                    pe.wait_ge(ready.sem, ready.at(n))
                    for j in range(NQ):
                        pe.matmul(pO[j * T:(j + 1) * T, b, :, :], vs[:, b, c, j * T:(j + 1) * T], prT[:, c, j, :],
                                  start=(c == 0), stop=False, skip_group_check=True)
                pe.matmul(pO[:, b, :, :], vl[:, b, :], prl[:, :], start=False, stop=True,
                          skip_group_check=True).then_inc(o_done.sem, 1)

            def scales(g):
                pe.wait_ge(rm_ready.sem, rm_ready.at(g))
                for b in range(BG):
                    mm = pe.matmul(pM[:, b * T:(b + 1) * T], rm[:, b, :, :], k("qsel"), start=True, stop=True)
                mm.then_inc(rT_done.sem, 1)

            def project(g):
                pe.wait_ge(ob_ready.sem, ob_ready.at(g))
                pe.matmul(pM[:, P:2 * P], ob[:, :], w("wo1"), start=True, stop=True).then_inc(y_done.sem, 1)

            def group_product(b, g, first, last):
                if b > 0:
                    values_left(g * BG + b)
                if b == 1 and not last:
                    norm_T(g + 1)
                if b == 2 and not first:
                    scales(g - 1)
                if b == BG - 1:
                    if not last:
                        queries(g + 1)
                    if not first:
                        project(g - 1)

            def group_product_left(b, g, first, last):
                if b == 1 and not last:
                    pe.wait_ge(hT_ready.sem, hT_ready.at(g + 1))
                if b == 2 and not first:
                    pe.wait_ge(on_ready.sem, on_ready.at(g - 1))
                if b == BG - 1:
                    if not last:
                        pe.wait_ge(q_ready.sem, q_ready.at(g + 1))
                    if not first:
                        pe.wait_ge(yb_ready.sem, yb_ready.at(g - 1))

            def body(g, first, last):
                for b in range(BG):
                    n = g * BG + b
                    turns, more = not first or b > 0, b < BG - 1 or not last
                    scores(b, n)
                    group_product(b, g, first, last)
                    if not first or b > 1:
                        if b == 2 and not first:
                            pe.wait_ge(om_ready.sem, om_ready.at(g - 1))
                        sums((b - 2) % BG, n - 2)
                    if turns:
                        turn((b - 1) % BG, n - 1, 0)
                    if b == 0:
                        values_left(n)
                    group_product_left(b, g, first, last)
                    if more:
                        keys(g if b < BG - 1 else g + 1, (b + 1) % BG, n + 1)
                    if turns:
                        turn((b - 1) % BG, n - 1, 1)
                    if more:
                        mm = values((b + 1) % BG, n + 1)
                    if turns:
                        mm = last_weights((b - 1) % BG)
                    mm.then_inc(v_done.sem, 1)

            norm_T(0)
            queries(0)
            pe.wait_ge(q_ready.sem, q_ready.at(0))
            keys(0, 0, 0)
            values(0, 0).then_inc(v_done.sem, 1)
            body(0, True, False)
            with pe.Fori(1, G - 1) as g:
                body(g, False, False)
            body(G - 1, False, True)
            sums(BG - 2, B - 2)
            for c in range(SC):
                turn(BG - 1, B - 1, c)
            last_weights(BG - 1).then_inc(v_done.sem, 1)
            sums(BG - 1, B - 1)
            scales(G - 1)
            project(G - 1)

        @block.scalar
        def _(act):
            act.sem_inc(e_ready.sem, e_ready.credit)

            def keys(b, n):
                act.wait_ge(k_done.sem, k_done.at(n))
                act.activation(ks[:, b % 2, :], pM[:, 0:S], ACT.Identity, bias=v("bk1")).then_inc(k_ready.sem, 1)

            def exps(b, n, quads):
                for c in quads:
                    act.wait_ge(max_ready.sem, max_ready.at(n, c + 1))
                    act.activation(pr[:, b % 2, c, :], pS[:, c, 0:S], ACT.Exp, bias=nm[:, c:c + 1],
                                   accum_out=den[:, b % 2, c:c + 1]).then_inc(e_ready.sem, 1)

            def turned(n):
                act.wait_ge(pT_done.sem, pT_done.at(n, 1))
                act.activation(prT[:, 0, :, :], pT[:, 0, :, :], ACT.Copy).then_inc(pT0_ready.sem, 1)

            def norm_T(g):
                act.wait_ge(hT_done.sem, hT_done.at(g))
                act.activation(hT[:, :], pM[:, 0:P], ACT.Copy).then_inc(hT_ready.sem, 1)

            def body(g, first, last):
                for b in range(BG):
                    n = g * BG + b
                    exps(b, n, range(NQ))
                    if b == 1 and not last:
                        norm_T(g + 1)
                    if not first or b > 0:
                        turned(n - 1)
                    if b < BG - 1 or not last:
                        keys((b + 1) % BG, n + 1)

            norm_T(0)
            keys(0, 0)
            body(0, True, False)
            with act.Fori(1, G - 1) as g:
                body(g, False, False)
            body(G - 1, False, True)
            turned(B - 1)

        @block.gpsimd
        def _(pool):
            def spread(b, n, g):
                pool.wait_ge(q_ready.sem, q_ready.at(g))
                if not (isinstance(n, int) and n < 2):
                    pool.wait_ge(s_done.sem, s_done.at(n - 2))
                pool.tensor_tensor(qq[:, b % 2, :, :], q[:, b * T:(b + 1) * T].unsqueeze(1).broadcast_to([P, HQ, T]),
                                   k("quad").unsqueeze(2).broadcast_to([P, HQ, T]), ALU.mult).then_inc(qq_ready.sem, 1)

            def scales(g):
                pool.wait_ge(rinv_ready.sem, rinv_ready.at(g * BG + BG - 1))
                pool.tensor_tensor(rm[:, :, :, :], rinv[:, :, :].unsqueeze(3).broadcast_to([P, BG, NQ, HQ * HD]),
                                   k("vmask").rearrange("p (c f) -> p c f", c=NQ).unsqueeze(1).broadcast_to([P, BG, NQ, HQ * HD]),
                                   ALU.mult).then_inc(rm_ready.sem, 1)

            def body(g, first, last):
                for b in range(BG):
                    n = g * BG + b
                    if b < BG - 1:
                        spread(b + 1, n + 1, g)
                    elif not last:
                        spread(0, n + 1, g + 1)
                    if b == 0:
                        if not last:
                            n4.gpsimd(pool, g + 1)
                        if not first:
                            scales(g - 1)

            n4.gpsimd(pool, 0)
            spread(0, 0, 0)
            body(0, True, False)
            with pool.Fori(1, G - 1) as g:
                body(g, False, False)
            body(G - 1, False, True)
            scales(G - 1)

        @block.vector
        def _(dve):
            def x_of(g):
                return X[:, bass.ds(g, 1), :].rearrange("p g d -> p (g d)")

            def queries(g):
                dve.wait_ge(q_done.sem, q_done.at(g))
                if not (isinstance(g, int) and g == 0):
                    dve.wait_ge(qq_ready.sem, qq_ready.at(g * BG - 1))
                dve.tensor_scalar(q[:, :], pM[:, 0:P], v("bq1"), SCALE, ALU.add, ALU.mult).then_inc(q_ready.sem, 1)

            def maxima(n):
                for c in range(NQ):
                    dve.wait_ge(s_done.sem, s_done.at(n, c + 1))
                    dve.tensor_reduce(nm[:, c:c + 1], pS[:, c, 0:S], AX.X, ALU.max, negate=True).then_inc(max_ready.sem, 1)

            def values(b, n):
                dve.wait_ge(v_done.sem, v_done.at(n))
                dve.tensor_copy(vs[:, b, :, :], pM[:, 0:SM].rearrange("p (c d) -> p c d", c=SC)).then_inc(v_ready.sem, 1)
                dve.tensor_tensor(vl[:, b, :], pM[0:NQ, SC * D:(SC + 1) * D], k("row4")[0:NQ, :], ALU.mult).then_inc(vl_ready.sem, 1)

            def turned(n):
                dve.wait_ge(pT_done.sem, pT_done.at(n))
                dve.tensor_copy(prT[:, 1, :, :], pT[:, 1, :, :]).then_inc(pT1_ready.sem, 1)

            def last_weights(b, n, g_read):
                dve.wait_ge(v_done.sem, v_done.at(n + 2))
                dve.tensor_copy(prl[:, :], pM[0:NQ, (SC + 1) * D:(SC + 2) * D]).then_inc(prl_ready.sem, 1)
                if g_read is not None:
                    dve.wait_ge(rm_ready.sem, rm_ready.at(g_read))
                dve.reciprocal(rinv[:, b, :], den[:, b % 2, :]).then_inc(rinv_ready.sem, 1)

            def gather(g):
                dve.wait_ge(o_done.sem, o_done.at(g * BG + BG - 1))
                dve.tensor_tensor(om[:, :, :, :], pO[:, :, :, :],
                                  k("quad").unsqueeze(1).unsqueeze(3).broadcast_to([P, BG, HQ, T]), ALU.mult).then_inc(om_ready.sem, 1)
                dve.wait_ge(om_ready.sem, om_ready.at(g))
                dve.tensor_reduce(osum[:, :, :], om[:, :, :, :].rearrange("p b h t -> p b t h"), AX.X, ALU.add
                                  ).then_inc(osum_ready.sem, 1)

            def scale(g):
                dve.wait_ge(rT_done.sem, rT_done.at(g))
                dve.wait_ge(osum_ready.sem, osum_ready.at(g))
                dve.tensor_tensor(on[:, :], pM[:, 0:P], osum[:, :, :].rearrange("p b t -> p (b t)"), ALU.mult).then_inc(on_ready.sem, 1)
                dve.wait_ge(on_ready.sem, on_ready.at(g))
                dve.tensor_scalar(ob[:, :], on[:, :], v("bv1"), None, ALU.add).then_inc(ob_ready.sem, 1)

            def finish(g):
                dve.wait_ge(y_done.sem, y_done.at(g))
                dve.tensor_tensor(yb[:, :], pM[:, P:2 * P], bo1[:, :], ALU.add).then_inc(yb_ready.sem, 1)
                dve.wait_ge(yb_ready.sem, yb_ready.at(g))
                dve.tensor_tensor(x_of(g), yb[:, :], x_of(g), ALU.add).then_inc(x_ready.sem, 1)

            def body(g, first, last):
                for b in range(BG):
                    n = g * BG + b
                    maxima(n)
                    if b == 0 and not last:
                        n4.vector_stats(dve, x_of(g + 1), g + 1)
                    if b == 1 and not first:
                        gather(g - 1)
                    if b == 2 and not first:
                        scale(g - 1)
                    if b == BG - 1:
                        if not last:
                            if not first:
                                dve.wait_ge(y_done.sem, y_done.at(g - 1))
                            queries(g + 1)
                        if not first:
                            finish(g - 1)
                    if not first or b > 0:
                        turned(n - 1)
                    if not first or b > 0:
                        last_weights((b - 1) % BG, n - 1, g - 1 if (b == 1 and not first) else None)
                    if b < BG - 1 or not last:
                        values((b + 1) % BG, n + 1)
                    if b == 0 and not last:
                        n4.vector_scale(dve, x_of(g + 1), g + 1)

            n4.vector_stats(dve, x_of(0), 0)
            n4.vector_scale(dve, x_of(0), 0)
            queries(0)
            values(0, 0)
            body(0, True, False)
            with dve.Fori(1, G - 1) as g:
                body(g, False, False)
            body(G - 1, False, True)
            turned(B - 1)
            last_weights(BG - 1, B - 1, None)
            gather(G - 1)
            scale(G - 1)
            finish(G - 1)


def self_layer1(env):
    nc, io, X, HT_all, LG, w, v, k = (env[n] for n in ("nc", "io", "X", "HT_all", "LG", "w", "v", "k"))
    ctx = Phase(nc, "s")
    with ctx:
        def sb(name, shape, dt=F32):
            return ctx.enter_context(nc.sbuf_tensor("s_" + name, shape, dt))

        def ps(name, shape):
            return ctx.enter_context(nc.psum_tensor("s_" + name, shape, F32))

        def sig(name, per=1, credit=0):
            return Signal(ctx, nc, "s_" + name, per, credit)

        wqkv, wout, gate = sb("wqkv", [P, 3, RI]), sb("wout", [P, RP, D]), sb("gate", [P, E])
        gamma1, sq, ss, root, rms, xn = (sb("gamma1", [P, 1]), sb("sq", [P, D]), sb("ss", [P, 1]), sb("root", [P, 1]), sb("rms", [P, 1]),
                                         sb("xn", [P, D]))
        irms = sb("irms", [P, 1])
        hT = sb("hT", [P, P])
        qT = sb("qT", [P, RP, P])
        kp = sb("kp", [P, RP, BG, 2, T])
        vs = sb("vs", [P, RI])
        smax, sd, se, ssum, sinv, sn = (sb("smax", [P, H]), sb("sd", [P, H, T]), sb("se", [P, H, T]), sb("ssum", [P, H]), sb("sinv", [P, H]),
                                        sb("sn", [P, H, T]))
        pt = sb("pt", [P, H, P])
        oT, h5T = sb("oT", [P, RP, P]), sb("h5T", [P, P])
        pA = ps("pA", [P, RP, P])
        pK = ps("pK", [P, RP, P])
        pV = ps("pV", [P, RI])
        pS = ps("pS", [P, H, T])
        pM = ps("pM", [P, 4, P])
        n5 = Norm(ctx, nc, "s_n5", env)
        n6 = Norm(ctx, nc, "s_n6", env)
        w_loaded, gamma_ready, zeroed = sig("w_loaded", 48), sig("gamma_ready"), sig("zeroed", 2)
        ss_ready, root_ready, rms_ready, irms_ready, xn_ready = (sig("ss_ready"), sig("root_ready"), sig("rms_ready"), sig("irms_ready"),
                                                                sig("xn_ready"))
        hT_done, hT_ready = sig("hT_done"), sig("hT_ready")
        q_done, q_ready = sig("q_done"), sig("q_ready")
        k_done, k_ready = sig("k_done"), sig("k_ready", 2)
        v_done, v_ready = sig("v_done"), sig("v_ready")
        s_done, max_ready, sd_ready, se_ready = sig("s_done"), sig("max_ready"), sig("sd_ready"), sig("se_ready")
        sum_ready, sinv_ready, sn_ready, pt_ready = sig("sum_ready"), sig("sinv_ready"), sig("sn_ready"), sig("pt_ready")
        o_done, o_ready, y_done, x_ready = sig("o_done"), sig("o_ready"), sig("y_done"), sig("x_ready")
        h5T_done, h5T_ready, h5T_kept = sig("h5T_done"), sig("h5T_ready"), sig("h5T_kept", credit=1)
        xh_ready, lg_done, lg_ready = sig("xh_ready"), sig("lg_done"), sig("lg_ready", credit=1)
        SCALE = float(RH) ** -0.5
        block = ctx.enter_context(nc.Block())

        def slots(eng, slot):
            slot(0, True, False, True)
            with eng.Fori(1, G - 2) as g:
                slot(g, False, False, True)
            slot(G - 2, False, False, False)
            slot(G - 1, False, True, False)

        @block.sync
        def _(sp):
            sp.dma_start(wqkv[:, :, :].rearrange("p a n -> p (a n)"), io["wqkv"]).then_inc(w_loaded.sem, 16)
            sp.dma_start(wout[:, :, :], io["wout"]).then_inc(w_loaded.sem, 16)
            sp.dma_start(gate[:, :], io["gate"]).then_inc(w_loaded.sem, 16)

        @block.tensor
        def _(pe):
            pe.wait_ge(w_loaded.sem, 3 * 16)

            def norm_T(g):
                pe.wait_ge(xn_ready.sem, xn_ready.at(g))
                pe.matmul(pM[:, 0, :], xn[:, :], k("ident"), start=True, stop=True).then_inc(hT_done.sem, 1)

            def queries_keys(g):
                pe.wait_ge(hT_ready.sem, hT_ready.at(g))
                for j in range(RP):
                    mm = pe.matmul(pA[:, j, :], wqkv[:, 0, j * P:(j + 1) * P], hT[:, :], start=True, stop=True)
                mm.then_inc(q_done.sem, 1)
                for j in range(RP):
                    mm = pe.matmul(pK[:, j, :], wqkv[:, 1, j * P:(j + 1) * P], hT[:, :], start=True, stop=True)
                mm.then_inc(k_done.sem, 1)

            def values(g):
                for c in range(2):
                    mm = pe.matmul(pV[:, c * 512:(c + 1) * 512], hT[:, :], wqkv[:, 2, c * 512:(c + 1) * 512], start=True, stop=True)
                mm.then_inc(v_done.sem, 1)

            def scores(g):
                pe.wait_ge(q_ready.sem, q_ready.at(g))
                pe.wait_ge(k_ready.sem, k_ready.at(g))
                for j in range(RP):
                    for b in range(BG):
                        mm = pe.matmul(pS[b * T:(b + 1) * T, 2 * j:2 * j + 2, :], qT[:, j, b * T:(b + 1) * T], kp[:, j, b, :, :],
                                       start=True, stop=True)
                mm.then_inc(s_done.sem, 1)

            def sums(g):
                pe.wait_ge(pt_ready.sem, pt_ready.at(g))
                pe.wait_ge(v_ready.sem, v_ready.at(g))
                for h in range(H):
                    r = slice(RH * (h % 2), RH * (h % 2) + RH)
                    mm = pe.matmul(pA[r, h // 2, :], vs[:, h * RH:(h + 1) * RH], pt[:, h, :], start=True, stop=True)
                mm.then_inc(o_done.sem, 1)

            def project(g):
                pe.wait_ge(o_ready.sem, o_ready.at(g))
                for j in range(RP):
                    mm = pe.matmul(pM[:, 1, :], oT[:, j, :], wout[:, j, :], start=(j == 0), stop=(j == RP - 1))
                mm.then_inc(y_done.sem, 1)

            def h5_T(g):
                pe.wait_ge(n6.h_ready.sem, n6.h_ready.at(g))
                pe.matmul(pM[:, 2, :], n6.h[:, :], k("ident"), start=True, stop=True).then_inc(h5T_done.sem, 1)

            def logits(g):
                pe.wait_ge(h5T_ready.sem, h5T_ready.at(g))
                pe.matmul(pM[:, 3, 0:E], h5T[:, :], gate[:, :], start=True, stop=True).then_inc(lg_done.sem, 1)

            def slot(g, first, last, norm):
                if not first:
                    pe.wait_ge(lg_ready.sem, lg_ready.at(g - 2))
                if not last:
                    norm_T(g + 1)
                scores(g)
                if not first:
                    if not last:
                        pe.wait_ge(hT_ready.sem, hT_ready.at(g + 1))
                    project(g - 1)
                if not last:
                    queries_keys(g + 1)
                if not first:
                    h5_T(g - 1)
                if not last:
                    pe.wait_ge(v_ready.sem, v_ready.at(g))
                    values(g + 1)
                    pe.wait_ge(q_ready.sem, q_ready.at(g + 1))
                if not first:
                    logits(g - 1)
                sums(g)

            norm_T(0)
            queries_keys(0)
            values(0)
            slots(pe, slot)
            pe.wait_ge(lg_ready.sem, lg_ready.at(G - 2))
            project(G - 1)
            h5_T(G - 1)
            logits(G - 1)

        @block.scalar
        def _(act):
            act.wait_ge(gamma_ready.sem, 1)
            act.wait_ge(zeroed.sem, 2)

            def norm_T(g):
                act.wait_ge(hT_done.sem, hT_done.at(g))
                act.activation(hT[:, :], pM[:, 0, :], ACT.Copy, scale=gamma1[:, :]).then_inc(hT_ready.sem, 1)

            def queries(g):
                act.wait_ge(q_done.sem, q_done.at(g))
                act.activation(qT[:, :, :], pA[:, :, :], ACT.Copy, scale=SCALE).then_inc(q_ready.sem, 1)

            def keys(g):
                act.wait_ge(k_done.sem, k_done.at(g))
                for i in range(2):
                    r = slice(RH * i, RH * i + RH)
                    act.activation(kp[r, :, :, i, :].rearrange("p j b s -> p (j b) s"),
                                   pK[r, :, :].rearrange("p j (b s) -> p (j b) s", b=BG), ACT.Copy).then_inc(k_ready.sem, 1)

            def values(g, first):
                act.wait_ge(v_done.sem, v_done.at(g))
                if not first:
                    act.wait_ge(o_done.sem, o_done.at(g - 1))
                act.activation(vs[:, :], pV[:, :], ACT.Copy).then_inc(v_ready.sem, 1)

            def outputs(g):
                act.wait_ge(o_done.sem, o_done.at(g))
                act.activation(oT[:, :, :], pA[:, :, :], ACT.Copy).then_inc(o_ready.sem, 1)

            def h5_T(g):
                act.wait_ge(h5T_done.sem, h5T_done.at(g))
                act.wait_ge(h5T_kept.sem, h5T_kept.at(g, 0))
                act.activation(h5T[:, :], pM[:, 2, :], ACT.Copy).then_inc(h5T_ready.sem, 1)

            def slot(g, first, last, norm):
                if not first:
                    outputs(g - 1)
                if not last:
                    norm_T(g + 1)
                values(g, first)
                act.wait_ge(sd_ready.sem, sd_ready.at(g))
                act.activation(se[:, :, :], sd[:, :, :], ACT.Exp).then_inc(se_ready.sem, 1)
                if not last:
                    queries(g + 1)
                    keys(g + 1)
                if not first:
                    h5_T(g - 1)

            norm_T(0)
            queries(0)
            keys(0)
            slots(act, slot)
            outputs(G - 1)
            h5_T(G - 1)

        @block.gpsimd
        def _(pool):
            pool.memset(kp[:, :, :, :, :], 0.0).then_inc(zeroed.sem, 1)
            pool.memset(pt[:, :, :], 0.0).then_inc(zeroed.sem, 1)
            pool.sem_inc(h5T_kept.sem, h5T_kept.credit)

            def root_of(g):
                pool.wait_ge(ss_ready.sem, ss_ready.at(g))
                pool.tensor_tensor(root[:, :], ss[:, :], k("root"), ALU.pow).then_inc(root_ready.sem, 1)

            def keep(g):
                pool.wait_ge(h5T_ready.sem, h5T_ready.at(g))
                pool.tensor_copy(HT_all[:, bass.ds(g, 1), :].rearrange("p g t -> p (g t)"), h5T[:, :]).then_inc(h5T_kept.sem, 1)

            def slot(g, first, last, norm):
                if norm:
                    n5.gpsimd(pool, g + 2)
                if not first:
                    n6.gpsimd(pool, g - 1)
                if norm:
                    root_of(g + 2)
                if not first:
                    keep(g - 1)

            for g in range(2):
                n5.gpsimd(pool, g)
                root_of(g)
            slots(pool, slot)
            n6.gpsimd(pool, G - 1)
            keep(G - 1)

        @block.vector
        def _(dve):
            dve.tensor_scalar(gamma1[:, :], v("gamma"), 1.0, None, ALU.add).then_inc(gamma_ready.sem, 1)
            dve.wait_ge(zeroed.sem, 2)
            dve.sem_inc(lg_ready.sem, lg_ready.credit)

            def x_of(g):
                return X[:, bass.ds(g, 1), :].rearrange("p g d -> p (g d)")

            def squares(g):
                n5.vector_scale(dve, x_of(g), g)
                dve.wait_ge(n5.h_ready.sem, n5.h_ready.at(g))
                dve.scalar_tensor_tensor(sq[:, :], n5.h[:, :], 1.0, n5.h[:, :], ALU.mult, ALU.mult, accum_out=ss[:, :]
                                         ).then_inc(ss_ready.sem, 1)

            def bound(g):
                dve.wait_ge(root_ready.sem, root_ready.at(g))
                dve.tensor_scalar(rms[:, :], root[:, :], 1e-12, None, ALU.max).then_inc(rms_ready.sem, 1)

            def inverse(g):
                dve.wait_ge(rms_ready.sem, rms_ready.at(g))
                dve.reciprocal(irms[:, :], rms[:, :]).then_inc(irms_ready.sem, 1)

            def scaled(g):
                dve.wait_ge(irms_ready.sem, irms_ready.at(g))
                dve.tensor_scalar(xn[:, :], n5.h[:, :], irms[:, :], float(D) ** 0.5, ALU.mult, ALU.mult).then_inc(xn_ready.sem, 1)

            def add_output(g):
                dve.wait_ge(y_done.sem, y_done.at(g))
                dve.tensor_tensor(x_of(g), pM[:, 1, :], x_of(g), ALU.add).then_inc(x_ready.sem, 1)

            def output_stats(g):
                dve.wait_ge(x_ready.sem, x_ready.at(g))
                carry(dve, ctx)
                n6.vector_stats(dve, x_of(g), g)

            def add_normed(g):
                dve.wait_ge(n6.h_ready.sem, n6.h_ready.at(g))
                dve.tensor_tensor(x_of(g), x_of(g), n6.h[:, :], ALU.add).then_inc(xh_ready.sem, 1)

            def keep_logits(g):
                dve.wait_ge(lg_done.sem, lg_done.at(g))
                dve.tensor_copy(LG[:, bass.ds(g, 1), :].rearrange("p g e -> p (g e)"), pM[:, 3, 0:E]).then_inc(lg_ready.sem, 1)

            def slot(g, first, last, norm):
                dve.wait_ge(s_done.sem, s_done.at(g))
                dve.tensor_reduce(smax[:, :], pS[:, :, :], AX.X, ALU.max).then_inc(max_ready.sem, 1)
                if norm:
                    n5.vector_stats(dve, x_of(g + 2), g + 2)
                dve.wait_ge(max_ready.sem, max_ready.at(g))
                dve.tensor_tensor(sd[:, :, :], pS[:, :, :], smax[:, :].unsqueeze(2).broadcast_to([P, H, T]), ALU.subtract
                                  ).then_inc(sd_ready.sem, 1)
                if not first:
                    add_output(g - 1)
                dve.wait_ge(se_ready.sem, se_ready.at(g))
                dve.tensor_reduce(ssum[:, :], se[:, :, :], AX.X, ALU.add).then_inc(sum_ready.sem, 1)
                if not first:
                    output_stats(g - 1)
                dve.wait_ge(sum_ready.sem, sum_ready.at(g))
                dve.reciprocal(sinv[:, :], ssum[:, :]).then_inc(sinv_ready.sem, 1)
                if norm:
                    squares(g + 2)
                dve.wait_ge(sinv_ready.sem, sinv_ready.at(g))
                dve.tensor_tensor(sn[:, :, :], se[:, :, :], sinv[:, :].unsqueeze(2).broadcast_to([P, H, T]), ALU.mult
                                  ).then_inc(sn_ready.sem, 1)
                if not first:
                    n6.vector_scale(dve, x_of(g - 1), g - 1)
                dve.wait_ge(sn_ready.sem, sn_ready.at(g))
                for b in range(BG):
                    r = slice(b * T, (b + 1) * T)
                    ins = dve.transpose(pt[r, :, b * T:(b + 1) * T], sn[r, :, :])
                ins.then_inc(pt_ready.sem, 1)
                if norm:
                    bound(g + 2)
                if not first:
                    add_normed(g - 1)
                if norm:
                    inverse(g + 2)
                if not first:
                    keep_logits(g - 1)
                if norm:
                    scaled(g + 2)

            for g in range(2):
                n5.vector_stats(dve, x_of(g), g)
                squares(g)
                bound(g)
                inverse(g)
                if g > 0:
                    dve.wait_ge(hT_done.sem, hT_done.at(g - 1))
                scaled(g)
            slots(dve, slot)
            add_output(G - 1)
            output_stats(G - 1)
            n6.vector_scale(dve, x_of(G - 1), G - 1)
            add_normed(G - 1)
            keep_logits(G - 1)


def kernel(**inputs):
    import concourse.bacc as _bacc
    from concourse.bass_utils import run_bass_kernel_spmd as _run

    a = {n: np.asarray(x) for n, x in inputs.items()}
    c = np.ascontiguousarray
    ctx = a["ctx_1024"]
    pair = np.arange(D).reshape(-1, 2)[:, ::-1].ravel()
    t = lambda m: m.T
    squares = {"wq0": t(a["L0_xattn_Wq"]), "wk0": a["L0_xattn_Wk"], "wv0": t(a["L0_xattn_Wv"]), "wo0": t(a["L0_xattn_Wo"]),
               "aq": t(a["L0_attn_W_Q"]), "aqr": t(a["L0_attn_W_Q"][pair]), "ak": t(a["L0_attn_W_K"]), "akr": t(a["L0_attn_W_K"][pair]),
               "av": t(a["L0_attn_W_V"]), "ao": t(a["L0_attn_W_O"]),
               "wq1": t(a["L1_xattn_Wq"]), "wk1": t(a["L1_xattn_Wk"]), "wv1": t(a["L1_xattn_Wv"]), "wo1": t(a["L1_xattn_Wo"])}
    vectors = [a["L0_xattn_bq"], a["L0_xattn_bk"], a["L0_xattn_bv"], a["L1_xattn_bq"], a["L1_xattn_bk"], a["L1_xattn_bv"], a["L1_attn_gamma"]]
    vectors += list(a["L0_ffn_b1"].reshape(-1, P)) + list(a["L1_ffn_b1"].reshape(-1, P))
    arrays = {
        "x": a["x"],
        "ctxR": ctx[:, :SM].reshape(G, BG, SC, P, D).transpose(0, 3, 2, 1, 4).reshape(G, P, SC * BG * D),
        "ctxT": ctx.reshape(G, BG, S, D).transpose(0, 3, 1, 2),
        "ctxL": ctx[:, SM],
        "wsq": np.stack([squares[n] for n in SQ], 1),
        "vec": np.stack(vectors, 1),
        "cst": constants(),
        "bo0": np.broadcast_to(a["L0_xattn_bo"], (P, D)),
        "bo1": np.broadcast_to(a["L1_xattn_bo"], (P, D)),
        "router": t(a["L0_ffn_router_w"]),
        "gate": a["L1_ffn_gate_W"],
        "f0_w1": a["L0_ffn_W1"].transpose(1, 0, 2),
        "f0_w2": a["L0_ffn_W2"].reshape(E, F0 // P, P, D).transpose(2, 0, 1, 3),
        "f0_b2": a["L0_ffn_b2"],
        "f1_w1": a["L1_ffn_W1"].transpose(1, 0, 2),
        "f1_w2": a["L1_ffn_W2"].reshape(E, F1 // P, P, D).transpose(2, 0, 1, 3),
        "f1_b2": a["L1_ffn_b2"],
        "wqkv": a["L1_attn_w_qkv"],
        "wout": a["L1_attn_w_out"].reshape(RP, P, D).transpose(1, 0, 2),
    }
    nc = _bacc.Bacc("TRN2", target_bir_lowering=False, num_devices=1)
    arrays = {f"in_{n}": c(x) for n, x in arrays.items()}
    io = {n[3:]: nc.dram_tensor(n, x.shape, mybir.dt.from_np(x.dtype), kind="ExternalInput").ap() for n, x in arrays.items()}
    io["out"] = nc.dram_tensor("out_dram", (B, T, D), F32, kind="ExternalOutput").ap()
    build_program(nc, io)
    r = _run(nc, [arrays], core_ids=[0])
    return r.results[0]["out_dram"]


def constants():
    p = np.arange(P)
    inv = 1.0 / np.float32(10000.0) ** (np.arange(0, HD, 2, dtype=np.float32) / HD)
    f = np.outer(inv, np.arange(T, dtype=np.float32)).astype(np.float32)
    angle = f[(p % HD) // 2]
    sign = np.where(p % 2 == 0, -1.0, 1.0)[:, None]
    parts = {
        "ident": np.eye(P),
        "rope": np.concatenate([np.cos(angle), sign * np.sin(angle)], 1),
        "quad": (p[:, None] // HD) % HQ == np.arange(HQ)[None],
        "vmask": (p[None] // HD) % HQ == p[:, None] // T,
        "batch": p[:, None] // T == np.arange(BG)[None],
        "qsel": p[:, None] % T == np.arange(T)[None],
        "row4": p[None] // T == p[:, None],
        "before": p[:, None] < p[None],
        "ones": np.ones((P, P)),
        "rank": np.broadcast_to(E - np.arange(E), (P, E)),
        "half": np.full((P, 1), -0.5),
        "root": np.full((P, 1), 0.5),
        "eps": np.full((P, 1), EPS),
    }
    return np.concatenate([np.asarray(parts[n], np.float32) for n in CONST], 1)
```

```python
from contextlib import ExitStack

import numpy as np

import concourse.bass as bass
from concourse import mybir

F32 = mybir.dt.float32
I32 = mybir.dt.int32
U32 = mybir.dt.uint32
F32R = mybir.dt.float32r
ALU = mybir.AluOpType
ACT = mybir.ActivationFunctionType
AX = mybir.AxisListType

B, T, D, S = 128, 32, 128, 257
P = 128
BG = P // T
G = B // BG
SC = S // P
SM = SC * P
SE = S + S % 2
TOP = 32
H = 16
HD = D // H
HQ = 4
NQ = H // HQ
RH = 64
RI = H * RH
RP = RI // P
E = 8
F0, F1 = 512, 256
CAP = 640
TG = 4
NB = G // TG
SLOTS = (E - 1) * CAP
NT = CAP // P
NO_SLOT = float(1 << 20)
EPS = 1e-5
NEG = -3.0e38
FIRST_PROB = 0x3E000000
PROB_BITS = 25
BITS = 5

SQ = ["wq0", "wk0", "wv0", "wo0", "aq", "aqr", "ak", "akr", "av", "ao", "wq1", "wk1", "wv1", "wo1"]
VEC = ["bq0", "bk0", "bv0", "bq1", "bk1", "bv1", "gamma"]
NVEC = len(VEC)
VB1_0 = NVEC
VB1_1 = VB1_0 + E * F0 // P
NV = VB1_1 + E * F1 // P
CONST = {"ident": 128, "rope": 64, "quad": 4, "vmask": 128, "batch": 4, "qsel": 32, "row4": 128,
         "before": 128, "ones": 128, "rank": 8, "slot": 8, "half": 1, "root": 1, "eps": 1}
COFF = {}
_o = 0
for _n, _w in CONST.items():
    COFF[_n] = _o
    _o += _w
NC = _o


class Phase(ExitStack):

    def __init__(self, nc, name):
        super().__init__()
        self.nc, self.semaphores = nc, []
        self.passed = self.semaphore(f"{name}_passed")
        self.callback(self.retire)

    def semaphore(self, name):
        self.semaphores.append(self.nc.alloc_semaphore(name))
        return self.semaphores[-1]

    def retire(self):
        self.nc.clear_and_free_semaphores(self.semaphores)
        self.nc.all_engine_barrier()


class Signal:

    def __init__(self, ctx, nc, name, per=1, credit=0):
        self.sem, self.per, self.credit = ctx.semaphore(name), per, credit

    def at(self, r, j=None):
        return r * self.per + (self.per if j is None else j) + self.credit


def carry(eng, phase):
    eng.sem_inc(phase.passed, 1)


def build_program(nc, io):
    ctx = ExitStack()
    with ctx:
        def sb(name, shape, dt=F32, c=ctx):
            return c.enter_context(nc.sbuf_tensor(name, shape, dt))

        X = sb("X", [P, G, D])
        LG = sb("LG", [P, G, E])
        MASK = sb("MASK", [P, G, E])
        wsq = sb("wsq", [P, len(SQ), P])
        vec = sb("vec", [P, NV])
        cst = sb("cst", [P, NC])
        bo0 = sb("bo0", [P, D])
        bo1 = sb("bo1", [P, D])
        layer0 = ctx.enter_context(ExitStack())
        ew = [(sb(f"{n}_w1", [P, E, f], c=c), sb(f"{n}_w2", [P, E, f // P, D], c=c)) for n, f, c in (("f1", F1, ctx), ("f0", F0, layer0))][::-1]
        HT_all = sb("HT_all", [P, G, P], c=layer0)
        H_all = sb("H_all", [P, G, D], c=layer0)
        slot_of = sb("slot_of", [P, G], U32, layer0)
        ew_loaded = [ctx.enter_context(nc.semaphore(f"{n}_w_loaded")) for n in ("f0", "f1")]
        rows_zeroed = ctx.enter_context(nc.semaphore("rows_zeroed"))
        rows_in = nc.dram_tensor("rows_in", (SLOTS, D), F32, kind="Internal").ap()
        rows_out = nc.dram_tensor("rows_out", (SLOTS, D), F32, kind="Internal").ap()
        loaded, rest_loaded = ctx.enter_context(nc.semaphore("loaded")), ctx.enter_context(nc.semaphore("rest_loaded"))

        def w(name):
            return wsq[:, SQ.index(name), :]

        def v(name):
            i = VEC.index(name)
            return vec[:, i:i + 1]

        def k(name):
            return cst[:, COFF[name]:COFF[name] + CONST[name]]

        env = dict(nc=nc, io=io, X=X, HT_all=HT_all, H_all=H_all, slot_of=slot_of,
                   rows_in=rows_in, rows_out=rows_out, ew=ew, ew_loaded=ew_loaded, rows_zeroed=rows_zeroed, rest_loaded=rest_loaded,
                   LG=LG, MASK=MASK, w=w, v=v, k=k, vec=vec, bo0=bo0, bo1=bo1)

        with nc.Block() as block:
            @block.sync
            def _(sp):
                x_in = io["x"].rearrange("(g bb) t d -> (bb t) g d", bb=BG)
                sp.dma_start(X[:, 0:2, :], x_in[:, 0:2, :]).then_inc(loaded, 16)
                sp.dma_start(cst[:, :], io["cst"]).then_inc(loaded, 16)
                sp.dma_start(vec[:, :], io["vec"]).then_inc(loaded, 16)
                sp.dma_start(wsq[:, :, :], io["wsq"]).then_inc(loaded, 16)
                sp.wait_ge(loaded, 4 * 16)

        attend_layer0(env)
        route_layer0(env)
        experts_layer0(env)
        layer0.close()
        cross_layer1(env)
        env["HT_parts"] = sb("HT_parts", [P, 2, G, P], F32R)
        self_layer1(env)
        gate_layer1(env)
        experts_layer1(env)


class Norm:

    def __init__(self, ctx, nc, name, env):
        self.env, self.ctx = env, ctx
        f = lambda n, s: ctx.enter_context(nc.sbuf_tensor(f"{name}_{n}", s, F32))
        self.stats, self.mv, self.ve, self.rstd = f("stats", [P, 6]), f("mv", [P, 2]), f("ve", [P, 1]), f("rstd", [P, 1])
        self.h = f("h", [P, D])
        self.stats_ready = Signal(ctx, nc, f"{name}_stats_ready")
        self.mv_ready = Signal(ctx, nc, f"{name}_mv_ready")
        self.ve_ready = Signal(ctx, nc, f"{name}_ve_ready")
        self.rstd_ready = Signal(ctx, nc, f"{name}_rstd_ready")
        self.h_ready = Signal(ctx, nc, f"{name}_h_ready")

    def vector_stats(self, dve, x, r):
        self.vector_rows(dve, x)
        self.vector_moments(dve, r)

    def vector_rows(self, dve, x):
        dve.bn_stats(self.stats[:, :], x).then_inc(self.stats_ready.sem, 1)

    def vector_moments(self, dve, r):
        dve.wait_ge(self.stats_ready.sem, self.stats_ready.at(r))
        carry(dve, self.ctx)
        dve.bn_aggr(self.mv[:, :], self.stats[:, :]).then_inc(self.mv_ready.sem, 1)

    def gpsimd(self, pool, r):
        pool.wait_ge(self.mv_ready.sem, self.mv_ready.at(r))
        pool.tensor_tensor(self.ve[:, :], self.mv[:, 1:2], self.env["k"]("eps"), ALU.add).then_inc(self.ve_ready.sem, 1)
        pool.wait_ge(self.ve_ready.sem, self.ve_ready.at(r))
        pool.tensor_tensor(self.rstd[:, :], self.ve[:, :], self.env["k"]("half"), ALU.pow).then_inc(self.rstd_ready.sem, 1)

    def vector_scale(self, dve, x, r, out=None):
        dve.wait_ge(self.rstd_ready.sem, self.rstd_ready.at(r))
        dve.tensor_scalar(self.h[:, :] if out is None else out, x, self.mv[:, 0:1], self.rstd[:, :], ALU.subtract, ALU.mult
                          ).then_inc(self.h_ready.sem, 1)


def attend_layer0(env):
    nc, io, X, HT_all, H_all, LG, w, v, k, bo0, bo1 = (env[n] for n in ("nc", "io", "X", "HT_all", "H_all", "LG", "w", "v", "k", "bo0", "bo1"))
    ctx = Phase(nc, "a")
    with ctx:
        def sb(name, shape, dt=F32):
            return ctx.enter_context(nc.sbuf_tensor("a_" + name, shape, dt))

        def ps(name, shape):
            return ctx.enter_context(nc.psum_tensor("a_" + name, shape, F32))

        def sig(name, per=1, credit=0):
            return Signal(ctx, nc, "a_" + name, per, credit)

        ctxN = sb("ctxN", [P, 2, SC, BG, D])
        ctxT = sb("ctxT", [P, 2, BG, S])
        ctxL = sb("ctxL", [BG, 2, D])
        wr = sb("router", [P, E])
        hT, q, q2, qb = sb("hT", [P, P]), sb("q", [P, P]), sb("q2", [P, P]), sb("qb", [P, 1])
        sc, work, top = sb("sc", [P, S]), sb("work", [P, S]), sb("top", [P, TOP])
        nmax, ex, pr, rsum, rinv = sb("nmax", [P, 1]), sb("ex", [P, S]), sb("pr", [P, S]), sb("rsum", [P, 1]), sb("rinv", [P, 1])
        prL, prT, prLT = sb("prL", [P, BG]), sb("prT", [P, SC, P]), sb("prLT", [BG, P])
        cu, uT, vT, yb = sb("u", [P, D]), sb("uT", [P, P]), sb("vT", [P, P]), sb("yb", [P, D])
        hT2, rot, qk = sb("hT2", [P, P]), sb("rot", [P, 2, 8, T]), sb("qk", [P, 2, P])
        kquad = sb("kquad", [P, BG, HQ, T])
        smax, sd, se, ssum, sinv = sb("smax", [P, H]), sb("sd", [P, H, T]), sb("se", [P, H, T]), sb("ssum", [P, H]), sb("sinv", [P, H])
        seT, vq, o, oT = sb("seT", [P, NQ, P]), sb("vq", [P, BG, D]), sb("o", [P, D]), sb("oT", [P, P])
        h3T = sb("h3T", [P, P])

        pX = ps("pX", [P, 4, P])
        pS = pX[:, :, :].rearrange("p a t -> p (a t)")[:, 0:S]
        pU = ps("pU", [P, 4, P])
        pB = ps("pB", [P, P])
        pQ = ps("pQ", [P, 4, 512])
        pO = ps("pO", [P, 4, P])

        zero = sb("zero", [P, NT * D])
        n1 = Norm(ctx, nc, "a_n1", env)
        n2 = Norm(ctx, nc, "a_n2", env)
        n3 = Norm(ctx, nc, "a_n3", env)
        router_loaded, zeroed = sig("router_loaded", 16), sig("zeroed")
        ctxT_loaded = [sig(f"ctxT_loaded{p}", 16) for p in range(2)]
        ctxN_loaded = [sig(f"ctxN_loaded{p}", 32) for p in range(2)]
        hT_done, hT_ready = sig("hT_done"), sig("hT_ready")
        q_done, q_ready = sig("q_done"), sig("q_ready")
        q2_done, q2_ready, qb_ready = sig("q2_done"), sig("q2_ready"), sig("qb_ready")
        s_done, s_ready = sig("s_done"), sig("s_ready")
        topk = sig("topk", 8)
        nmax_ready, e_ready = sig("nmax_ready"), sig("e_ready")
        p_ready, rinv_ready, pL_ready = sig("p_ready"), sig("rinv_ready"), sig("pL_ready")
        pT_done, pT_ready = sig("pT_done"), sig("pT_ready", 2)
        u_done, u_ready = sig("u_done"), sig("u_ready")
        uT_done, uT_ready = sig("uT_done"), sig("uT_ready")
        v_done, v_ready = sig("v_done"), sig("v_ready")
        y_done, yb_ready, x1_ready = sig("y_done"), sig("yb_ready"), sig("x1_ready")
        h2T_done, h2T_ready = sig("h2T_done"), sig("h2T_ready")
        qk_done, rot_ready, qk_ready, kq_ready = sig("qk_done"), sig("rot_ready"), sig("qk_ready"), sig("kq_ready")
        ss_done, smax_ready, sd_ready, se_ready = sig("ss_done"), sig("smax_ready"), sig("sd_ready"), sig("se_ready")
        ssum_ready, sinv_ready = sig("ssum_ready"), sig("sinv_ready")
        seT_done, seT_ready = sig("seT_done"), sig("seT_ready")
        vq_done, vq_ready = sig("vq_done"), sig("vq_ready")
        o_done, o_ready, oT_done, oT_ready = sig("o_done"), sig("o_ready"), sig("oT_done"), sig("oT_ready")
        y2_done, x2_ready = sig("y2_done"), sig("x2_ready")
        h3T_done, h3T_ready, h3T_kept = sig("h3T_done"), sig("h3T_ready"), sig("h3T_kept", credit=1)
        h3_kept = sig("h3_kept")
        lg_done, lg_ready = sig("lg_done"), sig("lg_ready")
        SCALE = float(D) ** -0.5
        SCALE2 = float(HD) ** -0.5
        ident = k("ident")

        def slots(eng, slot):
            def groups(s):
                return [g if 0 <= g < G else None for g in range(s + 1, s - 6, -1)]

            peeled = 5
            for s in range(peeled):
                slot(*groups(s), s % 2, s // 2)
            pairs = (G - 1 - peeled) // 2
            with eng.Fori(0, pairs) as i:
                for s in (peeled, peeled + 1):
                    slot(*(i * 2 + g for g in range(s + 1, s - 6, -1)), s % 2, i + s // 2)
            for s in range(peeled + 2 * pairs, G + 5):
                slot(*groups(s), s % 2, s // 2)

        def run(step, g):
            if g is not None:
                step(g)

        def later(g):
            return not (isinstance(g, int) and g == 0)

        block = ctx.enter_context(nc.Block())

        @block.sync
        def _(sp):
            sp.dma_start(wr[:, :], io["router"]).then_inc(router_loaded.sem, 16)

            def load_scored(g, p, wait=True):
                if wait:
                    sp.wait_ge(s_done.sem, s_done.at(g - 2))
                sp.dma_start(ctxT[:, p, :, :].unsqueeze(1), io["ctxT"][bass.ds(g, 1), :, :, :].rearrange("g p b s -> p g b s")
                             ).then_inc(ctxT_loaded[p].sem, 16)

            def load_summed(g, p, wait=True):
                if wait:
                    sp.wait_ge(u_done.sem, u_done.at(g - 2))
                sp.dma_start(ctxN[:, p, :, :, :].rearrange("p c b d -> p (c b d)").unsqueeze(1),
                             io["ctxR"][bass.ds(g, 1), :, :].rearrange("g p n -> p g n")).then_inc(ctxN_loaded[p].sem, 16)
                sp.dma_start(ctxL[:, p, :], io["ctxL"][bass.ds(g * BG, BG), :]).then_inc(ctxN_loaded[p].sem, 16)

            load_scored(0, 0, False)
            x_in = io["x"].rearrange("(g bb) t d -> (bb t) g d", bb=BG)
            sp.dma_start(bo0[:, :], io["bo0"]).then_inc(env["rest_loaded"], 16)
            sp.dma_start(bo1[:, :], io["bo1"]).then_inc(env["rest_loaded"], 16)
            for r in (slice(2, G // 2), slice(G // 2, G)):
                sp.dma_start(X[:, r, :], x_in[:, r, :]).then_inc(env["rest_loaded"], 16)
            load_scored(1, 1, False)
            for p in range(2):
                load_scored(2 + p, p)
                load_summed(p, p, False)

            def load_ahead(e):
                for (w1, w2), name, loaded in zip(env["ew"], ("f0", "f1"), env["ew_loaded"]):
                    sp.dma_start(w1[:, e, :], io[name + "_w1"][:, e, :]).then_inc(loaded, 16)
                    sp.dma_start(w2[:, e, :, :], io[name + "_w2"][:, e, :, :]).then_inc(loaded, 16)
                if e > 0:
                    sp.dma_start(env["rows_in"][(e - 1) * CAP:e * CAP, :].rearrange("(k p) d -> p k d", p=P),
                                 zero[:, :].rearrange("p (k d) -> p k d", d=D)).then_inc(env["rows_zeroed"], 16)

            sp.wait_ge(zeroed.sem, 1)
            for e in range(E):
                for p in range(2):
                    load_scored(2 * e + 4 + p, p)
                    load_summed(2 * e + 2 + p, p)
                load_ahead(e)
            with sp.Fori(1 + E, G // 2 - 1) as i:
                for p in range(2):
                    load_scored(i * 2 + 2 + p, p)
                    load_summed(i * 2 + p, p)
            for p in range(2):
                load_summed(G - 2 + p, p)

        @block.tensor
        def _(pe):
            pe.wait_ge(router_loaded.sem, 16)

            def turn(out, in_):
                return pe.transpose(out, in_, ident)

            def turn_x(x):
                pe.wait_ge(n1.h_ready.sem, n1.h_ready.at(x))
                if later(x):
                    pe.wait_ge(s_ready.sem, s_ready.at(x - 1))
                turn(pX[:, 0, :], n1.h[:, :]).then_inc(hT_done.sem, 1)

            def queries(x):
                pe.wait_ge(hT_ready.sem, hT_ready.at(x))
                pe.matmul(pX[:, 1, :], w("wq0"), hT[:, :], start=True, stop=True).then_inc(q_done.sem, 1)

            def queries_by_keys(x):
                pe.wait_ge(q_ready.sem, q_ready.at(x))
                pe.matmul(pX[:, 2, :], w("wk0"), q[:, :], start=True, stop=True)
                pe.matmul(pX[:, 3, 0:1], q[:, :], v("bk0"), start=True, stop=True).then_inc(q2_done.sem, 1)

            def scores(x, p, r):
                pe.wait_ge(q2_ready.sem, q2_ready.at(x))
                pe.wait_ge(ctxT_loaded[p].sem, ctxT_loaded[p].at(r))
                for b in range(BG):
                    mm = pe.matmul(pS[b * T:(b + 1) * T, :], q2[:, b * T:(b + 1) * T], ctxT[:, p, b, :],
                                   start=True, stop=True)
                mm.then_inc(s_done.sem, 1)

            def turn_weights(u):
                pe.wait_ge(pL_ready.sem, pL_ready.at(u))
                for c in range(SC):
                    turn(pU[:, c, :], pr[:, c * P:(c + 1) * P])
                turn(pU[0:BG, SC, :], prL[:, :]).then_inc(pT_done.sem, 1)

            def sums(u, p, r):
                pe.wait_ge(pT_ready.sem, pT_ready.at(u))
                pe.wait_ge(ctxN_loaded[p].sem, ctxN_loaded[p].at(r - 1))
                for c in range(SC):
                    for b in range(BG):
                        pe.matmul(pU[b * T:(b + 1) * T, 3, :], prT[:, c, b * T:(b + 1) * T], ctxN[:, p, c, b, :],
                                  start=(c == 0), stop=False, skip_group_check=True)
                pe.matmul(pU[:, 3, :], prLT[:, :], ctxL[:, p, :], start=False, stop=True,
                          skip_group_check=True).then_inc(u_done.sem, 1)

            def turn_sums(u):
                pe.wait_ge(u_ready.sem, u_ready.at(u))
                turn(pU[:, 0, :], cu[:, :]).then_inc(uT_done.sem, 1)

            def sums_by_values(u):
                pe.wait_ge(uT_ready.sem, uT_ready.at(u))
                pe.matmul(pU[:, 1, :], w("wv0"), uT[:, :], start=True, stop=True).then_inc(v_done.sem, 1)

            def project(u):
                pe.wait_ge(v_ready.sem, v_ready.at(u))
                pe.matmul(pU[:, 2, :], vT[:, :], w("wo0"), start=True, stop=True).then_inc(y_done.sem, 1)

            def turn_a(a):
                pe.wait_ge(n2.h_ready.sem, n2.h_ready.at(a))
                turn(pB[:, :], n2.h[:, :]).then_inc(h2T_done.sem, 1)

            def self_queries_keys(a):
                pe.wait_ge(h2T_ready.sem, h2T_ready.at(a))
                for j, name in enumerate(("aq", "ak", "aqr", "akr")):
                    mm = pe.matmul(pQ[:, 0, j * P:(j + 1) * P], w(name), hT2[:, :], start=True, stop=True)
                mm.then_inc(qk_done.sem, 1)

            def self_values(a):
                for b in range(BG):
                    for h in range(HQ):
                        mm = pe.matmul(pQ[h * T:(h + 1) * T, 1, b * D:(b + 1) * D], hT2[:, b * T:(b + 1) * T], w("av"),
                                       start=True, stop=True)
                mm.then_inc(vq_done.sem, 1)

            def self_scores(a):
                pe.wait_ge(kq_ready.sem, kq_ready.at(a))
                pe.wait_ge(vq_ready.sem, vq_ready.at(a))
                carry(pe, ctx)
                for b in range(BG):
                    for c in range(NQ):
                        r_ = slice(c * T, (c + 1) * T)
                        mm = pe.matmul(pQ[b * T:(b + 1) * T, c, 0:P], qk[r_, 0, b * T:(b + 1) * T],
                                       kquad[r_, b, :, :], start=True, stop=True)
                mm.then_inc(ss_done.sem, 1)

            def turn_self_weights(z):
                pe.wait_ge(se_ready.sem, se_ready.at(z))
                if later(z):
                    pe.wait_ge(lg_ready.sem, lg_ready.at(z - 1))
                for c in range(NQ):
                    mm = turn(pO[:, c, :], se[:, c * HQ:(c + 1) * HQ, :])
                mm.then_inc(seT_done.sem, 1)

            def self_sums(z):
                pe.wait_ge(seT_ready.sem, seT_ready.at(z))
                for b in range(BG):
                    for c in range(NQ):
                        mm = pe.matmul(pO[b * T:(b + 1) * T, 0, c * T:(c + 1) * T], seT[:, c, b * T:(b + 1) * T],
                                       vq[:, b, c * T:(c + 1) * T], start=True, stop=True)
                mm.then_inc(o_done.sem, 1)

            def turn_self_sums(z):
                pe.wait_ge(o_ready.sem, o_ready.at(z))
                turn(pO[:, 1, :], o[:, :]).then_inc(oT_done.sem, 1)

            def self_project(z):
                pe.wait_ge(oT_ready.sem, oT_ready.at(z))
                pe.matmul(pO[:, 2, :], oT[:, :], w("ao"), start=True, stop=True).then_inc(y2_done.sem, 1)

            def turn_z(z):
                pe.wait_ge(n3.h_ready.sem, n3.h_ready.at(z))
                turn(pO[:, 3, :], n3.h[:, :]).then_inc(h3T_done.sem, 1)

            def logits(z):
                pe.wait_ge(h3T_ready.sem, h3T_ready.at(z))
                pe.matmul(pO[:, 0, 0:E], h3T[:, :], wr[:, :], start=True, stop=True).then_inc(lg_done.sem, 1)

            def slot(w_, x, t, u, a, z, l, p, r):
                run(logits, l)
                run(turn_x, x)
                run(turn_a, a)
                run(turn_self_weights, z)
                run(turn_weights, u)
                run(self_queries_keys, a)
                run(lambda u: sums(u, p, r), u)
                run(self_sums, z)
                run(turn_sums, u)
                run(self_values, a)
                run(turn_self_sums, z)
                run(sums_by_values, u)
                run(queries, x)
                run(self_project, z)
                run(project, u)
                run(queries_by_keys, x)
                run(self_scores, a)
                run(lambda x: scores(x, p, r), x)
                run(turn_z, z)

            slots(pe, slot)

        @block.scalar
        def _(act):
            def normed_x(x):
                act.wait_ge(hT_done.sem, hT_done.at(x))
                act.activation(hT[:, :], pX[:, 0, :], ACT.Copy).then_inc(hT_ready.sem, 1)

            def queries(x):
                act.wait_ge(q_done.sem, q_done.at(x))
                act.activation(q[:, :], pX[:, 1, :], ACT.Identity, bias=v("bq0")).then_inc(q_ready.sem, 1)

            def queries_by_keys(x):
                act.wait_ge(q2_done.sem, q2_done.at(x))
                act.activation(qb[:, :], pX[:, 3, 0:1], ACT.Copy).then_inc(qb_ready.sem, 1)
                act.activation(q2[:, :], pX[:, 2, :], ACT.Copy).then_inc(q2_ready.sem, 1)

            def scores(x):
                act.wait_ge(s_done.sem, s_done.at(x))
                act.wait_ge(qb_ready.sem, qb_ready.at(x))
                if later(x):
                    act.wait_ge(topk.sem, topk.at(x - 1, 2))
                act.activation(sc[:, :], pS, ACT.Identity, bias=qb[:, :]).then_inc(s_ready.sem, 1)

            def exponentials(t):
                act.wait_ge(nmax_ready.sem, nmax_ready.at(t))
                act.activation(ex[:, :], sc[:, :], ACT.Exp, bias=nmax[:, :], scale=SCALE).then_inc(e_ready.sem, 1)

            def turned_weights(u):
                act.wait_ge(pT_done.sem, pT_done.at(u))
                act.activation(prT[:, :, :], pU[:, 0:SC, :], ACT.Copy).then_inc(pT_ready.sem, 1)
                act.activation(prLT[:, :], pU[0:BG, SC, :], ACT.Copy).then_inc(pT_ready.sem, 1)

            def sums(u):
                act.wait_ge(rinv_ready.sem, rinv_ready.at(u))
                act.wait_ge(u_done.sem, u_done.at(u))
                act.activation(cu[:, :], pU[:, 3, :], ACT.Copy, scale=rinv[:, :]).then_inc(u_ready.sem, 1)

            def turned_sums(u):
                act.wait_ge(uT_done.sem, uT_done.at(u))
                act.activation(uT[:, :], pU[:, 0, :], ACT.Copy).then_inc(uT_ready.sem, 1)

            def sums_by_values(u):
                act.wait_ge(v_done.sem, v_done.at(u))
                act.activation(vT[:, :], pU[:, 1, :], ACT.Identity, bias=v("bv0")).then_inc(v_ready.sem, 1)

            def normed_a(a):
                act.wait_ge(h2T_done.sem, h2T_done.at(a))
                act.activation(hT2[:, :], pB[:, :], ACT.Copy).then_inc(h2T_ready.sem, 1)

            def self_exponentials(a):
                act.wait_ge(sd_ready.sem, sd_ready.at(a))
                act.activation(se[:, :, :], sd[:, :, :], ACT.Exp, scale=SCALE2).then_inc(se_ready.sem, 1)

            def turned_self_weights(z):
                act.wait_ge(seT_done.sem, seT_done.at(z))
                act.activation(seT[:, :, :], pO[:, :, :], ACT.Copy).then_inc(seT_ready.sem, 1)

            def turned_self_sums(z):
                act.wait_ge(oT_done.sem, oT_done.at(z))
                act.activation(oT[:, :], pO[:, 1, :], ACT.Copy).then_inc(oT_ready.sem, 1)

            def normed_z(z):
                act.wait_ge(h3T_done.sem, h3T_done.at(z))
                act.wait_ge(h3T_kept.sem, h3T_kept.at(z, 0))
                act.activation(h3T[:, :], pO[:, 3, :], ACT.Copy).then_inc(h3T_ready.sem, 1)

            def slot(w_, x, t, u, a, z, l, p, r):
                run(normed_a, a)
                run(turned_weights, u)
                run(turned_self_weights, z)
                run(normed_x, x)
                run(sums, u)
                run(turned_sums, u)
                run(turned_self_sums, z)
                run(sums_by_values, u)
                run(queries, x)
                run(exponentials, t)
                run(queries_by_keys, x)
                run(scores, x)
                run(normed_z, z)
                run(self_exponentials, a)

            slots(act, slot)

        @block.gpsimd
        def _(pool):
            pool.sem_inc(h3T_kept.sem, h3T_kept.credit)
            n1.gpsimd(pool, 0)
            pool.memset(zero[:, :], 0.0).then_inc(zeroed.sem, 1)

            def spread_keys(a):
                pool.wait_ge(qk_ready.sem, qk_ready.at(a))
                pool.tensor_tensor(kquad[:, :, :, :],
                                   qk[:, 1, :].rearrange("p (b s) -> p b s", b=BG).unsqueeze(2).broadcast_to([P, BG, HQ, T]),
                                   k("quad").unsqueeze(1).unsqueeze(3).broadcast_to([P, BG, HQ, T]), ALU.mult
                                   ).then_inc(kq_ready.sem, 1)

            def keep(z):
                pool.wait_ge(n3.h_ready.sem, n3.h_ready.at(z))
                pool.tensor_copy(H_all[:, bass.ds(z, 1), :].rearrange("p g d -> p (g d)"), n3.h[:, :]).then_inc(h3_kept.sem, 1)
                pool.wait_ge(h3T_ready.sem, h3T_ready.at(z))
                pool.tensor_copy(HT_all[:, bass.ds(z, 1), :].rearrange("p g t -> p (g t)"), h3T[:, :]).then_inc(h3T_kept.sem, 1)

            def slot(w_, x, t, u, a, z, l, p, r):
                run(lambda g: n1.gpsimd(pool, g), w_)
                run(spread_keys, a)
                run(lambda g: n3.gpsimd(pool, g), z)
                run(lambda g: n2.gpsimd(pool, g), u)
                run(keep, z)

            slots(pool, slot)

        @block.vector
        def _(dve):
            def x_of(g):
                return X[:, bass.ds(g, 1), :].rearrange("p g d -> p (g d)")

            def scale_w(w_):
                if later(w_):
                    dve.wait_ge(hT_done.sem, hT_done.at(w_ - 1))
                n1.vector_scale(dve, x_of(w_), w_)

            def largest(i):
                def step(t):
                    if i == 0:
                        dve.wait_ge(s_ready.sem, s_ready.at(t))
                    else:
                        dve.wait_ge(topk.sem, topk.at(t, 2 * i))
                    carry(dve, ctx)
                    dve.max(top[:, i * 8:i * 8 + 8], (work if i else sc)[:, :]).then_inc(topk.sem, 1)
                return step

            def mark(i):
                def step(t):
                    dve.wait_ge(topk.sem, topk.at(t, 2 * i + 1))
                    carry(dve, ctx)
                    dve.match_replace(work[:, :], top[:, i * 8:i * 8 + 8], (work if i else sc)[:, :], NEG).then_inc(topk.sem, 1)
                return step

            def negated_max(t):
                dve.wait_ge(topk.sem, topk.at(t, 1))
                dve.tensor_scalar(nmax[:, :], top[:, 0:1], -SCALE, None, ALU.mult).then_inc(nmax_ready.sem, 1)

            def weights(u):
                dve.wait_ge(topk.sem, topk.at(u))
                dve.wait_ge(e_ready.sem, e_ready.at(u))
                dve.scalar_tensor_tensor(pr[:, :], work[:, :], NEG, ex[:, :], ALU.is_equal, ALU.mult,
                                         accum_out=rsum[:, :]).then_inc(p_ready.sem, 1)

            def last_weights(u):
                dve.wait_ge(p_ready.sem, p_ready.at(u))
                dve.tensor_scalar(prL[:, :], k("batch"), pr[:, SM:S], None, ALU.mult).then_inc(pL_ready.sem, 1)

            def inverse_sum(u):
                dve.reciprocal(rinv[:, :], rsum[:, :]).then_inc(rinv_ready.sem, 1)

            def add_bias(u):
                dve.wait_ge(y_done.sem, y_done.at(u))
                dve.tensor_tensor(yb[:, :], pU[:, 2, :], bo0[:, :], ALU.add).then_inc(yb_ready.sem, 1)

            def add_output(u):
                dve.wait_ge(yb_ready.sem, yb_ready.at(u))
                dve.tensor_tensor(x_of(u), yb[:, :], x_of(u), ALU.add).then_inc(x1_ready.sem, 1)

            def rows_u(u):
                dve.wait_ge(x1_ready.sem, x1_ready.at(u))
                carry(dve, ctx)
                n2.vector_rows(dve, x_of(u))

            def rotate(a):
                dve.wait_ge(qk_done.sem, qk_done.at(a))
                dve.tensor_tensor(rot[:, :, :, :], pQ[:, 0, :].rearrange("p (c n t) -> p c n t", c=2, t=T),
                                  k("rope").rearrange("p (c t) -> p c t", c=2).unsqueeze(2).broadcast_to([P, 2, 8, T]),
                                  ALU.mult).then_inc(rot_ready.sem, 1)

            def rotated(a):
                dve.wait_ge(rot_ready.sem, rot_ready.at(a))
                dve.tensor_tensor(qk[:, :, :].rearrange("p a t -> p (a t)"), rot[:, 0, :, :].rearrange("p n t -> p (n t)"),
                                  rot[:, 1, :, :].rearrange("p n t -> p (n t)"), ALU.add).then_inc(qk_ready.sem, 1)

            def self_values(a):
                dve.wait_ge(vq_done.sem, vq_done.at(a))
                dve.tensor_tensor(vq[:, :, :], pQ[:, 1, :].rearrange("p (b d) -> p b d", b=BG),
                                  k("vmask").unsqueeze(1).broadcast_to([P, BG, D]), ALU.mult).then_inc(vq_ready.sem, 1)

            s4 = pQ[:, :, 0:P].rearrange("p c (h s) -> p c h s", h=HQ)

            def self_maxima(a):
                dve.wait_ge(ss_done.sem, ss_done.at(a))
                dve.tensor_reduce(smax[:, :], s4, AX.X, ALU.max).then_inc(smax_ready.sem, 1)

            def self_below_max(a):
                dve.wait_ge(smax_ready.sem, smax_ready.at(a))
                dve.tensor_tensor(sd[:, :, :].rearrange("p (c h) s -> p c h s", c=NQ), s4,
                                  smax[:, :].rearrange("p (c h) -> p c h", c=NQ).unsqueeze(3).broadcast_to([P, NQ, HQ, T]),
                                  ALU.subtract).then_inc(sd_ready.sem, 1)

            def self_weight_sums(z):
                dve.wait_ge(se_ready.sem, se_ready.at(z))
                dve.tensor_reduce(ssum[:, :], se[:, :, :], AX.X, ALU.add).then_inc(ssum_ready.sem, 1)

            def self_inverse_sums(z):
                dve.wait_ge(ssum_ready.sem, ssum_ready.at(z))
                dve.reciprocal(sinv[:, :], ssum[:, :]).then_inc(sinv_ready.sem, 1)

            def self_sums(z):
                dve.wait_ge(sinv_ready.sem, sinv_ready.at(z))
                dve.wait_ge(o_done.sem, o_done.at(z))
                dve.tensor_tensor(o[:, :].rearrange("p (h d) -> p h d", h=H), pO[:, 0, :].rearrange("p (h d) -> p h d", h=H),
                                  sinv[:, :].unsqueeze(2).broadcast_to([P, H, HD]), ALU.mult).then_inc(o_ready.sem, 1)

            def add_self_output(z):
                dve.wait_ge(y2_done.sem, y2_done.at(z))
                dve.tensor_tensor(x_of(z), pO[:, 2, :], x_of(z), ALU.add).then_inc(x2_ready.sem, 1)

            def rows_z(z):
                dve.wait_ge(x2_ready.sem, x2_ready.at(z))
                carry(dve, ctx)
                n3.vector_rows(dve, x_of(z))

            def scale_z(z):
                if later(z):
                    dve.wait_ge(h3_kept.sem, h3_kept.at(z - 1))
                n3.vector_scale(dve, x_of(z), z)

            def keep_logits(z):
                dve.wait_ge(lg_done.sem, lg_done.at(z))
                dve.tensor_copy(LG[:, bass.ds(z, 1), :].rearrange("p g e -> p (g e)"), pO[:, 0, 0:E]).then_inc(lg_ready.sem, 1)

            def slot(w_, x, t, u, a, z, l, p, r):
                if isinstance(x, int) and x == 1:
                    dve.wait_ge(env["rest_loaded"], 4 * 16)
                run(weights, u)
                run(keep_logits, l)
                run(largest(0), t)
                run(last_weights, u)
                run(inverse_sum, u)
                run(mark(0), t)
                run(self_weight_sums, z)
                run(largest(1), t)
                run(lambda g: n1.vector_rows(dve, x_of(g)), w_)
                run(mark(1), t)
                run(self_inverse_sums, z)
                run(rotate, a)
                run(largest(2), t)
                run(self_sums, z)
                run(lambda g: n1.vector_moments(dve, g), w_)
                run(mark(2), t)
                run(rotated, a)
                run(largest(3), t)
                run(self_values, a)
                run(scale_w, w_)
                run(add_self_output, z)
                run(add_bias, u)
                run(rows_z, z)
                run(add_output, u)
                run(negated_max, t)
                run(lambda g: n3.vector_moments(dve, g), z)
                run(rows_u, u)
                run(mark(3), t)
                run(lambda g: n2.vector_moments(dve, g), u)
                run(self_maxima, a)
                run(scale_z, z)
                run(self_below_max, a)
                run(lambda g: n2.vector_scale(dve, x_of(g), g), u)

            n1.vector_stats(dve, X[:, 0, :], 0)
            scale_w(0)
            slots(dve, slot)


def route_layer0(env):
    nc, LG, MASK, slot_of, k = (env[n] for n in ("nc", "LG", "MASK", "slot_of", "k"))
    ctx = Phase(nc, "r")
    with ctx:
        def sb(name, shape, dt=F32):
            return ctx.enter_context(nc.sbuf_tensor("r_" + name, shape, dt))

        def sig(name, per=1, credit=0):
            return Signal(ctx, nc, "r_" + name, per, credit)

        lmax, d, e8, sm, prob = sb("lmax", [P, G]), sb("d", [P, G, E]), sb("e8", [P, G, E]), sb("sum", [P, G]), sb("prob", [P, G])
        eq, first, hot = sb("eq", [P, G, E]), sb("first", [P, G]), sb("hot", [P, G, E])
        pm, hit = sb("pm", [P, G, E]), sb("hit", [P, G, E])
        least, cand, bit, count, kept = (sb("least", [P, E], I32), sb("cand", [P, E], I32), sb("bit", [P, 1], I32),
                                         sb("count", [P, E]), sb("kept", [P, E]))
        over, same, need, scan, rank, fit = (sb("over", [P, G, E]), sb("same", [P, G, E]), sb("need", [P, E]),
                                             sb("scan", [P, E, G]), sb("rank", [P, G, E]), sb("fit", [P, G, E]))
        held, slot = sb("held", [P, G]), sb("slot", [P, G])
        pC = ctx.enter_context(nc.psum_tensor("r_pC", [P, 512], F32))
        pB = ctx.enter_context(nc.psum_tensor("r_pB", [P, 512], F32))
        d_ready, e_ready = sig("d_ready"), sig("e_ready")
        step = sig("step", 1)
        found = sig("found", 5 * BITS)
        count_ready, total_ready = sig("count_ready", BITS), sig("total_ready", BITS)
        over_ready, over_total = sig("over_ready"), sig("over_total")
        same_ready, same_total = sig("same_ready"), sig("same_total")
        mask_ready, mask_total = sig("mask_ready"), sig("mask_total")
        block = ctx.enter_context(nc.Block())

        def per_group(t):
            return t[:, :].unsqueeze(2).broadcast_to([P, G, E])

        def per_expert(t):
            return t.unsqueeze(1).broadcast_to([P, G, E])

        @block.scalar
        def _(act):
            act.wait_ge(d_ready.sem, 1)
            act.activation(e8[:, :, :], d[:, :, :], ACT.Exp).then_inc(e_ready.sem, 1)

        @block.tensor
        def _(pe):
            with pe.Fori(0, PROB_BITS // BITS) as n:
                for b in range(BITS):
                    pe.wait_ge(count_ready.sem, count_ready.at(n, b + 1))
                    pe.matmul(pC[:, 0:E], k("ones"), count[:, :], start=True, stop=True).then_inc(total_ready.sem, 1)
            pe.wait_ge(over_ready.sem, 1)
            pe.matmul(pC[:, 0:E], k("ones"), count[:, :], start=True, stop=True).then_inc(over_total.sem, 1)
            pe.wait_ge(same_ready.sem, 1)
            pe.matmul(pB[:, 0:G * E], k("ones"), same[:, :, :], start=True, stop=True)
            pe.matmul(pB[:, G * E:2 * G * E], k("before"), same[:, :, :], start=True, stop=True).then_inc(same_total.sem, 1)
            pe.wait_ge(mask_ready.sem, 1)
            pe.matmul(pB[:, 0:G * E], k("ones"), MASK[:, :, :], start=True, stop=True)
            pe.matmul(pB[:, G * E:2 * G * E], k("before"), MASK[:, :, :], start=True, stop=True).then_inc(mask_total.sem, 1)

        @block.vector
        def _(dve):
            done = [0]

            def then(ins):
                done[0] += 1
                ins.then_inc(step.sem, 1)
                dve.wait_ge(step.sem, done[0])

            then(dve.tensor_reduce(lmax[:, :], LG[:, :, :], AX.X, ALU.max))
            dve.tensor_tensor(d[:, :, :], LG[:, :, :], per_group(lmax), ALU.subtract).then_inc(d_ready.sem, 1)
            then(dve.tensor_tensor(eq[:, :, :], LG[:, :, :], per_group(lmax), ALU.is_equal))
            then(dve.tensor_tensor(eq[:, :, :], eq[:, :, :], per_expert(k("rank")), ALU.mult))
            then(dve.tensor_reduce(first[:, :], eq[:, :, :], AX.X, ALU.max))
            then(dve.tensor_tensor(hot[:, :, :], eq[:, :, :], per_group(first), ALU.is_equal))
            dve.wait_ge(e_ready.sem, 1)
            then(dve.tensor_reduce(sm[:, :], e8[:, :, :], AX.X, ALU.add))
            then(dve.reciprocal(prob[:, :], sm[:, :]))
            then(dve.tensor_tensor(pm[:, :, :], hot[:, :, :], per_group(prob), ALU.mult))
            then(dve.memset(least[:, :], FIRST_PROB))
            then(dve.memset(bit[:, :], 1 << (PROB_BITS - 1)))
            with dve.Fori(0, PROB_BITS // BITS) as n:
                for b in range(BITS):
                    def then_bit(ins, at):
                        ins.then_inc(found.sem, 1)
                        dve.wait_ge(found.sem, found.at(n, b * 5 + at))

                    then_bit(dve.tensor_tensor(cand[:, :], least[:, :], bit[:, 0:1].broadcast_to([P, E]), ALU.bitwise_or), 1)
                    then_bit(dve.tensor_tensor(hit[:, :, :], pm[:, :, :], per_expert(cand[:, :].bitcast(F32)), ALU.is_ge), 2)
                    dve.tensor_reduce(count[:, :], hit[:, :, :].rearrange("p g e -> p e g"), AX.X, ALU.add).then_inc(count_ready.sem, 1)
                    then_bit(dve.tensor_single_scalar(bit[:, :], bit[:, :], 1, ALU.logical_shift_right), 3)
                    dve.wait_ge(total_ready.sem, total_ready.at(n, b + 1))
                    then_bit(dve.scalar_tensor_tensor(kept[:, :], pC[:, 0:E], float(CAP), cand[:, :].bitcast(F32), ALU.is_ge, ALU.mult), 4)
                    then_bit(dve.tensor_tensor(least[:, :].bitcast(F32), least[:, :].bitcast(F32), kept[:, :], ALU.max), 5)
            then(dve.tensor_tensor(over[:, :, :], pm[:, :, :], per_expert(least[:, :].bitcast(F32)), ALU.is_gt))
            dve.tensor_reduce(count[:, :], over[:, :, :].rearrange("p g e -> p e g"), AX.X, ALU.add).then_inc(over_ready.sem, 1)
            dve.tensor_tensor(same[:, :, :], pm[:, :, :], per_expert(least[:, :].bitcast(F32)), ALU.is_equal).then_inc(same_ready.sem, 1)
            dve.wait_ge(over_total.sem, 1)
            then(dve.tensor_scalar(need[:, :], pC[:, 0:E], -1.0, float(CAP), ALU.mult, ALU.add))
            totals = pB[:, 0:G * E].rearrange("p (g e) -> p g e", e=E)

            def rank_from_totals():
                for e in range(E):
                    last = dve.tensor_tensor_scan(scan[:, e, :], k("ones")[:, 0:G], totals[:, :, e], 0.0, ALU.mult, ALU.add)
                    if e < E - 1:
                        last.then_inc(step.sem, 1)
                        done[0] += 1
                then(last)
                then(dve.tensor_tensor(rank[:, :, :], scan[:, :, :].rearrange("p e g -> p g e"), totals, ALU.subtract))
                then(dve.tensor_tensor(rank[:, :, :], rank[:, :, :], pB[:, G * E:2 * G * E].rearrange("p (g e) -> p g e", e=E), ALU.add))

            dve.wait_ge(same_total.sem, 1)
            rank_from_totals()
            then(dve.tensor_tensor(fit[:, :, :], rank[:, :, :], per_expert(need[:, :]), ALU.is_lt))
            then(dve.tensor_tensor(fit[:, :, :], fit[:, :, :], same[:, :, :], ALU.mult))
            then(dve.tensor_tensor(MASK[:, :, :], over[:, :, :], fit[:, :, :], ALU.add))
            then(dve.tensor_reduce(held[:, :], MASK[:, :, 1:E], AX.X, ALU.add))
            dve.tensor_scalar(MASK[:, :, 0], held[:, :], -1.0, 1.0, ALU.mult, ALU.add).then_inc(mask_ready.sem, 1)
            dve.wait_ge(mask_total.sem, 1)
            rank_from_totals()
            then(dve.tensor_tensor(rank[:, :, :], rank[:, :, :], per_expert(k("slot")), ALU.add))
            then(dve.tensor_tensor(rank[:, :, :], rank[:, :, :], MASK[:, :, :], ALU.mult))
            then(dve.tensor_reduce(slot[:, :], rank[:, :, :], AX.X, ALU.add))
            then(dve.tensor_copy(slot_of[:, :], slot[:, :]))


def gate_layer1(env):
    nc, LG, MASK, k = (env[n] for n in ("nc", "LG", "MASK", "k"))
    ctx = Phase(nc, "t")
    with ctx:
        def sb(name, shape, dt=F32):
            return ctx.enter_context(nc.sbuf_tensor("t_" + name, shape, dt))

        def sig(name, per=1, credit=0):
            return Signal(ctx, nc, "t_" + name, per, credit)

        lmax, d, gates, sm, inv = sb("lmax", [P, G]), sb("d", [P, G, E]), sb("gates", [P, G, E]), sb("sum", [P, G]), sb("inv", [P, G])
        eq, first, hot, rest = sb("eq", [P, G, E]), sb("first", [P, G]), [sb("hot0", [P, G, E]), sb("hot1", [P, G, E])], sb("rest", [P, G, E])
        best = [sb("best0", [P, G]), sb("best1", [P, G])]
        d_ready, e_ready, step = sig("d_ready"), sig("e_ready"), sig("step")
        block = ctx.enter_context(nc.Block())

        def per_group(t):
            return t[:, :].unsqueeze(2).broadcast_to([P, G, E])

        @block.scalar
        def _(act):
            act.wait_ge(d_ready.sem, 1)
            act.activation(gates[:, :, :], d[:, :, :], ACT.Exp).then_inc(e_ready.sem, 1)

        @block.vector
        def _(dve):
            done = [0]

            def then(ins):
                done[0] += 1
                ins.then_inc(step.sem, 1)
                dve.wait_ge(step.sem, done[0])

            then(dve.tensor_reduce(lmax[:, :], LG[:, :, :], AX.X, ALU.max))
            dve.tensor_tensor(d[:, :, :], LG[:, :, :], per_group(lmax), ALU.subtract).then_inc(d_ready.sem, 1)
            dve.wait_ge(e_ready.sem, 1)
            then(dve.tensor_reduce(sm[:, :], gates[:, :, :], AX.X, ALU.add))
            then(dve.reciprocal(inv[:, :], sm[:, :]))
            then(dve.tensor_tensor(gates[:, :, :], gates[:, :, :], per_group(inv), ALU.mult))
            for n in range(2):
                src = gates if n == 0 else rest
                then(dve.tensor_reduce(best[n][:, :], src[:, :, :], AX.X, ALU.max))
                then(dve.tensor_tensor(eq[:, :, :], src[:, :, :], per_group(best[n]), ALU.is_equal))
                then(dve.tensor_tensor(eq[:, :, :], eq[:, :, :], k("rank").unsqueeze(1).broadcast_to([P, G, E]), ALU.mult))
                then(dve.tensor_reduce(first[:, :], eq[:, :, :], AX.X, ALU.max))
                then(dve.tensor_tensor(hot[n][:, :, :], eq[:, :, :], per_group(first), ALU.is_equal))
                if n == 0:
                    then(dve.scalar_tensor_tensor(rest[:, :, :], hot[0][:, :, :], -2.0, gates[:, :, :], ALU.mult, ALU.add))
            then(dve.tensor_tensor(sm[:, :], best[0][:, :], best[1][:, :], ALU.add))
            then(dve.tensor_scalar(sm[:, :], sm[:, :], 1e-8, None, ALU.add))
            then(dve.reciprocal(inv[:, :], sm[:, :]))
            then(dve.tensor_tensor(hot[0][:, :, :], hot[0][:, :, :], hot[1][:, :, :], ALU.add))
            then(dve.tensor_tensor(gates[:, :, :], gates[:, :, :], hot[0][:, :, :], ALU.mult))
            then(dve.tensor_tensor(MASK[:, :, :], gates[:, :, :], per_group(inv), ALU.mult))


def experts_layer0(env):
    nc, io, X, HT_all, H_all, MASK, slot_of, k, vec = (env[n] for n in ("nc", "io", "X", "HT_all", "H_all", "MASK", "slot_of", "k", "vec"))
    rows_in, rows_out, (w1, w2) = env["rows_in"], env["rows_out"], env["ew"][0]
    NF = F0 // P
    ctx = Phase(nc, "f0")
    with ctx:
        def sb(n, shape, dt=F32):
            return ctx.enter_context(nc.sbuf_tensor(f"f0_{n}", shape, dt))

        def ps(n, shape):
            return ctx.enter_context(nc.psum_tensor(f"f0_{n}", shape, F32))

        N, HALF = TG * P, CAP // 2
        b2 = sb("b2", [P, E, D])
        hid = sb("hid", [P, 2, NF, CAP])
        bias = sb("bias", [P, G, D])
        h, hT, y = sb("h", [P, 2, NT, D]), sb("hT", [P, 2, CAP]), sb("y", [P, 2, NT, D])
        back = sb("back", [P, G, D])
        pT = ps("pT", [P, 2, 512])
        pH = ps("pH", [P, 4, 512])
        pY = ps("pY", [P, 2, 4, D])
        b2_loaded, scattered, gathered = (ctx.semaphore("f0_b2_loaded"), ctx.semaphore("f0_scattered"),
                                          [ctx.semaphore(f"f0_gathered{n}") for n in range(NB)])
        h_loaded = [ctx.semaphore(f"f0_h_loaded{p}") for p in range(2)]
        y_stored = [ctx.semaphore(f"f0_y_stored{p}") for p in range(2)]
        back_zeroed, bias_ready = ctx.semaphore("f0_back_zeroed"), ctx.semaphore("f0_bias_ready")
        up_done, up_ready = ctx.semaphore("f0_up_done"), ctx.semaphore("f0_up_ready")
        down_done, added = ctx.semaphore("f0_down_done"), ctx.semaphore("f0_added")
        hT_done, hT_ready = ctx.semaphore("f0_hT_done"), ctx.semaphore("f0_hT_ready")
        sorted_up_done, sorted_up_ready = ctx.semaphore("f0_sorted_up_done"), ctx.semaphore("f0_sorted_up_ready")
        y_done, y_ready = ctx.semaphore("f0_y_done"), ctx.semaphore("f0_y_ready")
        block = ctx.enter_context(nc.Block())

        def all_phases(dense, sorted_):
            dense(0, NB // 2)
            sorted_()
            dense(NB // 2, NB)

        def rows(t, e):
            return t[(e - 1) * CAP:e * CAP, :].rearrange("(k p) d -> p k d", p=P)

        @block.sync
        def _(sp):
            sp.dma_start(b2[:, :, :], io["f0_b2"]).then_inc(b2_loaded, 16)
            sp.wait_ge(scattered, 16 * G)
            for e in range(1, E + 2):
                if e < E:
                    if e > 2:
                        sp.wait_ge(hT_done, e - 2)
                    sp.dma_start(h[:, e % 2, :, :], rows(rows_in, e)).then_inc(h_loaded[e % 2], 16)
                if e > 2:
                    sp.wait_ge(y_ready, e - 2)
                    sp.dma_start(rows(rows_out, e - 2), y[:, e % 2, :, :]).then_inc(y_stored[e % 2], 16)

        @block.tensor
        def _(pe):
            pe.wait_ge(env["ew_loaded"][0], 32 * E)

            def up(n):
                for c in range(NF):
                    m = n * NF + c
                    if m >= 4:
                        pe.wait_ge(up_ready, m - 3)
                    pe.matmul(pH[:, m % 4, :], w1[:, 0, c * P:(c + 1) * P],
                              HT_all[:, n * TG:(n + 1) * TG, :].rearrange("p g t -> p (g t)"), start=True, stop=True).then_inc(up_done, 1)

            def down(n):
                pe.wait_ge(up_ready, (n + 1) * NF)
                if n > 1:
                    pe.wait_ge(added, (n - 1) * TG)
                for t in range(TG):
                    for c in range(NF):
                        mm = pe.matmul(pY[:, n % 2, t, :], hid[:, n % 2, c, t * P:(t + 1) * P], w2[:, 0, c, :],
                                       start=(c == 0), stop=(c == NF - 1))
                mm.then_inc(down_done, 1)

            def dense(first, end):
                up(first)
                for n in range(first, end):
                    if n + 1 < end:
                        up(n + 1)
                    down(n)

            def turn(e):
                pe.wait_ge(h_loaded[e % 2], 16 * ((e + 1) // 2))
                if e > 1:
                    pe.wait_ge(hT_ready, 2 * (e - 1))
                for t in range(NT):
                    mm = pe.matmul(pT[:, t // 4, (t % 4) * P:(t % 4 + 1) * P], h[:, e % 2, t, :], k("ident"), start=True, stop=True)
                mm.then_inc(hT_done, 1)

            def sorted_up(e):
                pe.wait_ge(hT_ready, 2 * e)
                for c in range(NF):
                    m = (e - 1) * NF + c
                    if m >= 2:
                        pe.wait_ge(sorted_up_ready, m - 1)
                    for i in range(2):
                        mm = pe.matmul(pH[:, 2 * (m % 2) + i, 0:HALF], w1[:, e, c * P:(c + 1) * P],
                                       hT[:, e % 2, i * HALF:(i + 1) * HALF], start=True, stop=True)
                    mm.then_inc(sorted_up_done, 1)

            def sorted_down(e):
                pe.wait_ge(sorted_up_ready, e * NF)
                if e == 1:
                    pe.wait_ge(added, NB // 2 * TG)
                else:
                    pe.wait_ge(y_ready, e - 1)
                for t in range(NT):
                    for c in range(NF):
                        mm = pe.matmul(pY[:, t // 4, t % 4, :], hid[:, e % 2, c, t * P:(t + 1) * P], w2[:, e, c, :],
                                       start=(c == 0), stop=(c == NF - 1))
                mm.then_inc(y_done, 1)

            def sorted_():
                turn(1)
                sorted_up(1)
                for e in range(1, E):
                    if e + 1 < E:
                        turn(e + 1)
                        sorted_up(e + 1)
                    sorted_down(e)
                pe.wait_ge(y_ready, E - 1)

            all_phases(dense, sorted_)

        @block.scalar
        def _(act):
            def dense(first, end):
                for n in range(first, end):
                    if n > 1:
                        act.wait_ge(down_done, n - 1)
                    for c in range(NF):
                        m = n * NF + c
                        act.wait_ge(up_done, m + 1)
                        act.activation(hid[:, n % 2, c, 0:N], pH[:, m % 4, :], ACT.Relu, bias=vec[:, VB1_0 + c:VB1_0 + c + 1]
                                       ).then_inc(up_ready, 1)

            def turned(e):
                act.wait_ge(hT_done, e)
                act.activation(hT[:, e % 2, 0:N], pT[:, 0, :], ACT.Copy).then_inc(hT_ready, 1)
                act.activation(hT[:, e % 2, N:CAP], pT[:, 1, 0:CAP - N], ACT.Copy).then_inc(hT_ready, 1)

            def sorted_hidden(e):
                if e == 1:
                    act.wait_ge(down_done, NB // 2)
                elif e > 2:
                    act.wait_ge(y_done, e - 2)
                for c in range(NF):
                    m = (e - 1) * NF + c
                    act.wait_ge(sorted_up_done, m + 1)
                    act.activation(hid[:, e % 2, c, :].rearrange("p (i n) -> p i n", i=2), pH[:, 2 * (m % 2):2 * (m % 2) + 2, 0:HALF],
                                   ACT.Relu, bias=vec[:, VB1_0 + e * NF + c:VB1_0 + e * NF + c + 1]).then_inc(sorted_up_ready, 1)

            def sorted_():
                for e in range(1, E):
                    turned(e)
                    sorted_hidden(e)
                act.wait_ge(y_done, E - 1)

            all_phases(dense, sorted_)

        @block.gpsimd
        def _(pool):
            pool.wait_ge(env["rows_zeroed"], 16 * (E - 1))
            for g in range(G):
                pool.indirect_dma_start(rows_in, bass.IndirectOffsetOnAxis(ap=slot_of[:, g:g + 1], axis=0), H_all[:, g, :], None,
                                        bounds_check=SLOTS - 1, oob_is_err=False).then_inc(scattered, 16)
            pool.memset(back[:, :, :], 0.0).then_inc(back_zeroed, 1)
            pool.wait_ge(back_zeroed, 1)
            for p in range(2):
                pool.wait_ge(y_stored[p], 16 * ((E - 1 + p) // 2))
            for g in range(G):
                pool.indirect_dma_start(back[:, g, :], None, rows_out, bass.IndirectOffsetOnAxis(ap=slot_of[:, g:g + 1], axis=0),
                                        bounds_check=SLOTS - 1, oob_is_err=False).then_inc(gathered[g // TG], 16)

        @block.vector
        def _(dve):
            dve.wait_ge(b2_loaded, 16)
            for g in range(G):
                dve.tensor_scalar(bias[:, g, :], b2[:, 0, :], MASK[:, g, 0:1], None, ALU.mult).then_inc(bias_ready, 1)
            dve.wait_ge(bias_ready, G)
            dve.tensor_tensor(X[:, :, :], bias[:, :, :], X[:, :, :], ALU.add).then_inc(bias_ready, 1)
            dve.wait_ge(bias_ready, G + 1)

            def dense(first, end):
                for n in range(first, end):
                    dve.wait_ge(down_done, n + 1)
                    for t in range(TG):
                        g = n * TG + t
                        dve.scalar_tensor_tensor(X[:, g, :], pY[:, n % 2, t, :], MASK[:, g, 0:1], X[:, g, :], ALU.mult, ALU.add
                                                 ).then_inc(added, 1)

            def sorted_():
                for e in range(1, E):
                    dve.wait_ge(y_done, e)
                    if e > 2:
                        dve.wait_ge(y_stored[e % 2], 16 * ((e - 1) // 2))
                    dve.tensor_tensor(y[:, e % 2, :, :], pY[:, :, :, :].rearrange("p i t d -> p (i t) d")[:, 0:NT, :],
                                      b2[:, e, :].unsqueeze(1).broadcast_to([P, NT, D]), ALU.add).then_inc(y_ready, 1)

            all_phases(dense, sorted_)
            dve.wait_ge(added, G)
            for n in range(NB):
                r = slice(n * TG, (n + 1) * TG)
                dve.wait_ge(gathered[n], 16 * TG)
                dve.tensor_tensor(X[:, r, :], back[:, r, :], X[:, r, :], ALU.add).then_inc(added, 1)


def experts_layer1(env):
    nc, io, X, HT_parts, MASK, k, vec = (env[n] for n in ("nc", "io", "X", "HT_parts", "MASK", "k", "vec"))
    name, NF, out, (w1, w2), w_loaded = "f1", F1 // P, io["out"], env["ew"][1], env["ew_loaded"][1]
    ctx = Phase(nc, name)
    with ctx:
        def sb(n, shape, dt=F32):
            return ctx.enter_context(nc.sbuf_tensor(f"{name}_{n}", shape, dt))

        def sig(n, per=1, credit=0):
            return Signal(ctx, nc, f"{name}_{n}", per, credit)

        N = TG * P
        b2 = sb("b2", [E, D])
        w1s = sb("w1s", [P, 2, E, NF * P], F32R)
        mk, mkT = sb("mk", [P, TG, E]), sb("mkT", [E, TG, P])
        hid = sb("hid", [P, 2, NF, N])
        pH = ctx.enter_context(nc.psum_tensor(f"{name}_pH", [P, 4, N], F32))
        pY = ctx.enter_context(nc.psum_tensor(f"{name}_pY", [P, 2, TG, D], F32))
        pB = ctx.enter_context(nc.psum_tensor(f"{name}_pB", [P, TG, D], F32))
        b2_loaded = ctx.semaphore(f"{name}_b2_loaded")
        w1h_ready, w1l_ready = ctx.semaphore("f1_w1h_ready"), ctx.semaphore("f1_w1l_ready")
        mk_ready, mkT_done, mkT_ready = sig("mk_ready"), sig("mkT_done"), sig("mkT_ready")
        b_done, b_added = sig("b_done"), sig("b_added", TG)
        h_done, h_ready = sig("h_done", E * NF), sig("h_ready", E * NF, credit=4)
        y_done, y_added = sig("y_done", E, credit=2), sig("y_added", E * TG, credit=2 * TG)
        stored = ctx.semaphore(f"{name}_stored")
        block = ctx.enter_context(nc.Block())

        @block.sync
        def _(sp):
            sp.dma_start(b2[:, :], io["f1_b2"]).then_inc(b2_loaded, 16)
            with sp.Fori(0, NB) as n:
                sp.wait_ge(y_added.sem, y_added.at(n))
                sp.dma_start(out.rearrange("(g bb) t d -> (bb t) g d", bb=BG)[:, bass.ds(n * TG, TG), :],
                             X[:, bass.ds(n * TG, TG), :]).then_inc(stored, 16)
            sp.wait_ge(stored, 16 * NB)

        @block.tensor
        def _(pe):
            pe.wait_ge(w_loaded, 32 * E)
            pe.wait_ge(w1l_ready, 1)
            pe.wait_ge(b2_loaded, 16)
            pe.sem_inc(y_done.sem, y_done.credit)
            with pe.Fori(0, NB) as n:
                def turn_mask():
                    pe.wait_ge(mk_ready.sem, mk_ready.at(n))
                    for t in range(TG):
                        mm = pe.transpose(pB[0:E, t, :], mk[:, t, :], k("ident"))
                    mm.then_inc(mkT_done.sem, 1)

                def biases():
                    pe.wait_ge(mkT_ready.sem, mkT_ready.at(n))
                    for t in range(TG):
                        mm = pe.matmul(pB[:, t, :], mkT[:, t, :], b2[:, :], start=True, stop=True)
                    mm.then_inc(b_done.sem, 1)

                def up(e):
                    for c in range(NF):
                        m = e * NF + c
                        pe.wait_ge(h_ready.sem, h_ready.at(n, m + 1) - 4)
                        for i, (hw, ht) in enumerate(((1, 0), (0, 1), (0, 0))):
                            mm = pe.matmul(pH[:, m % 4, :], w1s[:, hw, e, c * P:(c + 1) * P],
                                           HT_parts[:, ht, bass.ds(n * TG, TG), :].rearrange("p g t -> p (g t)"),
                                           start=(i == 0), stop=(i == 2))
                        mm.then_inc(h_done.sem, 1)

                def down(e):
                    pe.wait_ge(h_ready.sem, h_ready.at(n, (e + 1) * NF))
                    pe.wait_ge(y_added.sem, y_added.at(n, (e - 1) * TG))
                    for t in range(TG):
                        for c in range(NF):
                            mm = pe.matmul(pY[:, e % 2, t, :], hid[:, e % 2, c, t * P:(t + 1) * P], w2[:, e, c, :],
                                           start=(c == 0), stop=(c == NF - 1))
                    mm.then_inc(y_done.sem, 1)

                up(0)
                turn_mask()
                up(1)
                biases()
                down(0)
                for e in range(1, E):
                    if e + 1 < E:
                        up(e + 1)
                    down(e)

        @block.scalar
        def _(act):
            act.sem_inc(h_ready.sem, h_ready.credit)
            act.wait_ge(w_loaded, 32 * E)
            act.activation(w1s[:, 0, :, :], w1[:, :, :], ACT.Copy).then_inc(w1h_ready, 1)
            with act.Fori(0, NB) as n:
                for e in range(E):
                    if e == 1:
                        act.wait_ge(mkT_done.sem, mkT_done.at(n))
                        act.activation(mkT[:, :, :], pB[0:E, :, :], ACT.Copy).then_inc(mkT_ready.sem, 1)
                    act.wait_ge(y_done.sem, y_done.at(n, e - 1))
                    for c in range(NF):
                        m = e * NF + c
                        act.wait_ge(h_done.sem, h_done.at(n, m + 1))
                        act.activation(hid[:, e % 2, c, :], pH[:, m % 4, :], ACT.Relu, bias=vec[:, VB1_1 + m:VB1_1 + m + 1]
                                       ).then_inc(h_ready.sem, 1)

        @block.vector
        def _(dve):
            dve.sem_inc(y_added.sem, y_added.credit)
            dve.wait_ge(w1h_ready, 1)
            dve.tensor_tensor(w1s[:, 1, :, :], w1[:, :, :], w1s[:, 0, :, :].bitcast(F32), ALU.subtract).then_inc(w1l_ready, 1)
            with dve.Fori(0, NB) as n:
                dve.tensor_copy(mk[:, :, :], MASK[:, bass.ds(n * TG, TG), :]).then_inc(mk_ready.sem, 1)
                dve.wait_ge(mk_ready.sem, mk_ready.at(n))
                dve.wait_ge(b_done.sem, b_done.at(n))
                for t in range(TG):
                    x = X[:, bass.ds(n * TG + t, 1), :].rearrange("p g d -> p (g d)")
                    dve.tensor_tensor(x, pB[:, t, :], x, ALU.add).then_inc(b_added.sem, 1)
                dve.wait_ge(b_added.sem, b_added.at(n))
                for e in range(E):
                    dve.wait_ge(y_done.sem, y_done.at(n, e + 1))
                    if e > 0:
                        dve.wait_ge(y_added.sem, y_added.at(n, e * TG))
                    for t in range(TG):
                        x = X[:, bass.ds(n * TG + t, 1), :].rearrange("p g d -> p (g d)")
                        dve.scalar_tensor_tensor(x, pY[:, e % 2, t, :], mk[:, t, e:e + 1], x, ALU.mult, ALU.add
                                                 ).then_inc(y_added.sem, 1)
                dve.wait_ge(y_added.sem, y_added.at(n))


def cross_layer1(env):
    nc, io, X, w, v, k, bo1 = (env[n] for n in ("nc", "io", "X", "w", "v", "k", "bo1"))
    ctx = Phase(nc, "c")
    with ctx:
        def sb(name, shape, dt=F32):
            return ctx.enter_context(nc.sbuf_tensor("c_" + name, shape, dt))

        def ps(name, shape):
            return ctx.enter_context(nc.psum_tensor("c_" + name, shape, F32))

        def sig(name, per=1, credit=0):
            return Signal(ctx, nc, "c_" + name, per, credit)

        ctxT = sb("ctxT", [P, BG, S])
        hT, q, qs = sb("hT", [P, P]), sb("q", [P, P]), sb("qs", [P, 2, P], F32R)
        qq = sb("qq", [P, 2, 2, HQ, T], F32R)
        ks = sb("ks", [P, S])
        ksp = sb("ksp", [P, 2, 2, SE], F32R)
        vs, vl = sb("vs", [P, BG, SC, D]), sb("vl", [NQ, BG, D])
        nm, den, rinv = sb("nm", [P, NQ]), sb("den", [P, 2, NQ]), sb("rinv", [P, BG, NQ])
        pr = sb("pr", [P, 2, NQ, S])
        prT, prl = sb("prT", [P, SC, NQ, P]), sb("prl", [NQ, P])
        rm = sb("rm", [P, BG, NQ, HQ * HD])
        om, osum, on, ob, yb = sb("om", [P, BG, HQ, T]), sb("osum", [P, BG, T]), sb("on", [P, P]), sb("ob", [P, P]), sb("yb", [P, D])
        pS = ps("pS", [P, NQ, 512])
        pT = ps("pT", [P, SC, NQ, P])
        pG = pT[:, 1, :, :].rearrange("p j t -> p (j t)")
        pM = ps("pM", [P, 512])
        pO = ps("pO", [P, BG, HQ, T])

        n4 = Norm(ctx, nc, "c_n4", env)
        ctx_loaded = [sig(f"ctx_loaded{b}", 16) for b in range(BG)]
        hT_done, hT_ready, q_done, q_ready = sig("hT_done"), sig("hT_ready"), sig("q_done"), sig("q_ready")
        qq_ready = sig("qq_ready")
        k_done, k_ready, kh_ready, kl_ready = sig("k_done"), sig("k_ready"), sig("kh_ready"), sig("kl_ready")
        qh_ready, ql_ready, k_padded = sig("qh_ready"), sig("ql_ready"), sig("k_padded")
        v_done, v_ready = sig("v_done", credit=BG), sig("v_ready")
        vl_ready, prl_ready = sig("vl_ready"), sig("prl_ready")
        s_done, max_ready, e_ready = sig("s_done", NQ), sig("max_ready", NQ), sig("e_ready", NQ, credit=NQ)
        pT_done, pT0_ready, pT1_ready = sig("pT_done", SC), sig("pT0_ready"), sig("pT1_ready")
        o_done, rinv_ready, rm_ready = sig("o_done"), sig("rinv_ready"), sig("rm_ready")
        om_ready, osum_ready = sig("om_ready"), sig("osum_ready")
        rT_done, on_ready, ob_ready, y_done, yb_ready, x_ready = (sig("rT_done"), sig("on_ready"), sig("ob_ready"), sig("y_done"),
                                                                 sig("yb_ready"), sig("x_ready"))
        SCALE = float(HD) ** -0.5

        block = ctx.enter_context(nc.Block())

        @block.sync
        def _(sp):
            with sp.Fori(0, G) as g:
                for b in range(BG):
                    sp.wait_ge(v_done.sem, v_done.at(g * BG + b - BG))
                    sp.dma_start(ctxT[:, b, :].unsqueeze(1), io["ctxT"][bass.ds(g, 1), :, b, :].rearrange("g p s -> p g s")
                                 ).then_inc(ctx_loaded[b].sem, 16)

        @block.tensor
        def _(pe):
            pe.sem_inc(v_done.sem, v_done.credit)

            pe.wait_ge(k_padded.sem, 1)

            def norm_T(g):
                pe.wait_ge(n4.h_ready.sem, n4.h_ready.at(g))
                pe.matmul(pG[:, 0:P], n4.h[:, :], k("ident"), start=True, stop=True).then_inc(hT_done.sem, 1)

            def queries(g):
                pe.wait_ge(hT_ready.sem, hT_ready.at(g))
                pe.matmul(pG[:, P:2 * P], w("wq1"), hT[:, :], start=True, stop=True).then_inc(q_done.sem, 1)

            def keys(g, b, n):
                pe.wait_ge(ctx_loaded[b].sem, ctx_loaded[b].at(g))
                pe.matmul(pM[:, 0:S], w("wk1"), ctxT[:, b, :], start=True, stop=True).then_inc(k_done.sem, 1)

            def values(b, n):
                pe.wait_ge(k_ready.sem, k_ready.at(n))
                for c in range(SC):
                    pe.matmul(pM[:, c * D:(c + 1) * D], ctxT[:, b, c * P:(c + 1) * P], w("wv1"), start=True, stop=True)
                return pe.matmul(pM[0:NQ, SC * D:(SC + 1) * D], ctxT[:, b, SM:S].broadcast_to([P, NQ]), w("wv1"),
                                 start=True, stop=True)

            def values_left(n):
                pe.wait_ge(vl_ready.sem, vl_ready.at(n))

            def last_weights(b, n):
                pe.wait_ge(e_ready.sem, e_ready.at(n))
                return pe.matmul(pM[0:NQ, (SC + 1) * D:(SC + 2) * D], pr[:, b % 2, :, SM], k("ident"), start=True, stop=True)

            def scores(b, n):
                pe.wait_ge(kl_ready.sem, kl_ready.at(n))
                pe.wait_ge(qq_ready.sem, qq_ready.at(n))
                for c in range(NQ):
                    r = slice(c * T, (c + 1) * T)
                    pe.wait_ge(e_ready.sem, e_ready.at(n - 1, c + 1))
                    for i, (hq, hk) in enumerate(((1, 0), (0, 1), (0, 0))):
                        mm = pe.matmul(pS[:, c, 0:SE], qq[r, b % 2, hq, :, :], ksp[r, b % 2, hk, :], start=(i == 0), stop=(i == 2))
                    mm.then_inc(s_done.sem, 1)

            def turn(b, n, c):
                for j in range(NQ):
                    mm = pe.transpose(pT[:, c, j, :], pr[:, b % 2, j, c * P:(c + 1) * P], k("ident"))
                mm.then_inc(pT_done.sem, 1)

            def sums(b, n):
                pe.wait_ge(prl_ready.sem, prl_ready.at(n))
                for c, ready in enumerate((pT0_ready, pT1_ready)):
                    pe.wait_ge(ready.sem, ready.at(n))
                    for j in range(NQ):
                        pe.matmul(pO[j * T:(j + 1) * T, b, :, :], vs[:, b, c, j * T:(j + 1) * T], prT[:, c, j, :],
                                  start=(c == 0), stop=False, skip_group_check=True)
                pe.matmul(pO[:, b, :, :], vl[:, b, :], prl[:, :], start=False, stop=True,
                          skip_group_check=True).then_inc(o_done.sem, 1)

            def scales(g):
                pe.wait_ge(rm_ready.sem, rm_ready.at(g))
                for b in range(BG):
                    mm = pe.matmul(pG[:, b * T:(b + 1) * T], rm[:, b, :, :], k("qsel"), start=True, stop=True)
                mm.then_inc(rT_done.sem, 1)

            def project(g):
                pe.wait_ge(ob_ready.sem, ob_ready.at(g))
                pe.matmul(pG[:, P:2 * P], ob[:, :], w("wo1"), start=True, stop=True).then_inc(y_done.sem, 1)

            def group_product(b, g, first, last):
                if b > 0 and not (first and b == 1):
                    pe.wait_ge(pT1_ready.sem, pT1_ready.at(g * BG + b - 2))
                if b == 1 and not last:
                    norm_T(g + 1)
                if b == 2:
                    if not first:
                        scales(g - 1)
                    if not last:
                        queries(g + 1)
                if b == BG - 1 and not first:
                    project(g - 1)

            def group_product_left(b, g, first, last):
                if b == 1 and not last:
                    pe.wait_ge(hT_ready.sem, hT_ready.at(g + 1))
                if b == 2:
                    if not first:
                        pe.wait_ge(on_ready.sem, on_ready.at(g - 1))
                    if not last:
                        pe.wait_ge(qh_ready.sem, qh_ready.at(g + 1))
                if b == BG - 1 and not first:
                    pe.wait_ge(yb_ready.sem, yb_ready.at(g - 1))

            def body(g, first, last):
                for b in range(BG):
                    n = g * BG + b
                    turns, more = not first or b > 0, b < BG - 1 or not last
                    scores(b, n)
                    if more:
                        values_left(n)
                        keys(g if b < BG - 1 else g + 1, (b + 1) % BG, n + 1)
                    group_product(b, g, first, last)
                    if not first or b > 1:
                        if b == 2 and not first:
                            pe.wait_ge(om_ready.sem, om_ready.at(g - 1))
                        sums((b - 2) % BG, n - 2)
                    if more:
                        mm = values((b + 1) % BG, n + 1)
                    if turns:
                        mm = last_weights((b - 1) % BG, n - 1)
                    mm.then_inc(v_done.sem, 1)
                    if turns:
                        turn((b - 1) % BG, n - 1, 0)
                    group_product_left(b, g, first, last)
                    if turns:
                        turn((b - 1) % BG, n - 1, 1)

            norm_T(0)
            pe.wait_ge(hT_ready.sem, hT_ready.at(0))
            queries(0)
            pe.wait_ge(qh_ready.sem, qh_ready.at(0))
            keys(0, 0, 0)
            values(0, 0).then_inc(v_done.sem, 1)
            body(0, True, False)
            with pe.Fori(1, G - 1) as g:
                body(g, False, False)
            body(G - 1, False, True)
            sums(BG - 2, B - 2)
            last_weights(BG - 1, B - 1).then_inc(v_done.sem, 1)
            for c in range(SC):
                turn(BG - 1, B - 1, c)
            sums(BG - 1, B - 1)
            pe.wait_ge(pT1_ready.sem, pT1_ready.at(B - 1))
            scales(G - 1)
            project(G - 1)

        @block.scalar
        def _(act):
            act.sem_inc(e_ready.sem, e_ready.credit)

            def keys(b, n):
                act.wait_ge(k_done.sem, k_done.at(n))
                act.activation(ks[:, :], pM[:, 0:S], ACT.Identity, bias=v("bk1")).then_inc(k_ready.sem, 1)

            def exps(b, n, quads):
                for c in quads:
                    act.wait_ge(max_ready.sem, max_ready.at(n, c + 1))
                    act.activation(pr[:, b % 2, c, :], pS[:, c, 0:S], ACT.Exp, bias=nm[:, c:c + 1],
                                   accum_out=den[:, b % 2, c:c + 1]).then_inc(e_ready.sem, 1)

            def turned(n):
                act.wait_ge(pT_done.sem, pT_done.at(n, 1))
                act.activation(prT[:, 0, :, :], pT[:, 0, :, :], ACT.Copy).then_inc(pT0_ready.sem, 1)

            def norm_T(g):
                act.wait_ge(hT_done.sem, hT_done.at(g))
                act.activation(hT[:, :], pG[:, 0:P], ACT.Copy).then_inc(hT_ready.sem, 1)

            def body(g, first, last):
                for b in range(BG):
                    n = g * BG + b
                    exps(b, n, range(NQ // 2))
                    if b < BG - 1 or not last:
                        keys((b + 1) % BG, n + 1)
                    exps(b, n, range(NQ // 2, NQ))
                    if b == 1 and not last:
                        norm_T(g + 1)
                    if not first or b > 0:
                        turned(n - 1)

            norm_T(0)
            keys(0, 0)
            body(0, True, False)
            with act.Fori(1, G - 1) as g:
                body(g, False, False)
            body(G - 1, False, True)
            turned(B - 1)

        @block.gpsimd
        def _(pool):
            def spread(b, n, g):
                pool.wait_ge(ql_ready.sem, ql_ready.at(g))
                if not (isinstance(n, int) and n < 2):
                    pool.wait_ge(s_done.sem, s_done.at(n - 2))
                for i in range(2):
                    ins = pool.tensor_tensor(qq[:, b % 2, i, :, :], qs[:, i, b * T:(b + 1) * T].bitcast(F32).unsqueeze(1).broadcast_to([P, HQ, T]),
                                             k("quad").unsqueeze(2).broadcast_to([P, HQ, T]), ALU.mult)
                ins.then_inc(qq_ready.sem, 1)

            def split_keys(b, n):
                pool.wait_ge(k_ready.sem, k_ready.at(n))
                carry(pool, ctx)
                pool.tensor_copy(ksp[:, b % 2, 0, 0:S], ks[:, :]).then_inc(kh_ready.sem, 1)
                pool.wait_ge(kh_ready.sem, kh_ready.at(n))
                pool.tensor_tensor(ksp[:, b % 2, 1, 0:S], ks[:, :], ksp[:, b % 2, 0, 0:S].bitcast(F32), ALU.subtract).then_inc(kl_ready.sem, 1)

            def scales(g):
                pool.wait_ge(rinv_ready.sem, rinv_ready.at(g * BG + BG - 1))
                pool.tensor_tensor(rm[:, :, :, :], rinv[:, :, :].unsqueeze(3).broadcast_to([P, BG, NQ, HQ * HD]),
                                   k("vmask").rearrange("p (c f) -> p c f", c=NQ).unsqueeze(1).broadcast_to([P, BG, NQ, HQ * HD]),
                                   ALU.mult).then_inc(rm_ready.sem, 1)

            def body(g, first, last):
                for b in range(BG):
                    n = g * BG + b
                    if b < BG - 1:
                        spread(b + 1, n + 1, g)
                        split_keys(b + 1, n + 1)
                    elif not last:
                        spread(0, n + 1, g + 1)
                        split_keys(0, n + 1)
                    if b == 0:
                        if not last:
                            n4.gpsimd(pool, g + 1)
                        if not first:
                            scales(g - 1)

            pool.tensor_copy(ksp[:, :, :, S:SE].rearrange("p a h s -> p (a h s)"), k("ones")[:, 0:4 * (SE - S)]).then_inc(k_padded.sem, 1)
            n4.gpsimd(pool, 0)
            spread(0, 0, 0)
            split_keys(0, 0)
            body(0, True, False)
            with pool.Fori(1, G - 1) as g:
                body(g, False, False)
            body(G - 1, False, True)
            scales(G - 1)

        @block.vector
        def _(dve):
            def x_of(g):
                return X[:, bass.ds(g, 1), :].rearrange("p g d -> p (g d)")

            def queries(g):
                dve.wait_ge(q_done.sem, q_done.at(g))
                if not (isinstance(g, int) and g == 0):
                    dve.wait_ge(qq_ready.sem, qq_ready.at(g * BG - 1))
                dve.tensor_scalar(q[:, :], pG[:, P:2 * P], v("bq1"), SCALE, ALU.add, ALU.mult).then_inc(q_ready.sem, 1)
                dve.tensor_scalar(qs[:, 0, :], pG[:, P:2 * P], v("bq1"), SCALE, ALU.add, ALU.mult).then_inc(qh_ready.sem, 1)
                dve.wait_ge(qh_ready.sem, qh_ready.at(g))
                dve.tensor_tensor(qs[:, 1, :], q[:, :], qs[:, 0, :].bitcast(F32), ALU.subtract).then_inc(ql_ready.sem, 1)

            def maxima(n):
                for c in range(NQ):
                    dve.wait_ge(s_done.sem, s_done.at(n, c + 1))
                    dve.tensor_reduce(nm[:, c:c + 1], pS[:, c, 0:S], AX.X, ALU.max, negate=True).then_inc(max_ready.sem, 1)

            def values(b, n):
                dve.wait_ge(v_done.sem, v_done.at(n))
                dve.tensor_copy(vs[:, b, :, :], pM[:, 0:SM].rearrange("p (c d) -> p c d", c=SC)).then_inc(v_ready.sem, 1)
                dve.tensor_tensor(vl[:, b, :], pM[0:NQ, SC * D:(SC + 1) * D], k("row4")[0:NQ, :], ALU.mult).then_inc(vl_ready.sem, 1)

            def turned(n):
                dve.wait_ge(pT_done.sem, pT_done.at(n))
                dve.tensor_copy(prT[:, 1, :, :], pT[:, 1, :, :]).then_inc(pT1_ready.sem, 1)

            def last_weights(b, n, g_read):
                dve.wait_ge(v_done.sem, v_done.at(n + 2))
                dve.tensor_copy(prl[:, :], pM[0:NQ, (SC + 1) * D:(SC + 2) * D]).then_inc(prl_ready.sem, 1)
                if g_read is not None:
                    dve.wait_ge(rm_ready.sem, rm_ready.at(g_read))
                dve.reciprocal(rinv[:, b, :], den[:, b % 2, :]).then_inc(rinv_ready.sem, 1)

            def gather(g):
                dve.wait_ge(o_done.sem, o_done.at(g * BG + BG - 1))
                dve.tensor_tensor(om[:, :, :, :], pO[:, :, :, :],
                                  k("quad").unsqueeze(1).unsqueeze(3).broadcast_to([P, BG, HQ, T]), ALU.mult).then_inc(om_ready.sem, 1)

            def gather_heads(g):
                dve.wait_ge(om_ready.sem, om_ready.at(g))
                dve.tensor_reduce(osum[:, :, :], om[:, :, :, :].rearrange("p b h t -> p b t h"), AX.X, ALU.add
                                  ).then_inc(osum_ready.sem, 1)

            def scale(g):
                dve.wait_ge(rT_done.sem, rT_done.at(g))
                dve.wait_ge(osum_ready.sem, osum_ready.at(g))
                dve.tensor_tensor(on[:, :], pG[:, 0:P], osum[:, :, :].rearrange("p b t -> p (b t)"), ALU.mult).then_inc(on_ready.sem, 1)
                dve.wait_ge(on_ready.sem, on_ready.at(g))
                dve.tensor_scalar(ob[:, :], on[:, :], v("bv1"), None, ALU.add).then_inc(ob_ready.sem, 1)

            def add_bias(g):
                dve.wait_ge(y_done.sem, y_done.at(g))
                dve.tensor_tensor(yb[:, :], pG[:, P:2 * P], bo1[:, :], ALU.add).then_inc(yb_ready.sem, 1)

            def add_output(g):
                dve.wait_ge(yb_ready.sem, yb_ready.at(g))
                dve.tensor_tensor(x_of(g), yb[:, :], x_of(g), ALU.add).then_inc(x_ready.sem, 1)

            def body(g, first, last):
                for b in range(BG):
                    n = g * BG + b
                    maxima(n)
                    if b == 1 and not first:
                        gather(g - 1)
                    if b == 2:
                        if not last:
                            queries(g + 1)
                        if not first:
                            gather_heads(g - 1)
                            scale(g - 1)
                    if b == BG - 1 and not first:
                        add_bias(g - 1)
                    if b == 0 and not last:
                        n4.vector_stats(dve, x_of(g + 1), g + 1)
                    if b == BG - 1 and not first:
                        add_output(g - 1)
                    if not first or b > 0:
                        last_weights((b - 1) % BG, n - 1, g - 1 if (b == 1 and not first) else None)
                    if b < BG - 1 or not last:
                        values((b + 1) % BG, n + 1)
                    if b == 0 and not last:
                        n4.vector_scale(dve, x_of(g + 1), g + 1)
                    if not first or b > 0:
                        turned(n - 1)

            n4.vector_stats(dve, x_of(0), 0)
            n4.vector_scale(dve, x_of(0), 0)
            queries(0)
            values(0, 0)
            body(0, True, False)
            with dve.Fori(1, G - 1) as g:
                body(g, False, False)
            body(G - 1, False, True)
            last_weights(BG - 1, B - 1, None)
            turned(B - 1)
            gather(G - 1)
            gather_heads(G - 1)
            scale(G - 1)
            add_bias(G - 1)
            add_output(G - 1)


def self_layer1(env):
    nc, io, X, HT_parts, LG, w, v, k = (env[n] for n in ("nc", "io", "X", "HT_parts", "LG", "w", "v", "k"))
    ctx = Phase(nc, "s")
    with ctx:
        def sb(name, shape, dt=F32):
            return ctx.enter_context(nc.sbuf_tensor("s_" + name, shape, dt))

        def ps(name, shape):
            return ctx.enter_context(nc.psum_tensor("s_" + name, shape, F32))

        def sig(name, per=1, credit=0):
            return Signal(ctx, nc, "s_" + name, per, credit)

        wqkv, wout, gate = sb("wqkv", [P, 3, RI]), sb("wout", [P, RP, D]), sb("gate", [P, E])
        gamma1, sq, ss, root, rms, xn = (sb("gamma1", [P, 1]), sb("sq", [P, D]), sb("ss", [P, 1]), sb("root", [P, 1]), sb("rms", [P, 1]),
                                         sb("xn", [P, D]))
        irms = sb("irms", [P, 1])
        hT = sb("hT", [P, P])
        qT = sb("qT", [P, RP, P])
        kp = sb("kp", [P, RP, BG, 2, T])
        vs = sb("vs", [P, RI])
        smax, sd, se, ssum, sinv, sn = (sb("smax", [P, H]), sb("sd", [P, H, T]), sb("se", [P, H, T]), sb("ssum", [P, H]), sb("sinv", [P, H]),
                                        sb("sn", [P, H, T]))
        pt = sb("pt", [P, H, P])
        oT, h5T = sb("oT", [P, RP, P]), sb("h5T", [P, P])
        pA = ps("pA", [P, RP, P])
        pK = ps("pK", [P, RP, P])
        pV = ps("pV", [P, RI])
        pS = ps("pS", [P, H, T])
        pM = ps("pM", [P, 4, P])
        n5 = Norm(ctx, nc, "s_n5", env)
        n6 = Norm(ctx, nc, "s_n6", env)
        w_loaded, gamma_ready, zeroed = sig("w_loaded", 48), sig("gamma_ready"), sig("zeroed", 2)
        ss_ready, root_ready, rms_ready, irms_ready, xn_ready = (sig("ss_ready"), sig("root_ready"), sig("rms_ready"), sig("irms_ready"),
                                                                sig("xn_ready"))
        hT_done, hT_ready = sig("hT_done"), sig("hT_ready")
        q_done, q_ready = sig("q_done"), sig("q_ready")
        k_done, k_ready = sig("k_done"), sig("k_ready", 2)
        v_done, v_ready = sig("v_done"), sig("v_ready")
        s_done, max_ready, sd_ready, se_ready = sig("s_done"), sig("max_ready"), sig("sd_ready"), sig("se_ready")
        sum_ready, sinv_ready, sn_ready, pt_ready = sig("sum_ready"), sig("sinv_ready"), sig("sn_ready"), sig("pt_ready")
        o_done, o_ready, y_done, x_ready = sig("o_done"), sig("o_ready"), sig("y_done"), sig("x_ready")
        h5T_done, h5T_ready, h5T_kept = sig("h5T_done"), sig("h5T_ready"), sig("h5T_kept", credit=1)
        high_kept = sig("high_kept")
        xh_ready, lg_done, lg_ready = sig("xh_ready"), sig("lg_done"), sig("lg_ready", credit=1)
        SCALE = float(RH) ** -0.5
        block = ctx.enter_context(nc.Block())

        def slots(eng, slot):
            slot(0, True, False, True)
            with eng.Fori(1, G - 2) as g:
                slot(g, False, False, True)
            slot(G - 2, False, False, False)
            slot(G - 1, False, True, False)

        @block.sync
        def _(sp):
            sp.dma_start(wqkv[:, :, :].rearrange("p a n -> p (a n)"), io["wqkv"]).then_inc(w_loaded.sem, 16)
            sp.dma_start(wout[:, :, :], io["wout"]).then_inc(w_loaded.sem, 16)
            sp.dma_start(gate[:, :], io["gate"]).then_inc(w_loaded.sem, 16)

        @block.tensor
        def _(pe):
            pe.wait_ge(w_loaded.sem, 3 * 16)

            def norm_T(g):
                pe.wait_ge(xn_ready.sem, xn_ready.at(g))
                pe.matmul(pM[:, 0, :], xn[:, :], k("ident"), start=True, stop=True).then_inc(hT_done.sem, 1)

            def queries_keys(g):
                pe.wait_ge(hT_ready.sem, hT_ready.at(g))
                for j in range(RP):
                    mm = pe.matmul(pA[:, j, :], wqkv[:, 0, j * P:(j + 1) * P], hT[:, :], start=True, stop=True)
                mm.then_inc(q_done.sem, 1)
                for j in range(RP):
                    mm = pe.matmul(pK[:, j, :], wqkv[:, 1, j * P:(j + 1) * P], hT[:, :], start=True, stop=True)
                mm.then_inc(k_done.sem, 1)

            def values(g):
                for c in range(2):
                    mm = pe.matmul(pV[:, c * 512:(c + 1) * 512], hT[:, :], wqkv[:, 2, c * 512:(c + 1) * 512], start=True, stop=True)
                mm.then_inc(v_done.sem, 1)

            def scores(g):
                pe.wait_ge(q_ready.sem, q_ready.at(g))
                pe.wait_ge(k_ready.sem, k_ready.at(g))
                for j in range(RP):
                    for b in range(BG):
                        mm = pe.matmul(pS[b * T:(b + 1) * T, 2 * j:2 * j + 2, :], qT[:, j, b * T:(b + 1) * T], kp[:, j, b, :, :],
                                       start=True, stop=True)
                mm.then_inc(s_done.sem, 1)

            def sums(g):
                pe.wait_ge(pt_ready.sem, pt_ready.at(g))
                pe.wait_ge(v_ready.sem, v_ready.at(g))
                for h in range(H):
                    r = slice(RH * (h % 2), RH * (h % 2) + RH)
                    mm = pe.matmul(pA[r, h // 2, :], vs[:, h * RH:(h + 1) * RH], pt[:, h, :], start=True, stop=True)
                mm.then_inc(o_done.sem, 1)

            def project(g):
                pe.wait_ge(o_ready.sem, o_ready.at(g))
                for j in range(RP):
                    mm = pe.matmul(pM[:, 1, :], oT[:, j, :], wout[:, j, :], start=(j == 0), stop=(j == RP - 1))
                mm.then_inc(y_done.sem, 1)

            def h5_T(g):
                pe.wait_ge(n6.h_ready.sem, n6.h_ready.at(g))
                pe.matmul(pM[:, 2, :], n6.h[:, :], k("ident"), start=True, stop=True).then_inc(h5T_done.sem, 1)

            def logits(g):
                pe.wait_ge(h5T_ready.sem, h5T_ready.at(g))
                pe.matmul(pM[:, 3, 0:E], h5T[:, :], gate[:, :], start=True, stop=True).then_inc(lg_done.sem, 1)

            def slot(g, first, last, norm):
                if not first:
                    pe.wait_ge(lg_ready.sem, lg_ready.at(g - 2))
                if not last:
                    norm_T(g + 1)
                scores(g)
                if not first:
                    if not last:
                        pe.wait_ge(hT_ready.sem, hT_ready.at(g + 1))
                    project(g - 1)
                if not last:
                    queries_keys(g + 1)
                if not first:
                    h5_T(g - 1)
                if not last:
                    pe.wait_ge(v_ready.sem, v_ready.at(g))
                    values(g + 1)
                    pe.wait_ge(q_ready.sem, q_ready.at(g + 1))
                if not first:
                    logits(g - 1)
                sums(g)

            norm_T(0)
            queries_keys(0)
            values(0)
            slots(pe, slot)
            pe.wait_ge(lg_ready.sem, lg_ready.at(G - 2))
            project(G - 1)
            h5_T(G - 1)
            logits(G - 1)

        @block.scalar
        def _(act):
            act.wait_ge(gamma_ready.sem, 1)
            act.wait_ge(zeroed.sem, 2)

            def norm_T(g):
                act.wait_ge(hT_done.sem, hT_done.at(g))
                act.activation(hT[:, :], pM[:, 0, :], ACT.Copy, scale=gamma1[:, :]).then_inc(hT_ready.sem, 1)

            def queries(g):
                act.wait_ge(q_done.sem, q_done.at(g))
                act.activation(qT[:, :, :], pA[:, :, :], ACT.Copy, scale=SCALE).then_inc(q_ready.sem, 1)

            def keys(g):
                act.wait_ge(k_done.sem, k_done.at(g))
                for i in range(2):
                    r = slice(RH * i, RH * i + RH)
                    act.activation(kp[r, :, :, i, :].rearrange("p j b s -> p (j b) s"),
                                   pK[r, :, :].rearrange("p j (b s) -> p (j b) s", b=BG), ACT.Copy).then_inc(k_ready.sem, 1)

            def values(g, first):
                act.wait_ge(v_done.sem, v_done.at(g))
                if not first:
                    act.wait_ge(o_done.sem, o_done.at(g - 1))
                act.activation(vs[:, :], pV[:, :], ACT.Copy).then_inc(v_ready.sem, 1)

            def outputs(g):
                act.wait_ge(o_done.sem, o_done.at(g))
                act.activation(oT[:, :, :], pA[:, :, :], ACT.Copy).then_inc(o_ready.sem, 1)

            def h5_T(g):
                act.wait_ge(h5T_done.sem, h5T_done.at(g))
                act.wait_ge(h5T_kept.sem, h5T_kept.at(g, 0))
                act.activation(h5T[:, :], pM[:, 2, :], ACT.Copy).then_inc(h5T_ready.sem, 1)

            def slot(g, first, last, norm):
                if not first:
                    outputs(g - 1)
                if not last:
                    norm_T(g + 1)
                values(g, first)
                act.wait_ge(sd_ready.sem, sd_ready.at(g))
                act.activation(se[:, :, :], sd[:, :, :], ACT.Exp).then_inc(se_ready.sem, 1)
                if not last:
                    queries(g + 1)
                    keys(g + 1)
                if not first:
                    h5_T(g - 1)

            norm_T(0)
            queries(0)
            keys(0)
            slots(act, slot)
            outputs(G - 1)
            h5_T(G - 1)

        @block.gpsimd
        def _(pool):
            pool.memset(kp[:, :, :, :, :], 0.0).then_inc(zeroed.sem, 1)
            pool.memset(pt[:, :, :], 0.0).then_inc(zeroed.sem, 1)
            pool.sem_inc(h5T_kept.sem, h5T_kept.credit)

            def root_of(g):
                pool.wait_ge(ss_ready.sem, ss_ready.at(g))
                pool.tensor_tensor(root[:, :], ss[:, :], k("root"), ALU.pow).then_inc(root_ready.sem, 1)

            def keep(g):
                high, low = (HT_parts[:, i, bass.ds(g, 1), :].rearrange("p g t -> p (g t)") for i in range(2))
                pool.wait_ge(h5T_ready.sem, h5T_ready.at(g))
                carry(pool, ctx)
                pool.tensor_copy(high, h5T[:, :]).then_inc(high_kept.sem, 1)
                pool.wait_ge(high_kept.sem, high_kept.at(g))
                pool.tensor_tensor(low, h5T[:, :], high.bitcast(F32), ALU.subtract).then_inc(h5T_kept.sem, 1)

            def slot(g, first, last, norm):
                if norm:
                    n5.gpsimd(pool, g + 2)
                if not first:
                    n6.gpsimd(pool, g - 1)
                if norm:
                    root_of(g + 2)
                if not first:
                    keep(g - 1)

            for g in range(2):
                n5.gpsimd(pool, g)
                root_of(g)
            slots(pool, slot)
            n6.gpsimd(pool, G - 1)
            keep(G - 1)

        @block.vector
        def _(dve):
            dve.tensor_scalar(gamma1[:, :], v("gamma"), 1.0, None, ALU.add).then_inc(gamma_ready.sem, 1)
            dve.wait_ge(zeroed.sem, 2)
            dve.sem_inc(lg_ready.sem, lg_ready.credit)

            def x_of(g):
                return X[:, bass.ds(g, 1), :].rearrange("p g d -> p (g d)")

            def squares(g):
                n5.vector_scale(dve, x_of(g), g)
                dve.wait_ge(n5.h_ready.sem, n5.h_ready.at(g))
                dve.scalar_tensor_tensor(sq[:, :], n5.h[:, :], 1.0, n5.h[:, :], ALU.mult, ALU.mult, accum_out=ss[:, :]
                                         ).then_inc(ss_ready.sem, 1)

            def bound(g):
                dve.wait_ge(root_ready.sem, root_ready.at(g))
                dve.tensor_scalar(rms[:, :], root[:, :], 1e-12, None, ALU.max).then_inc(rms_ready.sem, 1)

            def inverse(g):
                dve.wait_ge(rms_ready.sem, rms_ready.at(g))
                dve.reciprocal(irms[:, :], rms[:, :]).then_inc(irms_ready.sem, 1)

            def scaled(g):
                dve.wait_ge(irms_ready.sem, irms_ready.at(g))
                dve.tensor_scalar(xn[:, :], n5.h[:, :], irms[:, :], float(D) ** 0.5, ALU.mult, ALU.mult).then_inc(xn_ready.sem, 1)

            def add_output(g):
                dve.wait_ge(y_done.sem, y_done.at(g))
                dve.tensor_tensor(x_of(g), pM[:, 1, :], x_of(g), ALU.add).then_inc(x_ready.sem, 1)

            def output_stats(g):
                dve.wait_ge(x_ready.sem, x_ready.at(g))
                carry(dve, ctx)
                n6.vector_stats(dve, x_of(g), g)

            def add_normed(g):
                dve.wait_ge(n6.h_ready.sem, n6.h_ready.at(g))
                dve.tensor_tensor(x_of(g), x_of(g), n6.h[:, :], ALU.add).then_inc(xh_ready.sem, 1)

            def keep_logits(g):
                dve.wait_ge(lg_done.sem, lg_done.at(g))
                dve.tensor_copy(LG[:, bass.ds(g, 1), :].rearrange("p g e -> p (g e)"), pM[:, 3, 0:E]).then_inc(lg_ready.sem, 1)

            def slot(g, first, last, norm):
                dve.wait_ge(s_done.sem, s_done.at(g))
                dve.tensor_reduce(smax[:, :], pS[:, :, :], AX.X, ALU.max).then_inc(max_ready.sem, 1)
                if norm:
                    n5.vector_stats(dve, x_of(g + 2), g + 2)
                dve.wait_ge(max_ready.sem, max_ready.at(g))
                dve.tensor_tensor(sd[:, :, :], pS[:, :, :], smax[:, :].unsqueeze(2).broadcast_to([P, H, T]), ALU.subtract
                                  ).then_inc(sd_ready.sem, 1)
                if not first:
                    add_output(g - 1)
                dve.wait_ge(se_ready.sem, se_ready.at(g))
                dve.tensor_reduce(ssum[:, :], se[:, :, :], AX.X, ALU.add).then_inc(sum_ready.sem, 1)
                if not first:
                    output_stats(g - 1)
                dve.wait_ge(sum_ready.sem, sum_ready.at(g))
                dve.reciprocal(sinv[:, :], ssum[:, :]).then_inc(sinv_ready.sem, 1)
                if norm:
                    squares(g + 2)
                dve.wait_ge(sinv_ready.sem, sinv_ready.at(g))
                dve.tensor_tensor(sn[:, :, :], se[:, :, :], sinv[:, :].unsqueeze(2).broadcast_to([P, H, T]), ALU.mult
                                  ).then_inc(sn_ready.sem, 1)
                if not first:
                    n6.vector_scale(dve, x_of(g - 1), g - 1)
                dve.wait_ge(sn_ready.sem, sn_ready.at(g))
                for b in range(BG):
                    r = slice(b * T, (b + 1) * T)
                    ins = dve.transpose(pt[r, :, b * T:(b + 1) * T], sn[r, :, :])
                ins.then_inc(pt_ready.sem, 1)
                if norm:
                    bound(g + 2)
                if not first:
                    add_normed(g - 1)
                if norm:
                    inverse(g + 2)
                if not first:
                    keep_logits(g - 1)
                if norm:
                    scaled(g + 2)

            for g in range(2):
                n5.vector_stats(dve, x_of(g), g)
                squares(g)
                bound(g)
                inverse(g)
                if g > 0:
                    dve.wait_ge(hT_done.sem, hT_done.at(g - 1))
                scaled(g)
            slots(dve, slot)
            add_output(G - 1)
            output_stats(G - 1)
            n6.vector_scale(dve, x_of(G - 1), G - 1)
            add_normed(G - 1)
            keep_logits(G - 1)


def kernel(**inputs):
    import concourse.bacc as _bacc
    from concourse.bass_utils import run_bass_kernel_spmd as _run

    a = {n: np.asarray(x) for n, x in inputs.items()}
    c = np.ascontiguousarray
    ctx = a["ctx_1024"]
    pair = np.arange(D).reshape(-1, 2)[:, ::-1].ravel()
    t = lambda m: m.T
    squares = {"wq0": t(a["L0_xattn_Wq"]), "wk0": a["L0_xattn_Wk"], "wv0": t(a["L0_xattn_Wv"]), "wo0": t(a["L0_xattn_Wo"]),
               "aq": t(a["L0_attn_W_Q"]), "aqr": t(a["L0_attn_W_Q"][pair]), "ak": t(a["L0_attn_W_K"]), "akr": t(a["L0_attn_W_K"][pair]),
               "av": t(a["L0_attn_W_V"]), "ao": t(a["L0_attn_W_O"]),
               "wq1": t(a["L1_xattn_Wq"]), "wk1": t(a["L1_xattn_Wk"]), "wv1": t(a["L1_xattn_Wv"]), "wo1": t(a["L1_xattn_Wo"])}
    vectors = [a["L0_xattn_bq"], a["L0_xattn_bk"], a["L0_xattn_bv"], a["L1_xattn_bq"], a["L1_xattn_bk"], a["L1_xattn_bv"], a["L1_attn_gamma"]]
    vectors += list(a["L0_ffn_b1"].reshape(-1, P)) + list(a["L1_ffn_b1"].reshape(-1, P))
    arrays = {
        "x": a["x"],
        "ctxR": ctx[:, :SM].reshape(G, BG, SC, P, D).transpose(0, 3, 2, 1, 4).reshape(G, P, SC * BG * D),
        "ctxT": ctx.reshape(G, BG, S, D).transpose(0, 3, 1, 2),
        "ctxL": ctx[:, SM],
        "wsq": np.stack([squares[n] for n in SQ], 1),
        "vec": np.stack(vectors, 1),
        "cst": constants(),
        "bo0": np.broadcast_to(a["L0_xattn_bo"], (P, D)),
        "bo1": np.broadcast_to(a["L1_xattn_bo"], (P, D)),
        "router": t(a["L0_ffn_router_w"]),
        "gate": a["L1_ffn_gate_W"],
        "f0_w1": a["L0_ffn_W1"].transpose(1, 0, 2),
        "f0_w2": a["L0_ffn_W2"].reshape(E, F0 // P, P, D).transpose(2, 0, 1, 3),
        "f0_b2": np.broadcast_to(a["L0_ffn_b2"], (P, E, D)),
        "f1_w1": a["L1_ffn_W1"].transpose(1, 0, 2),
        "f1_w2": a["L1_ffn_W2"].reshape(E, F1 // P, P, D).transpose(2, 0, 1, 3),
        "f1_b2": a["L1_ffn_b2"],
        "wqkv": a["L1_attn_w_qkv"],
        "wout": a["L1_attn_w_out"].reshape(RP, P, D).transpose(1, 0, 2),
    }
    nc = _bacc.Bacc("TRN2", target_bir_lowering=False, num_devices=1)
    arrays = {f"in_{n}": c(x) for n, x in arrays.items()}
    io = {n[3:]: nc.dram_tensor(n, x.shape, mybir.dt.from_np(x.dtype), kind="ExternalInput").ap() for n, x in arrays.items()}
    io["out"] = nc.dram_tensor("out_dram", (B, T, D), F32, kind="ExternalOutput").ap()
    build_program(nc, io)
    r = _run(nc, [arrays], core_ids=[0])
    return r.results[0]["out_dram"]


def constants():
    p = np.arange(P)
    inv = 1.0 / np.float32(10000.0) ** (np.arange(0, HD, 2, dtype=np.float32) / HD)
    f = np.outer(inv, np.arange(T, dtype=np.float32)).astype(np.float32)
    angle = f[(p % HD) // 2]
    sign = np.where(p % 2 == 0, -1.0, 1.0)[:, None]
    parts = {
        "ident": np.eye(P),
        "rope": np.concatenate([np.cos(angle), sign * np.sin(angle)], 1),
        "quad": (p[:, None] // HD) % HQ == np.arange(HQ)[None],
        "vmask": (p[None] // HD) % HQ == p[:, None] // T,
        "batch": p[:, None] // T == np.arange(BG)[None],
        "qsel": p[:, None] % T == np.arange(T)[None],
        "row4": p[None] // T == p[:, None],
        "before": p[:, None] < p[None],
        "ones": np.ones((P, P)),
        "rank": np.broadcast_to(E - np.arange(E), (P, E)),
        "slot": np.broadcast_to(np.r_[NO_SLOT, CAP * np.arange(E - 1)], (P, E)),
        "half": np.full((P, 1), -0.5),
        "root": np.full((P, 1), 0.5),
        "eps": np.full((P, 1), EPS),
    }
    return np.concatenate([np.asarray(parts[n], np.float32) for n in CONST], 1)
```
